# Optimizing a Trainium2 kernel written in Bass

```python
import numpy as np
import jax
import jax.numpy as jnp

def _softmax(x, axis=-1):
    return jax.nn.softmax(x, axis=axis)

def _gelu(x):
    return jax.nn.gelu(x, approximate=True)

def _silu(x):
    return jax.nn.silu(x)

def _sigmoid(x):
    return jax.nn.sigmoid(x)

def _layernorm(x, axis=-1, eps=1e-05):
    m = jnp.mean(x, axis=axis, keepdims=True)
    v = jnp.var(x, axis=axis, keepdims=True)
    return (x - m) / jnp.sqrt(v + eps)

def _scatter_add(tgt, idx, src, axis=0):
    return tgt.at[idx].add(src)

def _segment_sum(src, seg, n):
    return jax.ops.segment_sum(src, seg, n)
kernel_name = 'mk_adaln_attn_ffn_d1_seqx_r8_f23410'

def setup_inputs(seed: int=0):
    np.random.seed(seed)
    _w = jnp.asarray

    def _rec_inputs():
        import jax
        import jax.numpy as jnp
        _rk = jax.random.key(seed)
        x = -0.0003929 + 0.9999 * jax.random.normal(jax.random.fold_in(_rk, 1), (16, 128, 256), jnp.float32)
        _lenS = 128 - jax.random.randint(jax.random.fold_in(_rk, 7), (16,), 0, max(1, 128 // 4) + 1, jnp.int32)
        _lenS2 = 128 - jax.random.randint(jax.random.fold_in(_rk, 8), (16,), 0, max(1, 128 // 4) + 1, jnp.int32)
        cond_1 = jax.random.uniform(jax.random.fold_in(_rk, 11), (16, 1), jnp.float32, 0.0, 1.37214)
        itok_B_0_7 = jax.random.randint(jax.random.fold_in(_rk, 12), (16,), 0, 8, jnp.int32)
        return (x, cond_1, itok_B_0_7)
    x, cond_1, itok_B_0_7 = _rec_inputs()

    def _L0_cond_setup():
        import jax, jax.numpy as jnp
        import numpy as np
        B, S, D_MODEL, NHEAD = (4, 256, 256, 16)
        HEAD_DIM = D_MODEL // NHEAD
        key = jax.random.key(seed)
        ks = jax.random.split(key, 6)
        scale = 1.0 / np.sqrt(D_MODEL)
        return {'hidden_states': jax.random.normal(ks[0], (B, S, D_MODEL), dtype=jnp.float32), 'attention_precision': jax.random.uniform(ks[1], (B, 1, 1), dtype=jnp.float32, minval=0.5, maxval=2.0), 'Wq': jax.random.normal(ks[2], (D_MODEL, D_MODEL), dtype=jnp.float32) * scale, 'Wk': jax.random.normal(ks[3], (D_MODEL, D_MODEL), dtype=jnp.float32) * scale, 'Wv': jax.random.normal(ks[4], (D_MODEL, D_MODEL), dtype=jnp.float32) * scale, 'Wo': jax.random.normal(ks[5], (D_MODEL, D_MODEL), dtype=jnp.float32) * scale}
    _L0_cond_all = _L0_cond_setup()
    _L0_cond_in = {k: v for k, v in _L0_cond_all.items() if k in ('Wq', 'Wk', 'Wv', 'Wo')}
    del _L0_cond_all

    def _L0_attn_setup():
        import jax, jax.numpy as jnp
        import numpy as np
        HS = 256
        NK = 16
        NV = 32
        DK = 128
        DV = 128
        KCONV = 4
        CHUNK = 64
        EPS = 1e-06
        KEY_DIM = NK * DK
        VAL_DIM = NV * DV
        CONV_DIM = 2 * KEY_DIM + VAL_DIM
        SEQ = 512

        def _l2norm(x, eps=1e-06):
            return x * jax.lax.rsqrt(jnp.sum(x * x, axis=-1, keepdims=True) + eps)

        def _causal_conv(x, w):
            K = w.shape[1]
            xp = jnp.pad(x, ((0, 0), (K - 1, 0), (0, 0)))
            s = x.shape[1]
            out = xp[:, 0:s, :] * w[:, 0]
            for j in range(1, K):
                out = out + xp[:, j:j + s, :] * w[:, j]
            return out

        def _chunk_gated_delta_rule(q, k, v, g, beta):
            q = _l2norm(q)
            k = _l2norm(k)
            tr = lambda x: jnp.swapaxes(x, 1, 2).astype(jnp.float32)
            q, k, v = (tr(q), tr(k), tr(v))
            g = jnp.swapaxes(g, 1, 2).astype(jnp.float32)
            beta = jnp.swapaxes(beta, 1, 2).astype(jnp.float32)
            b, h, s, dk = k.shape
            dv = v.shape[-1]
            pad = -s % CHUNK
            if pad:
                p4 = ((0, 0), (0, 0), (0, pad), (0, 0))
                p3 = ((0, 0), (0, 0), (0, pad))
                q = jnp.pad(q, p4)
                k = jnp.pad(k, p4)
                v = jnp.pad(v, p4)
                g = jnp.pad(g, p3)
                beta = jnp.pad(beta, p3)
            t = s + pad
            nc = t // CHUNK
            q = q * dk ** (-0.5)
            v_beta = v * beta[..., None]
            k_beta = k * beta[..., None]
            resh = lambda x: x.reshape(b, h, nc, CHUNK, x.shape[-1])
            q, k, v, k_beta, v_beta = map(resh, (q, k, v, k_beta, v_beta))
            g = jnp.cumsum(g.reshape(b, h, nc, CHUNK), axis=-1)
            decay = jnp.tril(jnp.exp(jnp.tril(g[..., :, None] - g[..., None, :])))
            A = jnp.tril(-(k_beta @ jnp.swapaxes(k, -1, -2)) * decay, -1)
            eye = jnp.eye(CHUNK, dtype=jnp.float32)
            T = jax.scipy.linalg.solve_triangular(eye - A, jnp.broadcast_to(eye, A.shape), lower=True)
            u = T @ v_beta
            w = T @ (k_beta * jnp.exp(g)[..., None])
            g_last = g[..., -1]
            mv = lambda x: jnp.moveaxis(x, 2, 0)
            qs, ks, us, ws, decs = map(mv, (q, k, u, w, decay))
            gs = mv(g)
            gls = mv(g_last)

            def step(state, inp):
                q_i, k_i, u_i, w_i, dec_i, g_i, gl = inp
                attn = jnp.tril(q_i @ jnp.swapaxes(k_i, -1, -2) * dec_i)
                v_new = u_i - w_i @ state
                out_i = q_i * jnp.exp(g_i)[..., None] @ state + attn @ v_new
                kd = k_i * jnp.exp(gl[..., None] - g_i)[..., None]
                state = state * jnp.exp(gl)[..., None, None] + jnp.swapaxes(kd, -1, -2) @ v_new
                return (state, out_i)
            state0 = jnp.zeros((b, h, dk, dv), jnp.float32)
            _, outs = jax.lax.scan(step, state0, (qs, ks, us, ws, decs, gs, gls))
            out = jnp.moveaxis(outs, 0, 2).reshape(b, h, t, dv)[:, :, :s]
            return jnp.swapaxes(out, 1, 2)
        key = jax.random.key(seed)
        ks = jax.random.split(key, 9)
        n = lambda k, shp, sc: jax.random.normal(k, shp, jnp.float32) * sc
        return {'hidden_states': jax.random.normal(ks[0], (1, SEQ, HS), jnp.float32), 'W_qkv': n(ks[1], (HS, CONV_DIM), 0.02), 'W_z': n(ks[2], (HS, VAL_DIM), 0.02), 'W_b': n(ks[3], (HS, NV), 0.02), 'W_a': n(ks[4], (HS, NV), 0.02), 'conv_w': n(ks[5], (CONV_DIM, KCONV), 0.2), 'dt_bias': jnp.ones((NV,), jnp.float32), 'A_log': jnp.log(jax.random.uniform(ks[6], (NV,), jnp.float32, 0.5, 8.0)), 'norm_w': jnp.ones((DV,), jnp.float32), 'W_out': n(ks[7], (VAL_DIM, HS), 0.02)}
    _L0_attn_all = _L0_attn_setup()
    _L0_attn_in = {k: v for k, v in _L0_attn_all.items() if k in ('W_qkv', 'W_z', 'W_b', 'W_a', 'conv_w', 'dt_bias', 'A_log', 'norm_w', 'W_out')}
    del _L0_attn_all

    def _L0_cond2_setup():
        import jax, jax.numpy as jnp
        import numpy as np

        def _lora_linear(x, W, A, B, adapter_indices):
            base = jnp.einsum('bsd,df->bsf', x, W)
            Ai = A[adapter_indices]
            Bi = B[adapter_indices]
            lora = jnp.einsum('bsr,brf->bsf', jnp.einsum('bsd,bdr->bsr', x, Ai), Bi)
            return base + lora
        key = jax.random.key(seed)
        ks = jax.random.split(key, 10)
        H, I, N, R = (256, 1024, 8, 16)
        B, S = (4, 256)
        std_h = 1.0 / np.sqrt(H)
        std_i = 1.0 / np.sqrt(I)
        x = jax.random.normal(ks[0], (B, S, H), dtype=jnp.float32)
        adapter_indices = jax.random.randint(ks[1], (B,), 0, N, dtype=jnp.int32)
        Wg = jax.random.normal(ks[2], (H, I), dtype=jnp.float32) * std_h
        Wu = jax.random.normal(ks[3], (H, I), dtype=jnp.float32) * std_h
        Wd = jax.random.normal(ks[4], (I, H), dtype=jnp.float32) * std_i
        Ag = jax.random.normal(ks[5], (N, H, R), dtype=jnp.float32) * std_h
        Bg = jnp.zeros((N, R, I), dtype=jnp.float32) + 0.01
        Au = jax.random.normal(ks[6], (N, H, R), dtype=jnp.float32) * std_h
        Bu = jnp.zeros((N, R, I), dtype=jnp.float32) + 0.01
        Ad = jax.random.normal(ks[7], (N, I, R), dtype=jnp.float32) * std_i
        Bd = jnp.zeros((N, R, H), dtype=jnp.float32) + 0.01
        return {'x': x, 'Wg': Wg, 'Wu': Wu, 'Wd': Wd, 'Ag': Ag, 'Bg': Bg, 'Au': Au, 'Bu': Bu, 'Ad': Ad, 'Bd': Bd, 'adapter_indices': adapter_indices}
    _L0_cond2_all = _L0_cond2_setup()
    _L0_cond2_in = {k: v for k, v in _L0_cond2_all.items() if k in ('Wg', 'Wu', 'Wd', 'Ag', 'Bg', 'Au', 'Bu', 'Ad', 'Bd')}
    del _L0_cond2_all

    def _L0_ffn_setup():
        import jax, jax.numpy as jnp
        import numpy as np
        B, S, H, I = (1, 64, 256, 768)

        def _quantized_matmul(x, w, scale):
            wq = w.astype(jnp.float8_e4m3fn).astype(x.dtype)
            y = jnp.einsum('bsi,io->bso', x, wq)
            return y * scale
        key = jax.random.key(seed)
        ks = jax.random.split(key, 7)
        return {'x': jax.random.normal(ks[0], (B, S, H), dtype=jnp.float32), 'gate_w': jax.random.normal(ks[1], (H, I), dtype=jnp.float32) * 0.02, 'up_w': jax.random.normal(ks[2], (H, I), dtype=jnp.float32) * 0.02, 'down_w': jax.random.normal(ks[3], (I, H), dtype=jnp.float32) * 0.02, 'gate_scale': jax.random.uniform(ks[4], (I,), dtype=jnp.float32, minval=0.5, maxval=1.5), 'up_scale': jax.random.uniform(ks[5], (I,), dtype=jnp.float32, minval=0.5, maxval=1.5), 'down_scale': jax.random.uniform(ks[6], (H,), dtype=jnp.float32, minval=0.5, maxval=1.5)}
    _L0_ffn_all = _L0_ffn_setup()
    _L0_ffn_in = {k: v for k, v in _L0_ffn_all.items() if k in ('gate_w', 'up_w', 'down_w', 'gate_scale', 'up_scale', 'down_scale')}
    del _L0_ffn_all
    return {'x': x, 'cond_1': cond_1, 'itok_B_0_7': itok_B_0_7, 'L0_cond_Wq': _L0_cond_in['Wq'], 'L0_cond_Wk': _L0_cond_in['Wk'], 'L0_cond_Wv': _L0_cond_in['Wv'], 'L0_cond_Wo': _L0_cond_in['Wo'], 'L0_attn_W_qkv': _L0_attn_in['W_qkv'], 'L0_attn_W_z': _L0_attn_in['W_z'], 'L0_attn_W_b': _L0_attn_in['W_b'], 'L0_attn_W_a': _L0_attn_in['W_a'], 'L0_attn_conv_w': _L0_attn_in['conv_w'], 'L0_attn_dt_bias': _L0_attn_in['dt_bias'], 'L0_attn_A_log': _L0_attn_in['A_log'], 'L0_attn_norm_w': _L0_attn_in['norm_w'], 'L0_attn_W_out': _L0_attn_in['W_out'], 'L0_cond2_Wg': _L0_cond2_in['Wg'], 'L0_cond2_Wu': _L0_cond2_in['Wu'], 'L0_cond2_Wd': _L0_cond2_in['Wd'], 'L0_cond2_Ag': _L0_cond2_in['Ag'], 'L0_cond2_Bg': _L0_cond2_in['Bg'], 'L0_cond2_Au': _L0_cond2_in['Au'], 'L0_cond2_Bu': _L0_cond2_in['Bu'], 'L0_cond2_Ad': _L0_cond2_in['Ad'], 'L0_cond2_Bd': _L0_cond2_in['Bd'], 'L0_ffn_gate_w': _L0_ffn_in['gate_w'], 'L0_ffn_up_w': _L0_ffn_in['up_w'], 'L0_ffn_down_w': _L0_ffn_in['down_w'], 'L0_ffn_gate_scale': _L0_ffn_in['gate_scale'], 'L0_ffn_up_scale': _L0_ffn_in['up_scale'], 'L0_ffn_down_scale': _L0_ffn_in['down_scale']}

def reference(x, cond_1, itok_B_0_7, L0_cond_Wq, L0_cond_Wk, L0_cond_Wv, L0_cond_Wo, L0_attn_W_qkv, L0_attn_W_z, L0_attn_W_b, L0_attn_W_a, L0_attn_conv_w, L0_attn_dt_bias, L0_attn_A_log, L0_attn_norm_w, L0_attn_W_out, L0_cond2_Wg, L0_cond2_Wu, L0_cond2_Wd, L0_cond2_Ag, L0_cond2_Bg, L0_cond2_Au, L0_cond2_Bu, L0_cond2_Ad, L0_cond2_Bd, L0_ffn_gate_w, L0_ffn_up_w, L0_ffn_down_w, L0_ffn_gate_scale, L0_ffn_up_scale, L0_ffn_down_scale):
    import jax
    import jax.numpy as jnp

    def _L0_cond_ref(hidden_states, attention_precision, Wq, Wk, Wv, Wo):
        import jax, jax.numpy as jnp
        import numpy as np
        B, S, D_MODEL, NHEAD = (4, 256, 256, 16)
        HEAD_DIM = D_MODEL // NHEAD
        b, s, _ = hidden_states.shape

        def proj(x, W):
            y = jnp.einsum('bsd,ed->bse', x, W)
            return y.reshape(b, s, NHEAD, HEAD_DIM).transpose(0, 2, 1, 3)
        q = proj(hidden_states, Wq)
        k = proj(hidden_states, Wk)
        v = proj(hidden_states, Wv)
        beta = jnp.minimum(attention_precision, 4.0)[:, None]
        q = q * beta
        scores = jnp.einsum('bhqd,bhkd->bhqk', q, k) / np.sqrt(HEAD_DIM)
        causal = jnp.tril(jnp.ones((s, s), dtype=bool))
        scores = jnp.where(causal, scores, jnp.finfo(scores.dtype).min)
        attn = jax.nn.softmax(scores, axis=-1)
        out = jnp.einsum('bhqk,bhkd->bhqd', attn, v)
        out = out.transpose(0, 2, 1, 3).reshape(b, s, D_MODEL)
        return jnp.einsum('bsd,ed->bse', out, Wo)

    def _L0_attn_ref(hidden_states, W_qkv, W_z, W_b, W_a, conv_w, dt_bias, A_log, norm_w, W_out):
        import jax, jax.numpy as jnp
        import numpy as np
        HS = 256
        NK = 16
        NV = 32
        DK = 128
        DV = 128
        KCONV = 4
        CHUNK = 64
        EPS = 1e-06
        KEY_DIM = NK * DK
        VAL_DIM = NV * DV
        CONV_DIM = 2 * KEY_DIM + VAL_DIM
        SEQ = 512

        def _l2norm(x, eps=1e-06):
            return x * jax.lax.rsqrt(jnp.sum(x * x, axis=-1, keepdims=True) + eps)

        def _causal_conv(x, w):
            K = w.shape[1]
            xp = jnp.pad(x, ((0, 0), (K - 1, 0), (0, 0)))
            s = x.shape[1]
            out = xp[:, 0:s, :] * w[:, 0]
            for j in range(1, K):
                out = out + xp[:, j:j + s, :] * w[:, j]
            return out

        def _chunk_gated_delta_rule(q, k, v, g, beta):
            q = _l2norm(q)
            k = _l2norm(k)
            tr = lambda x: jnp.swapaxes(x, 1, 2).astype(jnp.float32)
            q, k, v = (tr(q), tr(k), tr(v))
            g = jnp.swapaxes(g, 1, 2).astype(jnp.float32)
            beta = jnp.swapaxes(beta, 1, 2).astype(jnp.float32)
            b, h, s, dk = k.shape
            dv = v.shape[-1]
            pad = -s % CHUNK
            if pad:
                p4 = ((0, 0), (0, 0), (0, pad), (0, 0))
                p3 = ((0, 0), (0, 0), (0, pad))
                q = jnp.pad(q, p4)
                k = jnp.pad(k, p4)
                v = jnp.pad(v, p4)
                g = jnp.pad(g, p3)
                beta = jnp.pad(beta, p3)
            t = s + pad
            nc = t // CHUNK
            q = q * dk ** (-0.5)
            v_beta = v * beta[..., None]
            k_beta = k * beta[..., None]
            resh = lambda x: x.reshape(b, h, nc, CHUNK, x.shape[-1])
            q, k, v, k_beta, v_beta = map(resh, (q, k, v, k_beta, v_beta))
            g = jnp.cumsum(g.reshape(b, h, nc, CHUNK), axis=-1)
            decay = jnp.tril(jnp.exp(jnp.tril(g[..., :, None] - g[..., None, :])))
            A = jnp.tril(-(k_beta @ jnp.swapaxes(k, -1, -2)) * decay, -1)
            eye = jnp.eye(CHUNK, dtype=jnp.float32)
            T = jax.scipy.linalg.solve_triangular(eye - A, jnp.broadcast_to(eye, A.shape), lower=True)
            u = T @ v_beta
            w = T @ (k_beta * jnp.exp(g)[..., None])
            g_last = g[..., -1]
            mv = lambda x: jnp.moveaxis(x, 2, 0)
            qs, ks, us, ws, decs = map(mv, (q, k, u, w, decay))
            gs = mv(g)
            gls = mv(g_last)

            def step(state, inp):
                q_i, k_i, u_i, w_i, dec_i, g_i, gl = inp
                attn = jnp.tril(q_i @ jnp.swapaxes(k_i, -1, -2) * dec_i)
                v_new = u_i - w_i @ state
                out_i = q_i * jnp.exp(g_i)[..., None] @ state + attn @ v_new
                kd = k_i * jnp.exp(gl[..., None] - g_i)[..., None]
                state = state * jnp.exp(gl)[..., None, None] + jnp.swapaxes(kd, -1, -2) @ v_new
                return (state, out_i)
            state0 = jnp.zeros((b, h, dk, dv), jnp.float32)
            _, outs = jax.lax.scan(step, state0, (qs, ks, us, ws, decs, gs, gls))
            out = jnp.moveaxis(outs, 0, 2).reshape(b, h, t, dv)[:, :, :s]
            return jnp.swapaxes(out, 1, 2)
        b, s, _ = hidden_states.shape
        mixed = hidden_states @ W_qkv
        z = (hidden_states @ W_z).reshape(b, s, NV, DV)
        beta = jax.nn.sigmoid(hidden_states @ W_b)
        g = -jnp.exp(A_log) * jax.nn.softplus(hidden_states @ W_a + dt_bias)
        mixed = jax.nn.silu(_causal_conv(mixed, conv_w))
        q, k, v = jnp.split(mixed, [KEY_DIM, 2 * KEY_DIM], axis=-1)
        q = q.reshape(b, s, NK, DK)
        k = k.reshape(b, s, NK, DK)
        v = v.reshape(b, s, NV, DV)
        rep = NV // NK
        q = jnp.repeat(q, rep, axis=2)
        k = jnp.repeat(k, rep, axis=2)
        core = _chunk_gated_delta_rule(q, k, v, g, beta)
        core = core * jax.lax.rsqrt(jnp.mean(core * core, axis=-1, keepdims=True) + EPS) * norm_w
        core = core * jax.nn.silu(z)
        return core.reshape(b, s, VAL_DIM) @ W_out

    def _L0_cond2_ref(x, Wg, Wu, Wd, Ag, Bg, Au, Bu, Ad, Bd, adapter_indices):
        import jax, jax.numpy as jnp
        import numpy as np

        def _lora_linear(x, W, A, B, adapter_indices):
            base = jnp.einsum('bsd,df->bsf', x, W)
            Ai = A[adapter_indices]
            Bi = B[adapter_indices]
            lora = jnp.einsum('bsr,brf->bsf', jnp.einsum('bsd,bdr->bsr', x, Ai), Bi)
            return base + lora
        gate = _lora_linear(x, Wg, Ag, Bg, adapter_indices)
        up = _lora_linear(x, Wu, Au, Bu, adapter_indices)
        h = jax.nn.silu(gate) * up
        return _lora_linear(h, Wd, Ad, Bd, adapter_indices)

    def _L0_ffn_ref(x, gate_w, up_w, down_w, gate_scale, up_scale, down_scale):
        import jax, jax.numpy as jnp
        import numpy as np
        B, S, H, I = (1, 64, 256, 768)

        def _quantized_matmul(x, w, scale):
            wq = w.astype(jnp.float8_e4m3fn).astype(x.dtype)
            y = jnp.einsum('bsi,io->bso', x, wq)
            return y * scale
        gate = jax.nn.silu(_quantized_matmul(x, gate_w, gate_scale))
        up = _quantized_matmul(x, up_w, up_scale)
        fuse = gate * up
        return _quantized_matmul(fuse, down_w, down_scale)
    x = x + _L0_attn_ref(_L0_cond_ref(x, cond_1[:, None, :], L0_cond_Wq, L0_cond_Wk, L0_cond_Wv, L0_cond_Wo), L0_attn_W_qkv, L0_attn_W_z, L0_attn_W_b, L0_attn_W_a, L0_attn_conv_w, L0_attn_dt_bias, L0_attn_A_log, L0_attn_norm_w, L0_attn_W_out)
    x = x + _L0_ffn_ref(_L0_cond2_ref(x, L0_cond2_Wg, L0_cond2_Wu, L0_cond2_Wd, L0_cond2_Ag, L0_cond2_Bg, L0_cond2_Au, L0_cond2_Bu, L0_cond2_Ad, L0_cond2_Bd, itok_B_0_7), L0_ffn_gate_w, L0_ffn_up_w, L0_ffn_down_w, L0_ffn_gate_scale, L0_ffn_up_scale, L0_ffn_down_scale)
    return x

_drawn_inputs = setup_inputs


def setup_inputs(seed=0):
    import zlib

    import numpy as np

    out = dict(_drawn_inputs(seed))
    spreads = {'L0_attn_dt_bias': (1.0, 0.2),
     'L0_attn_norm_w': (1.0, 0.2),
     'L0_cond2_Bg': (0.009999999776482582, 0.2),
     'L0_cond2_Bu': (0.009999999776482582, 0.2),
     'L0_cond2_Bd': (0.009999999776482582, 0.2)}
    factors = {}
    for name, (base, spread) in spreads.items():
        noise = np.random.default_rng([zlib.crc32(name.encode()), seed]).standard_normal(out[name].shape)
        drawn = base * np.exp(spread * noise) if base else spread * noise
        out[name] = jnp.asarray(drawn.astype(out[name].dtype))
    for name, factor in factors.items():
        out[name] = (out[name] * factor).astype(out[name].dtype)
    return out
```

```python
from contextlib import ExitStack

import concourse.bass as bass
from concourse import mybir

F32 = mybir.dt.float32
BF16 = mybir.dt.bfloat16
FP8 = mybir.dt.float8e4
I32 = mybir.dt.int32
ALU = mybir.AluOpType
ACT = mybir.ActivationFunctionType
AX_X = mybir.AxisListType.X

P = 128
B, S, D = 16, 128, 256
DC = D // P
G = 4
NG = B // G
TG = G * S
NH_A, HD_A = 16, 16
NK, NV, DK, DV, KC = 16, 32, 128, 128, 4
HH = NV // NK
UN = B * HH
UG = G * HH
BK = 32
EPS = 1e-6
BIG = 1e30
RSQRT_SEED = 1597463007.0
N_AD, RK, I2, I3 = 8, 16, 1024, 768


class Signal:

    def __init__(self, sem, per):
        self.sem, self.per, self.passed = sem, per, {}

    def wait(self, eng, step, n):
        seen, most = self.passed.get(id(eng), (None, 0))
        if seen is step and most >= n:
            return
        self.passed[id(eng)] = (step, n)
        value = step * self.per + n
        if isinstance(value, int) and value <= 0:
            return
        eng.wait_ge(self.sem, value)


def first_then_loop(eng, steps, body):
    body(0)
    with eng.Fori(1, steps) as step:
        body(step)


class Banks:

    def __init__(self, banks, uses):
        assert len(uses) % len(banks) == 0
        self.banks, self.uses = banks, uses
        self.index = {key: n for n, (key, _, _) in enumerate(uses)}

    def bank(self, key):
        return self.banks[self.index[key] % len(self.banks)]

    def wait_free(self, eng, step, key):
        n = self.index[key] - len(self.banks)
        _, reader, count = self.uses[n]
        reader.wait(eng, step, count if n >= 0 else count - reader.per)


def build(nc, x, prec, adapter, Wq, Wk, Wv, Wo, W_qkv, W_z, W_b, W_a, conv_w, dt_bias, A_log, norm_w,
          W_out, Wg, Wu, Wd, Ag, Bg, Au, Bu, Ad, Bd, gate_w, up_w, down_w, gate_s, up_s, down_s, out):
    top = ExitStack()

    def sem(name):
        return top.enter_context(nc.semaphore(name))

    def sig(name, per):
        return Signal(sem(name), per)

    def tile(stack, name, shape, dt=F32):
        return stack.enter_context(nc.sbuf_tensor(name, shape, dt))

    with top:
        ps = [top.enter_context(nc.psum_tensor(f"bank{i}", [P, 512], F32)) for i in range(8)]

        acc = tile(top, "acc", [P, B, D])
        ident = tile(top, "ident", [P, P])
        identb = tile(top, "identb", [P, P], BF16)
        later_t = tile(top, "later_t", [P, P])
        upto_t = tile(top, "upto_t", [P, P])
        ones = tile(top, "ones", [P, 1])
        cm_qk = tile(top, "cm_qk", [P, P], BF16)
        cm_kq = tile(top, "cm_kq", [P, P], BF16)
        head_even = tile(top, "head_even", [P, 1])
        head_odd = tile(top, "head_odd", [P, 1])
        part = tile(top, "part", [P, 3], I32)
        own = tile(top, "own", [P, 1])

        consts = sem("consts")
        x_in = sem("x_in")

        fr = ExitStack()
        beta = tile(top, "beta", [P, NK, B, HH])
        gdec = tile(top, "gdec", [P, NK, B, HH])
        xT = tile(top, "xT", [P, DC, B * S])
        w_raw = tile(fr, "w_raw", [P, 4, 2, D])
        w_t = tile(fr, "w_t", [P, 4, 2, D])
        w_ba = tile(fr, "w_ba", [P, DC, 2, NV])
        xg = tile(fr, "xg", [P, G, D])
        xgT = tile(fr, "xgT", [P, DC, TG])
        precb = tile(fr, "precb", [P, B])
        precs = tile(fr, "precs", [P, B])
        qTa = tile(fr, "qTa", [P, 2, TG])
        kTe = tile(fr, "kTe", [P, 2, TG])
        kTo = tile(fr, "kTo", [P, 2, TG])
        vg = tile(fr, "vg", [P, G, D])
        rmax = tile(fr, "rmax", [P, 2, 4])
        nmax = tile(fr, "nmax", [P, 2, 4])
        rsum = tile(fr, "rsum", [P, 2, NH_A])
        rinv = tile(fr, "rinv", [P, 2, NH_A])
        prob = tile(fr, "prob", [P, 2, 4, P])
        probT = tile(fr, "probT", [P, 2, 4, P])
        oa = tile(fr, "oa", [P, G, D])
        oTg = tile(fr, "oTg", [P, 2, TG])
        cTg = tile(fr, "cTg", [P, DC, TG])
        ba = tile(fr, "ba", [P, 2 * NV, B])
        dtb = tile(fr, "dtb", [P, NV])
        alog = tile(fr, "alog", [P, NV])
        nega = tile(fr, "nega", [P, NV])
        sp = [tile(fr, f"sp{i}", [P, NV, B]) for i in range(4)]

        fr.close()
        gd = ExitStack()
        wqk = tile(gd, "wqk", [P, DC, 2, P])
        wv = tile(gd, "wv", [P, DC, HH * DV])
        wz = tile(gd, "wz", [P, DC, HH * DV])
        wo_in = tile(gd, "wo_in", [P, HH, D])
        wo = tile(gd, "wo", [P, HH, D])
        cw = tile(gd, "cw", [P, 2 + HH, KC])
        nw = tile(gd, "nw", [P, 1])
        cbuf = tile(gd, "cbuf", [P, 3, TG])
        kq = tile(gd, "kq", [P, NG, 2, TG])
        sqb = tile(gd, "sqb", [P, 2, TG])
        V = tile(gd, "V", [P, UG, P])
        E = tile(gd, "E", [P, 2, 4, P])
        Bm = tile(gd, "Bm", [P, UN, P])
        att = tile(gd, "att", [P, UN, P])
        w_tok = tile(gd, "w_tok", [P, UN, P])
        zg = tile(gd, "zg", [P, HH, B * S])
        Ue = tile(gd, "Ue", [P, UN, P])
        Le = tile(gd, "Le", [P, UN, 2 * BK])
        diag_l = tile(gd, "diag_l", [P, UN, BK])
        diag_u = tile(gd, "diag_u", [P, UN, BK])
        lane_T = tile(gd, "lane_T", [P, BK, BK])
        lane_p = tile(gd, "lane_p", [P, (BK // 2) ** 2])
        vT = tile(gd, "vT", [P, HH, TG])
        Y1 = tile(gd, "Y1", [P, 16, BK])
        Y2 = tile(gd, "Y2", [P, UG, 2 * BK])
        up = tile(gd, "up", [P, 2, 4, P])
        sqo = tile(gd, "sqo", [P, 2, 4, P])
        go = tile(gd, "go", [P, 2, 4, P])
        ksum = tile(gd, "ksum", [P, B])
        krec = tile(gd, "krec", [P, B])
        qeps = tile(gd, "qeps", [P, B])
        cpos = tile(gd, "cpos", [P, B, HH])
        cneg = tile(gd, "cneg", [P, B, HH])
        knorm = tile(gd, "knorm", [P, B])
        nt = tile(gd, "nt", [P, 3, UN])
        osc = tile(gd, "osc", [P, B, HH])
        gd.close()

        bk = ExitStack()
        wg_s = tile(bk, "wg_s", [P, DC, I2])
        wu_s = tile(bk, "wu_s", [P, DC, I2])
        wd_s = tile(bk, "wd_s", [P, I2 // P, D])
        ag_s = tile(bk, "ag_s", [P, DC, N_AD, RK])
        au_s = tile(bk, "au_s", [P, DC, N_AD, RK])
        ad_s = tile(bk, "ad_s", [P, I2 // P, N_AD, RK])
        bg_s = tile(bk, "bg_s", [P, I2])
        bu_s = tile(bk, "bu_s", [P, I2])
        bd_s = tile(bk, "bd_s", [P, D])
        qg_s = tile(bk, "qg_s", [P, DC * I3])
        qu_s = tile(bk, "qu_s", [P, DC * I3])
        qd_s = tile(bk, "qd_s", [P, I3 // P * D])
        q8a = tile(bk, "q8a", [P, DC * I3], FP8)
        q8b = tile(bk, "q8b", [P, DC * I3], FP8)
        qm = tile(bk, "qm", [P, DC * I3])
        qdif = tile(bk, "qdif", [P, DC * I3])
        gsc = tile(bk, "gsc", [P, I3 // P])
        usc = tile(bk, "usc", [P, I3 // P])
        dsc = tile(bk, "dsc", [P, D])
        idx_i = tile(bk, "idx_i", [P, B], I32)
        idx_f = tile(bk, "idx_f", [P, B])
        pick = tile(bk, "pick", [P, B])
        x1g = tile(bk, "x1g", [P, G, D])
        x1T = tile(bk, "x1T", [P, DC, TG])
        lg = tile(bk, "lg", [P, 3, TG])
        sg = tile(bk, "sg", [P, 2, TG])
        hT = tile(bk, "hT", [P, I2 // P, TG])
        yT = tile(bk, "yT", [P, DC, TG])
        fT = tile(bk, "fT", [P, I3 // P, TG])
        og = tile(bk, "og", [P, G, D])
        dn = tile(bk, "dn", [P, 2, D])
        bk.close()

        dram_w = {0: Wq, 1: Wk, 2: Wv, 3: Wo}

        a_win = sem("a_win")
        a_small_in = sem("a_small_in")
        a_xg_in = Signal(sem("a_xg_in"), 16)
        a_wt_ready = sem("a_wt_ready")
        a_wt_read = sem("a_wt_read")
        a_prec = sem("a_prec")
        a_x_ready, a_x_read = sig("a_x_ready", 2), sig("a_x_read", 2)
        a_q_ready, a_q_read = sig("a_q_ready", 2), sig("a_q_read", 2)
        a_k_ready, a_k_read = sig("a_k_ready", 2), sig("a_k_read", 4)
        a_v_ready, a_v_read = sig("a_v_ready", 2), sig("a_v_read", 2)
        a_s_ready, a_max, a_nmax = sig("a_s_ready", 16), sig("a_max", 16), sig("a_nmax", 16)
        a_prob = sig("a_prob", 16)
        a_pt_ready, a_pt_read = sig("a_pt_ready", 16), sig("a_pt_read", 16)
        a_pv_ready = sig("a_pv_ready", 16)
        a_rinv, a_o_read = sig("a_rinv", G), sig("a_o_read", G)
        a_ot_ready, a_ot_read = sig("a_ot_ready", 2), sig("a_ot_read", 2)
        a_c_ready, a_c_read = sig("a_c_ready", 2), sig("a_c_read", 2)
        a_xT = sig("a_xT", 1)
        a_ba_ready, a_ba_read = sig("a_ba_ready", G), sig("a_ba_read", G)
        gates, gates_act, picked = sem("gates"), sem("gates_act"), sem("picked")

        d_nw_in, d_cw_in = sem("d_nw_in"), Signal(sem("d_cw_in"), 48)
        d_qk_in = Signal(sem("d_qk_in"), 32)
        d_v_in, d_z_in, d_o_in = (Signal(sem(n), 16) for n in ("d_v_in", "d_z_in", "d_o_in"))
        d_wo = sig("d_wo", 1)
        d_qk_ready, d_v_ready, d_z_ready = sig("d_qk_ready", 8), sig("d_v_ready", 8), sig("d_z_ready", 8)
        d_tap, d_conv, d_conv_step = sig("d_tap", 16), sig("d_conv", 16), sig("d_conv_step", 32)
        d_silu, d_zg = sig("d_silu", 16), sig("d_zg", 8)
        d_sq, d_ss_ready, d_ss_read = sig("d_sq", NG), sig("d_ss_ready", NG), sig("d_ss_read", NG)
        d_rec, d_c1, d_c, d_cneg = (sig(n, NG) for n in ("d_rec", "d_c1", "d_c", "d_cneg"))
        d_V = sig("d_V", NG)
        d_gk_ready, d_ea_ready, d_E, d_B = (sig(n, 8) for n in ("d_gk_ready", "d_ea_ready", "d_E", "d_B"))
        d_diag = sig("d_diag", NG)
        d_lanes, d_solve, d_unlane = sig("d_lanes", 3), sig("d_solve", 2 * (BK - 1)), sig("d_unlane", 2)
        d_newt, d_knorm = sig("d_newt", 11), sig("d_knorm", 1)
        d_spread = sig("d_spread", 8)
        d_y1_ready, d_y1_read, d_t1_ready, d_t1_read = (sig(n, 4) for n in
                                                        ("d_y1_ready", "d_y1_read", "d_t1_ready", "d_t1_read"))
        d_y2_ready, d_y2_read, d_u2_ready, d_u2_read = (sig(n, NG) for n in
                                                        ("d_y2_ready", "d_y2_read", "d_u2_ready", "d_u2_read"))
        d_vt_ready, d_w = sig("d_vt_ready", 8), sig("d_w", 8)
        d_u_ready, d_up, d_o_ready, d_sqo, d_go = (sig(n, 8) for n in ("d_u_ready", "d_up", "d_o_ready", "d_sqo", "d_go"))
        d_so_ready, d_so_read, d_nto, d_osc = sig("d_so_ready", 8), sig("d_so_read", NG), sig("d_nto", 11 * NG), sig("d_osc", NG)
        d_y_ready, d_acc_step, d_acc = sig("d_y_ready", B), sig("d_acc_step", B), sig("d_acc", B)
        zeroed = sem("zeroed")

        m_in = sem("m_in")
        m_q = sem("m_q")
        m_idx, m_pick = sem("m_idx"), sem("m_pick")
        m_x1, m_x1T_ready, m_x1T = sig("m_x1", 1), sig("m_x1T_ready", 2), sig("m_x1T", 2)
        m_lg_ready, m_lg = sig("m_lg_ready", 2), sig("m_lg", 2)
        m_gu_ready, m_sg, m_h = sig("m_gu_ready", 16), sig("m_sg", 8), sig("m_h", 8)
        m_ld_ready, m_ld = sig("m_ld_ready", 2), sig("m_ld", 2)
        m_y_ready, m_y = sig("m_y_ready", 2), sig("m_y", 2)
        m_fgu_ready, m_fs, m_f = sig("m_fgu_ready", 12), sig("m_fs", 6), sig("m_f", 6)
        m_d_ready, m_dn, m_og = sig("m_d_ready", 4), sig("m_dn", 4), sig("m_og", 4)
        m_out = Signal(sem("m_out"), 16)

        A, Z, Q, VV, VT, M1, M2, UO = "A", "z", "qk", "v", "vt", "m1", "m2", "uo"
        PE_ORDER = [(Q, 0), (Z, 0), (Q, 1), (A, 0), (Z, 1), (Q, 2), (A, 1), (Z, 2), (Q, 3), (A, 2), (Z, 3),
                    (VV, 0), (A, 3), (VV, 1), (VT, 0), (VV, 2), (VT, 1), (VV, 3), (VT, 2), (VT, 3),
                    (M1, 0), (M1, 1), (M2, 0), (M2, 1), (UO, 0), (M2, 2), (UO, 1), (M2, 3), (UO, 2), (UO, 3)]
        CONV = [(Q, g, t) for g in range(NG) for t in range(2)] + [(VV, g, t) for g in range(NG) for t in range(HH)]
        conv_n = {c: n for n, c in enumerate(CONV)}

        def conv_row(kind, t):
            return t + (2 if kind == VV else 0)

        proj_uses, work_uses, small_uses = [], [], []
        for kind, g in PE_ORDER:
            if kind in (Q, VV):
                proj_uses += [((kind, g, t), d_conv, conv_n[kind, g, t] + 1) for t in range(2)]
            elif kind == Z:
                proj_uses += [((Z, g, t), d_zg, 2 * g + t + 1) for t in range(2)]
            elif kind == A:
                small_uses += [(("ss", g), d_ss_read, g + 1)]
                work_uses += [(("gk", g, h), d_B, 2 * g + h + 1) for h in range(2)]
                work_uses += [(("ea", g, h), d_E, 2 * g + h + 1) for h in range(2)]
            elif kind == VT:
                work_uses += [(("vt", g, h), d_w, 2 * g + h + 1) for h in range(2)]
            elif kind == M1:
                work_uses += [(("y1", g, p), d_y1_read, 2 * g + p + 1) for p in range(2)]
                work_uses += [(("t1", g, p), d_t1_read, 2 * g + p + 1) for p in range(2)]
            elif kind == M2:
                work_uses += [(("y2", g), d_y2_read, g + 1), (("u2", g), d_u2_read, g + 1)]
            elif kind == UO:
                small_uses += [(("so", g), d_so_read, g + 1)]
                work_uses += [(("u", g, h), d_up, 2 * g + h + 1) for h in range(2)]
                work_uses += [(("o", g, h), d_go, 2 * g + h + 1) for h in range(2)]
                work_uses += [(("y", g, b), d_acc, G * g + b + 1) for b in range(G)]
        proj = Banks(ps[0:3], proj_uses)
        work = Banks(ps[3:7], work_uses)
        sums, small = Banks(ps[7:8], small_uses), ps[7]
        front = Banks(ps[0:4], [(("x", n), a_x_read, 2) for n in range(2)] + [(("q", n), a_q_read, n + 1) for n in range(2)]
                      + [(("k", n), a_k_read, 2 * n + 2) for n in range(2)] + [(("v", n), a_v_read, n + 1) for n in range(2)]
                      + [(("pv", b), a_o_read, b + 1) for b in range(G)] + [(("ot", n), a_ot_read, n + 1) for n in range(2)]
                      + [(("c", n), a_c_read, n + 1) for n in range(2)] + [(("ba", b), a_ba_read, b + 1) for b in range(G)])
        score = Banks(ps[4:6], [(n, a_prob, n + 1) for n in range(4 * G)])
        turned = Banks(ps[6:8], [(n, a_pt_read, n + 1) for n in range(4 * G)])
        pairs = []
        for c in range(I2 // P):
            pairs += [(("g", c), m_sg, c + 1), (("u", c), m_h, c + 1)]
        for c in range(I3 // P):
            pairs += [(("fg", c), m_fs, c + 1), (("fu", c), m_f, c + 1)]
        pairs = Banks(ps[0:4], pairs)
        rest = Banks(ps[4:8], [(("x", n), m_x1T, n + 1) for n in range(2)] + [(("lg", n), m_lg, n + 1) for n in range(2)]
                     + [(("ld", n), m_ld, n + 1) for n in range(2)] + [(("y", n), m_y, n + 1) for n in range(2)]
                     + [(("d", b), m_dn, b + 1) for b in range(G)])
        SK, SQ, SO = 0, B, 2 * B

        block = top.enter_context(nc.Block())
        CONSTS = 17
        GATE_STEPS = 9
        M_LOADS = 16 * (11 + 2 * DC + I2 // P + 2)

        @block.sync
        def _(sp_):
            for n in range(4):
                sp_.dma_start(w_raw[:, n, :, :], dram_w[n].rearrange("(c p) d -> p c d", p=P)).then_inc(a_win, 16)

            def load_xg(g):
                a_x_ready.wait(sp_, g, 0)
                sp_.dma_start(xg[:], x[bass.ds(g * G, G), :, :].rearrange("b t d -> t b d")).then_inc(a_xg_in.sem, 16)

            for t, v in ((dtb, dt_bias), (alog, A_log)):
                sp_.dma_start(t[:], v.rearrange("(a n) -> a n", a=1).broadcast_to([P, NV])).then_inc(a_small_in, 16)
            sp_.dma_start(precb[:], prec.rearrange("b a -> a b").broadcast_to([P, B])).then_inc(a_small_in, 16)
            for n, v in enumerate((W_b, W_a)):
                sp_.dma_start(w_ba[:, :, n, :], v.rearrange("(c p) n -> p c n", p=P)).then_inc(a_small_in, 16)
            first_then_loop(sp_, NG, load_xg)
            for g in range(NG):
                sp_.dma_start(acc[:, G * g:G * g + G, :], x[G * g:G * g + G, :, :].rearrange("b t d -> t b d")).then_inc(x_in, 16)

            sp_.wait_ge(gates, GATE_STEPS)
            taps = conv_w.rearrange("(n p) j -> p n j", p=P)
            sp_.dma_start(nw[:], norm_w.rearrange("(p a) -> p a", a=1)).then_inc(d_nw_in, 16)
            qkv = W_qkv.rearrange("(c p) n -> p c n", p=P)
            zz = W_z.rearrange("(c p) n -> p c n", p=P)

            def load_head(kh):
                d_qk_ready.wait(sp_, kh, 0)
                sp_.dma_start(wqk[:, :, 0, :], qkv[:, :, bass.ds(kh * DK + NK * DK, DK)]).then_inc(d_qk_in.sem, 16)
                sp_.dma_start(wqk[:, :, 1, :], qkv[:, :, bass.ds(kh * DK, DK)]).then_inc(d_qk_in.sem, 16)
                d_conv.wait(sp_, kh, 0)
                for t, first in ((0, kh + NK), (1, kh)):
                    sp_.dma_start(cw[:, t:t + 1, :], taps[:, bass.ds(first, 1), :]).then_inc(d_cw_in.sem, 16)
                sp_.dma_start(cw[:, 2:2 + HH, :], taps[:, bass.ds(kh * HH + 2 * NK, HH), :]).then_inc(d_cw_in.sem, 16)
                d_z_ready.wait(sp_, kh, 0)
                sp_.dma_start(wz[:], zz[:, :, bass.ds(kh * HH * DV, HH * DV)]).then_inc(d_z_in.sem, 16)
                d_v_ready.wait(sp_, kh, 0)
                sp_.dma_start(wv[:], qkv[:, :, bass.ds(kh * HH * DV + 2 * NK * DK, HH * DV)]).then_inc(d_v_in.sem, 16)
                d_wo.wait(sp_, kh, 0)
                sp_.dma_start(wo_in[:], W_out.rearrange("(h p) f -> p h f", p=P)[:, bass.ds(kh * HH, HH), :]).then_inc(d_o_in.sem, 16)

            first_then_loop(sp_, NK, load_head)

            d_acc.wait(sp_, NK, 0)
            for dst, src in (
                (wg_s[:], Wg.rearrange("(c p) n -> p c n", p=P)), (wu_s[:], Wu.rearrange("(c p) n -> p c n", p=P)),
                (bg_s[:], Bg.rearrange("n r i -> (n r) i")), (bu_s[:], Bu.rearrange("n r i -> (n r) i")),
                (wd_s[:], Wd.rearrange("(c p) n -> p c n", p=P)), (bd_s[:], Bd.rearrange("n r i -> (n r) i")),
                (qg_s[:].rearrange("p (c n) -> p c n", c=DC), gate_w.rearrange("(c p) n -> p c n", p=P)),
                (qu_s[:].rearrange("p (c n) -> p c n", c=DC), up_w.rearrange("(c p) n -> p c n", p=P)),
                (qd_s[:].rearrange("p (c n) -> p c n", c=I3 // P), down_w.rearrange("(c p) n -> p c n", p=P)),
                (dsc[:], down_s.rearrange("(a n) -> a n", a=1).broadcast_to([P, D])),
                (idx_i[:], adapter.rearrange("(a n) -> a n", a=1).broadcast_to([P, B])),
            ):
                sp_.dma_start(dst, src).then_inc(m_in, 16)
            for c in range(DC):
                sp_.dma_start(ag_s[:, c], Ag[:, c * P:(c + 1) * P, :].rearrange("n p r -> p n r")).then_inc(m_in, 16)
                sp_.dma_start(au_s[:, c], Au[:, c * P:(c + 1) * P, :].rearrange("n p r -> p n r")).then_inc(m_in, 16)
            for c in range(I2 // P):
                sp_.dma_start(ad_s[:, c], Ad[:, c * P:(c + 1) * P, :].rearrange("n p r -> p n r")).then_inc(m_in, 16)
            with nc.allow_non_contiguous_dma("scales by channel, once"):
                sp_.dma_start(gsc[:], gate_s.rearrange("(c p) -> p c", p=P)).then_inc(m_in, 16)
                sp_.dma_start(usc[:], up_s.rearrange("(c p) -> p c", p=P)).then_inc(m_in, 16)

            def store(g):
                m_og.wait(sp_, g, 4)
                sp_.dma_start(out[bass.ds(g * G, G), :, :].rearrange("b t d -> t b d"), og[:]).then_inc(m_out.sem, 16)

            first_then_loop(sp_, NG, store)
            m_out.wait(sp_, NG, 0)



        @block.gpsimd
        def _(pool):
            for t, v in ((ident, 0.0), (later_t, 1.0), (upto_t, 1.0), (cm_qk, 0.0), (cm_kq, 0.0), (identb, 0.0),
                         (ones, 1.0)):
                pool.memset(t[:], v).then_inc(consts, 1)
            pool.iota(part[:, 0:1], pattern=[[0, 1]], base=0, channel_multiplier=1).then_inc(consts, 1)
            pool.wait_ge(consts, 8)
            for t in (ident, identb):
                pool.affine_select(out=t[:], in_=t[:], compare_op=ALU.not_equal, fill=1.0, base=0,
                                   pattern=[[-1, P]], channel_multiplier=1).then_inc(consts, 1)
            for t, op, fill, sign in ((later_t, ALU.is_gt, 0.0, 1), (upto_t, ALU.is_ge, 0.0, -1),
                                      (cm_qk, ALU.is_ge, -BIG, 1), (cm_kq, ALU.is_ge, -BIG, -1)):
                pool.affine_select(out=t[:], in_=t[:], compare_op=op, fill=fill, base=0,
                                   pattern=[[-sign, P]], channel_multiplier=sign).then_inc(consts, 1)

            def keep_group(g):
                a_c_read.wait(pool, g, 2)
                pool.tensor_copy(xT[:, :, bass.ds(g * TG, TG)], cTg[:]).then_inc(a_xT.sem, 1)

            first_then_loop(pool, NG, keep_group)

            pool.wait_ge(gates, GATE_STEPS)
            a_xT.wait(pool, NG, 0)
            pool.memset(Ue[:], 0.0).then_inc(zeroed, 1)
            pool.memset(Le[:], 0.0).then_inc(zeroed, 1)

            def head(kh):
                pool.wait_ge(d_nw_in, 16)
                d_o_in.wait(pool, kh, 16)
                d_y_ready.wait(pool, kh, 0)
                pool.tensor_tensor(wo[:], wo_in[:], nw[:].rearrange("p (a b) -> p a b", a=1).broadcast_to([P, HH, D]), ALU.mult
                                   ).then_inc(d_wo.sem, 1)
                for g in range(NG):
                    d_ea_ready.wait(pool, kh, 2 * g)
                    pool.tensor_tensor(V[:], upto_t[:].rearrange("p (a i) -> p a i", a=1).broadcast_to([P, UG, P]),
                                       gdec[:, bass.ds(kh, 1), G * g:G * g + G, :].rearrange("p a b (h i) -> p (a b h) i", i=1)
                                       .broadcast_to([P, UG, P]), ALU.mult).then_inc(d_V.sem, 1)
                    d_silu.wait(pool, kh, 2 * g + 2)
                    d_ss_ready.wait(pool, kh, g)
                    pool.tensor_tensor(sqb[:], kq[:, g], kq[:, g], ALU.mult).then_inc(d_sq.sem, 1)
                d_lanes.wait(pool, kh, 3)
                lane_A = diag_u
                for j in range(BK - 1):
                    h, w = BK - 1 - j, j + 1
                    rows = lane_T[:, j + 1:BK, 0:w]
                    prod = lane_p[:, 0:h * w].rearrange("p (i k) -> p i k", k=w)
                    d_solve.wait(pool, kh, 2 * j)
                    pool.tensor_tensor(prod, lane_A[:, j + 1:BK, j:j + 1].broadcast_to([P, h, w]),
                                       lane_T[:, j:j + 1, 0:w].broadcast_to([P, h, w]), ALU.mult).then_inc(d_solve.sem, 1)
                    d_solve.wait(pool, kh, 1 + 2 * j)
                    pool.tensor_tensor(rows, rows, prod, ALU.add).then_inc(d_solve.sem, 1)

            first_then_loop(pool, NK, head)

            d_acc.wait(pool, NK, 0)

            def take_group(g):
                m_og.wait(pool, g, 0)
                pool.tensor_copy(x1g[:], acc[:, bass.ds(g * G, G), :]).then_inc(m_x1.sem, 1)

            first_then_loop(pool, NG, take_group)

        @block.tensor
        def _(pe):
            def mm(out_, lhsT, rhs, start, stop):
                return pe.matmul(out_, lhsT, rhs, start=start, stop=stop)

            pe.wait_ge(consts, CONSTS)
            pe.wait_ge(a_win, 64)
            for n in range(4):
                for e in range(2):
                    for d in range(2):
                        i = pe.transpose(ps[n][:, (2 * d + e) * P:(2 * d + e + 1) * P], w_raw[:, n, e, d * P:(d + 1) * P], ident[:])
                i.then_inc(a_wt_ready, 1)
            pe.wait_ge(a_wt_read, 4)
            pe.wait_ge(a_small_in, 80)

            def attend(g):
                a_xg_in.wait(pe, g, 16)
                for c in range(DC):
                    front.wait_free(pe, g, ("x", c))
                    for b in range(G):
                        i = pe.transpose(front.bank(("x", c))[:, b * P:(b + 1) * P], xg[:, b, c * P:(c + 1) * P], ident[:])
                    i.then_inc(a_x_ready.sem, 1)
                a_x_read.wait(pe, g, 2)
                for n, (name, ready) in enumerate((("q", a_q_ready), ("k", a_k_ready))):
                    for e in range(2):
                        front.wait_free(pe, g, (name, e))
                        for c in range(DC):
                            i = mm(front.bank((name, e))[:], w_t[:, n, c, e * P:(e + 1) * P], xgT[:, c, :], c == 0, c == DC - 1)
                        i.then_inc(ready.sem, 1)
                for m in range(2):
                    front.wait_free(pe, g, ("v", m))
                    for b in range(2):
                        for c in range(DC):
                            i = mm(front.bank(("v", m))[:, b * D:(b + 1) * D], xgT[:, c, (2 * m + b) * S:(2 * m + b + 1) * S],
                                   w_t[:, 2, c, :], c == 0, c == DC - 1)
                    i.then_inc(a_v_ready.sem, 1)
                a_q_read.wait(pe, g, 2)
                a_k_read.wait(pe, g, 4)
                a_v_read.wait(pe, g, 2)

                def scores(n):
                    b, j = n // 4, n % 4
                    score.wait_free(pe, g, n)
                    pe.matmul(score.bank(n)[:], identb[:], cm_qk[:].rearrange("p (a k) -> p a k", a=1).broadcast_to([P, 4, P]),
                              start=True, stop=False)
                    for s in range(4):
                        e, kt = s // 2, (kTe, kTo)[s % 2]
                        rows = slice(32 * j, 32 * j + 32)
                        i = mm(score.bank(n)[:, s * P:(s + 1) * P], qTa[rows, e, b * S:(b + 1) * S], kt[rows, e, b * S:(b + 1) * S],
                               False, s == 3)
                    i.then_inc(a_s_ready.sem, 1)

                def turn(n):
                    a_prob.wait(pe, g, n + 1)
                    turned.wait_free(pe, g, n)
                    for s in range(4):
                        i = pe.transpose(turned.bank(n)[:, s * P:(s + 1) * P], prob[:, n % 2, s, :], ident[:])
                    i.then_inc(a_pt_ready.sem, 1)

                def values(n):
                    b, j = n // 4, n % 4
                    a_pt_read.wait(pe, g, n + 1)
                    if j == 0:
                        front.wait_free(pe, g, ("pv", b))
                    for s in range(4):
                        h = 8 * (s // 2) + 2 * j + s % 2
                        i = mm(front.bank(("pv", b))[:, h * HD_A:(h + 1) * HD_A], probT[:, n % 2, s, :],
                               vg[:, b, h * HD_A:(h + 1) * HD_A], True, True)
                    i.then_inc(a_pv_ready.sem, 1)

                scores(0)
                scores(1)
                for n in range(4 * G + 1):
                    if n < 4 * G:
                        turn(n)
                    if n + 2 < 4 * G:
                        scores(n + 2)
                    if n >= 1:
                        values(n - 1)
                a_o_read.wait(pe, g, G)
                for e in range(2):
                    front.wait_free(pe, g, ("ot", e))
                    for b in range(G):
                        i = pe.transpose(front.bank(("ot", e))[:, b * P:(b + 1) * P], oa[:, b, e * P:(e + 1) * P], ident[:])
                    i.then_inc(a_ot_ready.sem, 1)
                a_ot_read.wait(pe, g, 2)
                for f in range(DC):
                    front.wait_free(pe, g, ("c", f))
                    for e in range(2):
                        i = mm(front.bank(("c", f))[:], w_t[:, 3, e, f * P:(f + 1) * P], oTg[:, e, :], e == 0, e == 1)
                    i.then_inc(a_c_ready.sem, 1)
                a_c_read.wait(pe, g, 2)
                for b in range(G):
                    front.wait_free(pe, g, ("ba", b))
                    for c in range(DC):
                        i = mm(front.bank(("ba", b))[:, 0:2 * NV], cTg[:, c, b * S:(b + 1) * S],
                               w_ba[:, c, :, :].rearrange("p a n -> p (a n)"), c == 0, c == DC - 1)
                    i.then_inc(a_ba_ready.sem, 1)

            first_then_loop(pe, NG, attend)

            pe.wait_ge(gates, GATE_STEPS)
            a_xT.wait(pe, NG, 0)
            pe.wait_ge(zeroed, 2)

            def head(kh):
                def project(kind, g, loaded, loads, weights, ready):
                    loaded.wait(pe, kh, loads)
                    for t in range(2):
                        proj.wait_free(pe, kh, (kind, g, t))
                        for c in range(DC):
                            i = mm(proj.bank((kind, g, t))[:], weights(c, t), xT[:, c, g * TG:(g + 1) * TG], c == 0, c == DC - 1)
                        i.then_inc(ready.sem, 1)

                def pairwise(g):
                    d_sq.wait(pe, kh, g + 1)
                    sums.wait_free(pe, kh, ("ss", g))
                    for t, col in enumerate((SK, SQ)):
                        for b in range(G):
                            i = mm(small[:, col + G * g + b:col + G * g + b + 1], sqb[:, t, b * S:(b + 1) * S], ones[:], True, True)
                    i.then_inc(d_ss_ready.sem, 1)
                    d_silu.wait(pe, kh, 2 * g + 2)
                    for h in range(2):
                        work.wait_free(pe, kh, ("gk", g, h))
                        for b in range(2):
                            t0 = (2 * h + b) * S
                            i = mm(work.bank(("gk", g, h))[:, b * 2 * P:(b + 1) * 2 * P], kq[:, g, 0, t0:t0 + S],
                                   kq[:, g, :, t0:t0 + S], True, True)
                        i.then_inc(d_gk_ready.sem, 1)
                    d_V.wait(pe, kh, g + 1)
                    for h in range(2):
                        work.wait_free(pe, kh, ("ea", g, h))
                        mm(work.bank(("ea", g, h))[:], later_t[:], V[:, 4 * h:4 * h + 4, :], True, False)
                        mm(work.bank(("ea", g, h))[:], identb[:],
                           cm_kq[:].rearrange("p (a k) -> p a k", a=1).broadcast_to([P, 4, P]), False, True).then_inc(d_ea_ready.sem, 1)

                def turn_v(g):
                    d_silu.wait(pe, kh, 8 + 2 * g + 2)
                    for h in range(2):
                        work.wait_free(pe, kh, ("vt", g, h))
                        for b in range(2):
                            for hh in range(HH):
                                i = pe.transpose(work.bank(("vt", g, h))[:, (2 * b + hh) * P:(2 * b + hh + 1) * P],
                                                 vT[:, hh, (2 * h + b) * S:(2 * h + b + 1) * S], ident[:])
                        i.then_inc(d_vt_ready.sem, 1)

                def merge_32(f):
                    for p in range(2):
                        lo, hi, both = slice(64 * p, 64 * p + BK), slice(64 * p + BK, 64 * p + 2 * BK), slice(64 * p, 64 * p + 2 * BK)
                        d_unlane.wait(pe, kh, 2)
                        work.wait_free(pe, kh, ("y1", f, p))
                        bank = work.bank(("y1", f, p))
                        for n in range(16):
                            u = 16 * f + n
                            rows = both if n == 0 else hi
                            i = mm(bank[rows, n * BK:(n + 1) * BK], Bm[lo, u, rows], diag_l[lo, u, :], True, True)
                        i.then_inc(d_y1_ready.sem, 1)
                    for p in range(2):
                        lo, hi = slice(64 * p, 64 * p + BK), slice(64 * p + BK, 64 * p + 2 * BK)
                        d_y1_read.wait(pe, kh, 2 * f + p + 1)
                        work.wait_free(pe, kh, ("t1", f, p))
                        bank = work.bank(("t1", f, p))
                        for n in range(16):
                            u = 16 * f + n
                            rows, cols = (slice(64 * p, 64 * p + 2 * BK), slice(0, 2)) if n == 0 else (lo, slice(n, n + 1))
                            mm(bank[rows, n * BK:(n + 1) * BK], Y1[hi, cols, :].rearrange("p a b -> p (a b)"), diag_u[hi, u, :], True, True)
                            i = mm(bank[hi, n * BK:(n + 1) * BK], diag_u[hi, u, :], Y1[hi, n, :], True, True)
                        i.then_inc(d_t1_ready.sem, 1)

                def merge_64(g):
                    d_spread.wait(pe, kh, 8)
                    d_t1_read.wait(pe, kh, 2 * (g // 2) + 2)
                    work.wait_free(pe, kh, ("y2", g))
                    for n in range(UG):
                        u = UG * g + n
                        i = mm(work.bank(("y2", g))[:, n * 64:(n + 1) * 64], Bm[0:64, u, :], Le[0:64, u, :], True, True)
                    i.then_inc(d_y2_ready.sem, 1)
                    d_y2_read.wait(pe, kh, g + 1)
                    work.wait_free(pe, kh, ("u2", g))
                    for n in range(UG):
                        u = UG * g + n
                        cols = slice(0, 2) if n == 0 else slice(n, n + 1)
                        i = mm(work.bank(("u2", g))[0:128 if n == 0 else 64, n * 64:(n + 1) * 64],
                               Y2[64:128, cols, :].rearrange("p a b -> p (a b)"), Ue[64:128, u, 64:128], True, True)
                    i.then_inc(d_u2_ready.sem, 1)

                def outputs(g):
                    d_u2_read.wait(pe, kh, g + 1)
                    for h in range(2):
                        d_w.wait(pe, kh, 2 * g + h + 1)
                        work.wait_free(pe, kh, ("u", g, h))
                        for n in range(4):
                            u = UG * g + 4 * h + n
                            i = mm(work.bank(("u", g, h))[:, n * P:(n + 1) * P], Ue[:, u, :], w_tok[:, u, :], True, True)
                        i.then_inc(d_u_ready.sem, 1)
                    for h in range(2):
                        d_up.wait(pe, kh, 2 * g + h + 1)
                        work.wait_free(pe, kh, ("o", g, h))
                        for n in range(4):
                            u = UG * g + 4 * h + n
                            i = mm(work.bank(("o", g, h))[:, n * P:(n + 1) * P], up[:, h, n, :], att[:, u, :], True, True)
                        i.then_inc(d_o_ready.sem, 1)
                    for h in range(2):
                        d_sqo.wait(pe, kh, 2 * g + h + 1)
                        if h == 0:
                            sums.wait_free(pe, kh, ("so", g))
                        for n in range(4):
                            u = UG * g + 4 * h + n
                            i = mm(small[:, SO + u:SO + u + 1], sqo[:, h, n, :], ones[:], True, True)
                        i.then_inc(d_so_ready.sem, 1)
                    for b in range(G):
                        d_go.wait(pe, kh, 2 * g + b // 2 + 1)
                        if g == 0 and b == 0:
                            d_wo.wait(pe, kh, 1)
                        work.wait_free(pe, kh, ("y", g, b))
                        for hh in range(HH):
                            i = mm(work.bank(("y", g, b))[:, hh * D:(hh + 1) * D], go[:, b // 2, 2 * (b % 2) + hh, :], wo[:, hh, :], True, True)
                        i.then_inc(d_y_ready.sem, 1)

                for kind, g in PE_ORDER:
                    if kind == Q:
                        project(Q, g, d_qk_in, 32, lambda c, t: wqk[:, c, t, :], d_qk_ready)
                    elif kind == Z:
                        project(Z, g, d_z_in, 16, lambda c, t: wz[:, c, t * DV:(t + 1) * DV], d_z_ready)
                    elif kind == VV:
                        project(VV, g, d_v_in, 16, lambda c, t: wv[:, c, t * DV:(t + 1) * DV], d_v_ready)
                    else:
                        {A: pairwise, VT: turn_v, M1: merge_32, M2: merge_64, UO: outputs}[kind](g)

            first_then_loop(pe, NK, head)

            d_acc.wait(pe, NK, 0)
            pe.wait_ge(m_in, M_LOADS)
            pe.wait_ge(m_q, 21)
            def mlps(g):
                m_x1.wait(pe, g, 1)
                for c in range(DC):
                    rest.wait_free(pe, g, ("x", c))
                    for b in range(G):
                        i = pe.transpose(rest.bank(("x", c))[:, b * P:(b + 1) * P], x1g[:, b, c * P:(c + 1) * P], ident[:])
                    i.then_inc(m_x1T_ready.sem, 1)
                m_x1T.wait(pe, g, 2)
                for n, a in enumerate((ag_s, au_s)):
                    rest.wait_free(pe, g, ("lg", n))
                    for c in range(DC):
                        i = mm(rest.bank(("lg", n))[:], a[:, c].rearrange("p n r -> p (n r)"), x1T[:, c, :], c == 0, c == DC - 1)
                    i.then_inc(m_lg_ready.sem, 1)
                for ct in range(I2 // P):
                    cols = slice(ct * P, (ct + 1) * P)
                    for n, (name, w, bb) in enumerate((("g", wg_s, bg_s), ("u", wu_s, bu_s))):
                        pairs.wait_free(pe, g, (name, ct))
                        for c in range(DC):
                            mm(pairs.bank((name, ct))[:], w[:, c, cols], x1T[:, c, :], c == 0, False)
                        if ct == 0:
                            m_lg.wait(pe, g, n + 1)
                        mm(pairs.bank((name, ct))[:], bb[:, cols], lg[:, n, :], False, True).then_inc(m_gu_ready.sem, 1)
                m_h.wait(pe, g, I2 // P)
                for n in range(2):
                    rest.wait_free(pe, g, ("ld", n))
                    for ct in range(I2 // P):
                        i = mm(rest.bank(("ld", n))[:, 0:256], ad_s[:, ct].rearrange("p n r -> p (n r)"),
                               hT[:, ct, n * 256:(n + 1) * 256], ct == 0, ct == I2 // P - 1)
                    i.then_inc(m_ld_ready.sem, 1)
                for e in range(DC):
                    rest.wait_free(pe, g, ("y", e))
                    for ct in range(I2 // P):
                        mm(rest.bank(("y", e))[:], wd_s[:, ct, e * P:(e + 1) * P], hT[:, ct, :], ct == 0, False)
                    m_ld.wait(pe, g, 2)
                    mm(rest.bank(("y", e))[:], bd_s[:, e * P:(e + 1) * P], lg[:, 2, :], False, True).then_inc(m_y_ready.sem, 1)
                m_y.wait(pe, g, 2)
                for ft in range(I3 // P):
                    for name, w in (("fg", qg_s), ("fu", qu_s)):
                        pairs.wait_free(pe, g, (name, ft))
                        for c in range(DC):
                            i = mm(pairs.bank((name, ft))[:], w[:, c * I3 + ft * P:c * I3 + (ft + 1) * P], yT[:, c, :], c == 0, c == DC - 1)
                        i.then_inc(m_fgu_ready.sem, 1)
                m_f.wait(pe, g, I3 // P)
                for b in range(G):
                    rest.wait_free(pe, g, ("d", b))
                    for ft in range(I3 // P):
                        i = mm(rest.bank(("d", b))[:, 0:D], fT[:, ft, b * S:(b + 1) * S], qd_s[:, ft * D:(ft + 1) * D], ft == 0, ft == I3 // P - 1)
                    i.then_inc(m_d_ready.sem, 1)

            first_then_loop(pe, NG, mlps)

        @block.scalar
        def _(act):
            def f(out_, in_, fn, **kw):
                return act.activation(out_, in_, fn, **kw)

            for n in range(4):
                act.wait_ge(a_wt_ready, n + 1)
                f(w_t[:, n].rearrange("p a b -> p (a b)"), ps[n][:], ACT.Copy).then_inc(a_wt_read, 1)

            def attend(g):
                a_x_ready.wait(act, g, 2)
                f(xgT[:, 1, :], front.bank(("x", 1))[:], ACT.Copy).then_inc(a_x_read.sem, 1)
                for m in range(2):
                    a_v_ready.wait(act, g, m + 1)
                    a_pv_ready.wait(act, g, 0)
                    f(vg[:, 2 * m:2 * m + 2, :].rearrange("p b d -> p (b d)"), front.bank(("v", m))[:], ACT.Copy).then_inc(a_v_read.sem, 1)
                for n in range(4 * G):
                    b, j = n // 4, n % 4
                    a_nmax.wait(act, g, n + 1)
                    a_pt_ready.wait(act, g, n - 1)
                    if j == 0:
                        a_rinv.wait(act, g, b - 1)
                    for s in range(4):
                        h = 8 * (s // 2) + 2 * j + s % 2
                        i = f(prob[:, n % 2, s, :], score.bank(n)[:, s * P:(s + 1) * P], ACT.Exp, bias=nmax[:, n % 2, s:s + 1],
                              accum_out=rsum[:, b % 2, h:h + 1])
                    i.then_inc(a_prob.sem, 1)
                for e in range(2):
                    a_ot_ready.wait(act, g, e + 1)
                    a_c_ready.wait(act, g, 0)
                    f(oTg[:, e, :], front.bank(("ot", e))[:], ACT.Copy).then_inc(a_ot_read.sem, 1)
                for e in range(2):
                    a_c_ready.wait(act, g, e + 1)
                    a_xT.wait(act, g, 0)
                    a_ba_ready.wait(act, g, 0)
                    f(cTg[:, e, :], front.bank(("c", e))[:], ACT.Copy).then_inc(a_c_read.sem, 1)

            first_then_loop(act, NG, attend)

            a_ba_read.wait(act, NG, 0)
            f(sp[0][:], ba[:, 0:NV, :], ACT.Tanh, scale=0.5).then_inc(gates_act, 1)
            f(nega[:], alog[:], ACT.Exp).then_inc(gates_act, 1)
            act.wait_ge(gates, 2)
            f(sp[3][:], sp[2][:], ACT.Exp, scale=-1.0).then_inc(gates_act, 1)
            act.wait_ge(gates_act, 3)
            f(sp[2][:], sp[3][:], ACT.Ln, bias=1.0).then_inc(gates_act, 1)

            act.wait_ge(gates, GATE_STEPS)

            def head(kh):
                def tap(kind, g):
                    for t in range(2):
                        n = conv_n[kind, g, t]
                        (d_qk_ready if kind == Q else d_v_ready).wait(act, kh, 2 * g + t + 1)
                        d_cw_in.wait(act, kh, 48)
                        d_silu.wait(act, kh, n - 2)
                        f(cbuf[:, n % 3, :], proj.bank((kind, g, t))[:], ACT.Copy,
                          scale=cw[:, conv_row(kind, t), KC - 1:KC]).then_inc(d_tap.sem, 1)

                def silu(kind, g):
                    for t in range(2):
                        n = conv_n[kind, g, t]
                        d_conv.wait(act, kh, n + 1)
                        if kind == Q:
                            d_gk_ready.wait(act, kh, 2 * g + 2 - 8)
                            d_sq.wait(act, kh, g + 1 - NG)
                            dst = kq[:, g, t, :]
                        else:
                            d_vt_ready.wait(act, kh, 2 * g)
                            dst = vT[:, t, :]
                        f(dst, cbuf[:, n % 3, :], ACT.Silu).then_inc(d_silu.sem, 1)

                def z_silu(g):
                    for t in range(2):
                        d_z_ready.wait(act, kh, 2 * g + t + 1)
                        d_go.wait(act, kh, 2 * g + 2 - 8)
                        f(zg[:, t, g * TG:(g + 1) * TG], proj.bank((Z, g, t))[:], ACT.Silu).then_inc(d_zg.sem, 1)

                def decays(g):
                    for h in range(2):
                        d_ea_ready.wait(act, kh, 2 * g + h + 1)
                        d_B.wait(act, kh, 2 * g + h - 1)
                        f(E[:, h].rearrange("p u i -> p (u i)"), work.bank(("ea", g, h))[:], ACT.Exp).then_inc(d_E.sem, 1)

                def keep_v(g):
                    d_knorm.wait(act, kh, 1)
                    d_u_ready.wait(act, kh, 2 * g + 2 - 8)
                    for h in range(2):
                        d_vt_ready.wait(act, kh, 2 * g + h + 1)
                        for b in range(2):
                            u = UG * g + 4 * h + 2 * b
                            s = G * g + 2 * h + b
                            i = f(w_tok[:, u:u + 2, :].rearrange("p u c -> p (u c)"), work.bank(("vt", g, h))[:, b * 2 * P:(b + 1) * 2 * P],
                                  ACT.Copy, scale=knorm[:, s:s + 1])
                        i.then_inc(d_w.sem, 1)

                def spread():
                    d_unlane.wait(act, kh, 2)
                    d_u_ready.wait(act, kh, 0)
                    for r in range(4):
                        rows = slice(BK * r, BK * r + BK)
                        f(Ue[rows, :, rows], diag_u[rows], ACT.Copy).then_inc(d_spread.sem, 1)
                        f(Le[rows, :, BK * (r % 2):BK * (r % 2) + BK], diag_l[rows], ACT.Copy).then_inc(d_spread.sem, 1)

                def read_y1(fh):
                    for p in range(2):
                        hi = slice(64 * p + BK, 64 * p + 2 * BK)
                        d_y1_ready.wait(act, kh, 2 * fh + p + 1)
                        d_t1_ready.wait(act, kh, 2 * fh + p - 1)
                        f(Y1[hi].rearrange("p u c -> p (u c)"), work.bank(("y1", fh, p))[hi, :], ACT.Copy).then_inc(d_y1_read.sem, 1)

                def read_y2(g):
                    d_y2_ready.wait(act, kh, g + 1)
                    d_u2_ready.wait(act, kh, g)
                    f(Y2[64:128].rearrange("p u c -> p (u c)"), work.bank(("y2", g))[64:128, :], ACT.Copy).then_inc(d_y2_read.sem, 1)

                def outputs(g):
                    for h in range(2):
                        d_u_ready.wait(act, kh, 2 * g + h + 1)
                        d_o_ready.wait(act, kh, 2 * g + h - 1)
                        for n in range(4):
                            b = G * g + 2 * h + n // 2
                            i = f(up[:, h, n, :], work.bank(("u", g, h))[:, n * P:(n + 1) * P], ACT.Copy, scale=cpos[:, b, n % 2:n % 2 + 1])
                        i.then_inc(d_up.sem, 1)
                    for h in range(2):
                        d_o_ready.wait(act, kh, 2 * g + h + 1)
                        d_so_ready.wait(act, kh, 2 * g + h - 1)
                        f(sqo[:, h].rearrange("p u c -> p (u c)"), work.bank(("o", g, h))[:], ACT.Square).then_inc(d_sqo.sem, 1)

                tap(Q, 0); z_silu(0); silu(Q, 0)
                tap(Q, 1); z_silu(1); silu(Q, 1)
                decays(0)
                tap(Q, 2); z_silu(2); silu(Q, 2)
                decays(1)
                tap(Q, 3); z_silu(3); silu(Q, 3)
                tap(VV, 0); decays(2); silu(VV, 0)
                decays(3)
                for g in range(1, NG):
                    tap(VV, g)
                    keep_v(g - 1)
                    silu(VV, g)
                keep_v(NG - 1)
                read_y1(0)
                read_y1(1)
                spread()
                read_y2(0)
                read_y2(1)
                outputs(0)
                read_y2(2)
                outputs(1)
                read_y2(3)
                outputs(2)
                outputs(3)

            first_then_loop(act, NK, head)

            d_acc.wait(act, NK, 0)
            act.wait_ge(m_in, M_LOADS)

            def mlps(g):
                m_x1T_ready.wait(act, g, 2)
                f(x1T[:, 1, :], rest.bank(("x", 1))[:], ACT.Copy).then_inc(m_x1T.sem, 1)
                for ct in range(I2 // P):
                    m_gu_ready.wait(act, g, 2 * ct + 1)
                    m_h.wait(act, g, ct - 1)
                    f(sg[:, ct % 2, :], pairs.bank(("g", ct))[:], ACT.Silu).then_inc(m_sg.sem, 1)
                for e in range(DC):
                    m_y_ready.wait(act, g, e + 1)
                    m_fgu_ready.wait(act, g, 0)
                    f(yT[:, e, :], rest.bank(("y", e))[:], ACT.Copy).then_inc(m_y.sem, 1)
                for ft in range(I3 // P):
                    m_fgu_ready.wait(act, g, 2 * ft + 1)
                    m_h.wait(act, g, I2 // P)
                    m_f.wait(act, g, ft - 1)
                    f(sg[:, ft % 2, :], pairs.bank(("fg", ft))[:], ACT.Silu, scale=gsc[:, ft:ft + 1]).then_inc(m_fs.sem, 1)

            first_then_loop(act, NG, mlps)

        @block.vector
        def _(dve):
            dve.wait_ge(consts, 14)
            dve.tensor_scalar(part[:, 1:2], part[:, 0:1], 16, None, ALU.bitwise_and).then_inc(consts, 1)
            dve.tensor_scalar(part[:, 2:3], part[:, 0:1], 4, None, ALU.logical_shift_right).then_inc(picked, 1)
            dve.wait_ge(consts, 15)
            dve.tensor_scalar(head_even[:], part[:, 1:2], 0, None, ALU.is_equal).then_inc(consts, 1)
            dve.tensor_scalar(head_odd[:], part[:, 1:2], 0, None, ALU.is_gt).then_inc(consts, 1)
            dve.wait_ge(picked, 1)
            dve.tensor_copy(own[:], part[:, 2:3]).then_inc(picked, 1)
            dve.wait_ge(a_small_in, 80)
            dve.tensor_scalar(precs[:], precb[:], 4.0, HD_A ** -0.5, ALU.min, ALU.mult).then_inc(a_prec, 1)
            dve.wait_ge(consts, CONSTS)
            dve.wait_ge(a_prec, 1)

            def attend(g):
                a_x_ready.wait(dve, g, 1)
                dve.tensor_copy(xgT[:, 0, :], front.bank(("x", 0))[:]).then_inc(a_x_read.sem, 1)
                for e in range(2):
                    a_q_ready.wait(dve, g, e + 1)
                    a_s_ready.wait(dve, g, 0)
                    dve.tensor_tensor(qTa[:, e, :].rearrange("p (b t) -> p b t", b=G), front.bank(("q", e))[:].rearrange("p (b t) -> p b t", b=G),
                                      precs[:, bass.ds(g * G, G)].rearrange("p (b t) -> p b t", t=1).broadcast_to([P, G, S]),
                                      ALU.mult).then_inc(a_q_read.sem, 1)
                for e in range(2):
                    a_k_ready.wait(dve, g, e + 1)
                    for kt, mask in ((kTe, head_even), (kTo, head_odd)):
                        dve.tensor_scalar(kt[:, e, :], front.bank(("k", e))[:], mask[:, 0:1], None, ALU.mult).then_inc(a_k_read.sem, 1)

                def maxima(n):
                    a_s_ready.wait(dve, g, n + 1)
                    dve.tensor_reduce(rmax[:, n % 2, :], score.bank(n)[:].rearrange("p (s k) -> p s k", s=4), AX_X, ALU.max).then_inc(a_max.sem, 1)
                    a_max.wait(dve, g, n + 1)
                    a_prob.wait(dve, g, n - 1)
                    dve.tensor_scalar(nmax[:, n % 2, :], rmax[:, n % 2, :], -1.0, None, ALU.mult).then_inc(a_nmax.sem, 1)

                maxima(0)
                maxima(1)
                for n in range(4 * G):
                    b = n // 4
                    a_pt_ready.wait(dve, g, n + 1)
                    a_pv_ready.wait(dve, g, n - 1)
                    dve.tensor_copy(probT[:, n % 2].rearrange("p s q -> p (s q)"), turned.bank(n)[:]).then_inc(a_pt_read.sem, 1)
                    if n + 2 < 4 * G:
                        maxima(n + 2)
                    if n % 4 == 3:
                        dve.reciprocal(rinv[:, b % 2, :], rsum[:, b % 2, :]).then_inc(a_rinv.sem, 1)
                        a_rinv.wait(dve, g, b + 1)
                        a_pv_ready.wait(dve, g, n + 1)
                        a_ot_ready.wait(dve, g, 0)
                        dve.tensor_tensor(oa[:, b, :].rearrange("p (h d) -> p h d", h=NH_A),
                                          front.bank(("pv", b))[:, 0:D].rearrange("p (h d) -> p h d", h=NH_A),
                                          rinv[:, b % 2, :].rearrange("p (h d) -> p h d", d=1).broadcast_to([P, NH_A, HD_A]),
                                          ALU.mult).then_inc(a_o_read.sem, 1)
                for b in range(G):
                    a_ba_ready.wait(dve, g, b + 1)
                    dve.tensor_copy(ba[:, :, bass.ds(g * G + b, 1)], front.bank(("ba", b))[:, 0:2 * NV].rearrange("p (c a) -> p c a", a=1)
                                    ).then_inc(a_ba_read.sem, 1)

            first_then_loop(dve, NG, attend)

            by_batch = lambda t: t.rearrange("p (n a) -> p n a", a=1).broadcast_to([P, NV, B])
            a_ba_read.wait(dve, NG, 0)
            dve.tensor_tensor(sp[1][:], ba[:, NV:2 * NV, :], by_batch(dtb[:]), ALU.add).then_inc(gates, 1)
            dve.wait_ge(gates, 1)
            flat = [t[:].rearrange("p n b -> p (n b)") for t in sp]
            dve.scalar_tensor_tensor(out=flat[2], in0=flat[1], scalar=-1.0, in1=flat[1], op0=ALU.mult, op1=ALU.max).then_inc(gates, 1)
            dve.wait_ge(gates_act, 2)
            for hh in range(HH):
                dve.tensor_scalar(beta[:, :, :, hh], sp[0][:].rearrange("p (k h) b -> p h k b", h=HH)[:, hh], 0.5, 0.5,
                                  ALU.mult, ALU.add).then_inc(gates, 1)
            dve.tensor_scalar(alog[:], nega[:], -1.0, None, ALU.mult).then_inc(gates, 1)
            dve.wait_ge(gates_act, 4)
            dve.scalar_tensor_tensor(out=flat[3], in0=flat[1], scalar=0.0, in1=flat[2], op0=ALU.max, op1=ALU.add).then_inc(gates, 1)
            dve.wait_ge(gates, 6)
            dve.tensor_tensor(sp[0][:], sp[3][:], by_batch(alog[:]), ALU.mult).then_inc(gates, 1)
            dve.wait_ge(gates, 7)
            for hh in range(HH):
                dve.tensor_copy(gdec[:, :, :, hh], sp[0][:].rearrange("p (k h) b -> p h k b", h=HH)[:, hh]).then_inc(gates, 1)
            dve.wait_ge(gates, GATE_STEPS)
            dve.wait_ge(x_in, 64)

            def rsqrt(kh, y, v, t, steps, first):
                n = first
                dve.tensor_scalar(t.bitcast(I32), v.bitcast(I32), 1, None, ALU.logical_shift_right).then_inc(steps.sem, 1)
                steps.wait(dve, kh, n + 1)
                dve.tensor_scalar(y.bitcast(I32), t.bitcast(I32), -1.0, RSQRT_SEED, ALU.mult, ALU.add).then_inc(steps.sem, 1)
                n += 2
                for k in range(3):
                    steps.wait(dve, kh, n)
                    dve.tensor_tensor(t, y, y, ALU.mult).then_inc(steps.sem, 1)
                    steps.wait(dve, kh, n + 1)
                    dve.scalar_tensor_tensor(out=t, in0=t, scalar=-0.5, in1=v, op0=ALU.mult, op1=ALU.mult).then_inc(steps.sem, 1)
                    steps.wait(dve, kh, n + 2)
                    i = dve.scalar_tensor_tensor(out=y, in0=t, scalar=1.5, in1=y, op0=ALU.add, op1=ALU.mult)
                    n += 3
                    i.then_inc(steps.sem, 1)
                return n

            def head(kh):
                def conv(kind, g):
                    for t in range(2):
                        n = conv_n[kind, g, t]
                        d_tap.wait(dve, kh, n + 1)
                        taps = proj.bank((kind, g, t))[:].rearrange("p (b t) -> p b t", b=G)
                        whole = cbuf[:, n % 3, :].rearrange("p (b t) -> p b t", b=G)
                        d_cw_in.wait(dve, kh, 48)
                        for d in range(1, KC):
                            if d > 1:
                                d_conv_step.wait(dve, kh, 2 * n + d - 1)
                            i = dve.scalar_tensor_tensor(out=whole[:, :, d:S], in0=taps[:, :, 0:S - d], scalar=cw[:, conv_row(kind, t), KC - 1 - d:KC - d],
                                                         in1=whole[:, :, d:S], op0=ALU.mult, op1=ALU.add)
                            i.then_inc(d_conv.sem if d == KC - 1 else d_conv_step.sem, 1)

                def factors(g):
                    bs = slice(G * g, G * g + G)
                    d_ss_ready.wait(dve, kh, g + 1)
                    d_up.wait(dve, kh, 2 * g + 2 - 8)
                    d_osc.wait(dve, kh, g + 1 - NG)
                    dve.tensor_scalar(ksum[:, bs], small[:, SK + G * g:SK + G * g + G], EPS, None, ALU.add).then_inc(d_rec.sem, 1)
                    dve.tensor_scalar(qeps[:, bs], small[:, SQ + G * g:SQ + G * g + G], EPS * DK, EPS * EPS * DK, ALU.mult, ALU.add
                                      ).then_inc(d_ss_read.sem, 1)
                    d_rec.wait(dve, kh, g + 1)
                    dve.reciprocal(krec[:, bs], ksum[:, bs]).then_inc(d_c1.sem, 1)
                    d_c1.wait(dve, kh, g + 1)
                    dve.tensor_tensor(cpos[:, bs, :], beta[:, bass.ds(kh, 1), bs, :].rearrange("p a b h -> p (a b) h"),
                                      krec[:, bs].rearrange("p (b h) -> p b h", h=1).broadcast_to([P, G, HH]), ALU.mult).then_inc(d_c.sem, 1)
                    d_c.wait(dve, kh, g + 1)
                    dve.tensor_scalar(cneg[:, bs, :], cpos[:, bs, :], -1.0, None, ALU.mult).then_inc(d_cneg.sem, 1)

                def masks(g):
                    d_cneg.wait(dve, kh, g + 1)
                    d_u_ready.wait(dve, kh, 0)
                    d_o_ready.wait(dve, kh, 2 * g + 2 - 8)
                    for h in range(2):
                        d_E.wait(dve, kh, 2 * g + h + 1)
                        d_gk_ready.wait(dve, kh, 2 * g + h + 1)
                        gk = work.bank(("gk", g, h))[:].rearrange("p (b t i) -> p b t i", b=2, t=2)
                        for n in range(4):
                            u = UG * g + 4 * h + n
                            b = G * g + 2 * h + n // 2
                            dve.scalar_tensor_tensor(out=Bm[:, u, :], in0=gk[:, n // 2, 0, :], scalar=cneg[:, b, n % 2:n % 2 + 1],
                                                     in1=E[:, h, n, :], op0=ALU.mult, op1=ALU.mult)
                        u = UG * g + 4 * h
                        dve.tensor_tensor(att[:, u:u + 4, :].rearrange("p (b h) i -> p b h i", b=2),
                                          gk[:, :, 1:2, :].broadcast_to([P, 2, HH, P]),
                                          E[:, h].rearrange("p (b h) i -> p b h i", b=2), ALU.mult).then_inc(d_B.sem, 1)

                def diagonal(g):
                    d_B.wait(dve, kh, 2 * g + 2)
                    us = slice(UG * g, UG * g + UG)
                    for r in range(4):
                        rows = slice(BK * r, BK * r + BK)
                        i = dve.tensor_copy(diag_l[rows, us, :], Bm[rows, us, rows])
                    i.then_inc(d_diag.sem, 1)

                def to_lanes():
                    dve.memset(lane_T[:], 0.0).then_inc(d_lanes.sem, 1)
                    d_lanes.wait(dve, kh, 1)
                    dve.memset(lane_T[:].rearrange("p a b -> p (a b)")[:, 0:BK * BK:BK + 1], 1.0).then_inc(d_lanes.sem, 1)
                    d_diag.wait(dve, kh, NG)
                    dve.transpose(diag_u[:], diag_l[:].rearrange("p u a -> p a u")).then_inc(d_lanes.sem, 1)

                def from_lanes():
                    d_solve.wait(dve, kh, d_solve.per)
                    dve.transpose(diag_l[:].rearrange("p u k -> p k u"), lane_T[:].rearrange("p i k -> p k i")).then_inc(d_unlane.sem, 1)
                    dve.transpose(diag_u[:].rearrange("p u i -> p i u"), lane_T[:]).then_inc(d_unlane.sem, 1)

                def key_norms():
                    d_rec.wait(dve, kh, NG)
                    d_w.wait(dve, kh, 0)
                    rsqrt(kh, nt[:, 0, 0:B], ksum[:], nt[:, 1, 0:B], d_newt, 0)
                    d_newt.wait(dve, kh, 11)
                    dve.tensor_tensor(knorm[:], nt[:, 0, 0:B], ksum[:], ALU.mult).then_inc(d_knorm.sem, 1)

                def read_t1(fh):
                    us = slice(16 * fh, 16 * fh + 16)
                    for p in range(2):
                        lo, hi = slice(64 * p, 64 * p + BK), slice(64 * p + BK, 64 * p + 2 * BK)
                        d_t1_ready.wait(dve, kh, 2 * fh + p + 1)
                        d_u_ready.wait(dve, kh, 0)
                        bank = work.bank(("t1", fh, p))[:].rearrange("p (u c) -> p u c", c=BK)
                        dve.tensor_copy(Le[hi, us, 0:BK], bank[hi])
                        dve.tensor_copy(Ue[lo, us, hi], bank[lo]).then_inc(d_t1_read.sem, 1)

                def read_u2(g):
                    d_u2_ready.wait(dve, kh, g + 1)
                    dve.tensor_copy(Ue[0:64, UG * g:UG * g + UG, 64:128],
                                    work.bank(("u2", g))[0:64, :].rearrange("p (u c) -> p u c", c=64)).then_inc(d_u2_read.sem, 1)

                def gate(g):
                    for h in range(2):
                        d_sqo.wait(dve, kh, 2 * g + h + 1)
                        d_zg.wait(dve, kh, 2 * g + 2)
                        d_y_ready.wait(dve, kh, G * g + 2 * h + 2 - G)
                        t0 = g * TG + h * 2 * S
                        dve.tensor_tensor(go[:, h].rearrange("p (b h) t -> p b h t", b=2), work.bank(("o", g, h))[:].rearrange("p (b h t) -> p b h t", b=2, h=HH),
                                          zg[:, :, t0:t0 + 2 * S].rearrange("p h (b t) -> p b h t", b=2), ALU.mult).then_inc(d_go.sem, 1)

                def out_norms(g):
                    bs = slice(G * g, G * g + G)
                    v = nt[:, 2, 0:UG]
                    d_so_ready.wait(dve, kh, 2 * g + 2)
                    dve.scalar_tensor_tensor(out=v.rearrange("p (b h) -> p b h", h=HH),
                                             in0=small[:, SO + UG * g:SO + UG * g + UG].rearrange("p (b h) -> p b h", h=HH), scalar=1.0 / DV,
                                             in1=qeps[:, bs].rearrange("p (b h) -> p b h", h=1).broadcast_to([P, G, HH]),
                                             op0=ALU.mult, op1=ALU.add).then_inc(d_so_read.sem, 1)
                    d_so_read.wait(dve, kh, g + 1)
                    n = rsqrt(kh, nt[:, 0, 0:UG], v, nt[:, 1, 0:UG], d_nto, 11 * g)
                    d_nto.wait(dve, kh, n)
                    dve.tensor_copy(osc[:, bs, :].rearrange("p b h -> p (b h)"), nt[:, 0, 0:UG]).then_inc(d_osc.sem, 1)
                    d_osc.wait(dve, kh, g + 1)

                def accumulate(g):
                    for b in range(G):
                        s = G * g + b
                        d_y_ready.wait(dve, kh, s + 1)
                        for hh in range(HH):
                            if hh:
                                d_acc_step.wait(dve, kh, s + 1)
                            i = dve.scalar_tensor_tensor(out=acc[:, s, :], in0=work.bank(("y", g, b))[:, hh * D:(hh + 1) * D], scalar=osc[:, s, hh:hh + 1],
                                                         in1=acc[:, s, :], op0=ALU.mult, op1=ALU.add)
                            i.then_inc(d_acc.sem if hh else d_acc_step.sem, 1)

                conv(Q, 0)
                conv(Q, 1)
                factors(0); masks(0); diagonal(0)
                conv(Q, 2)
                factors(1); masks(1); diagonal(1)
                conv(Q, 3)
                factors(2)
                conv(VV, 0)
                masks(2); diagonal(2)
                factors(3); masks(3); diagonal(3)
                to_lanes()
                key_norms()
                for g in range(1, NG):
                    conv(VV, g)
                from_lanes()
                read_t1(0)
                read_t1(1)
                read_u2(0)
                read_u2(1)
                gate(0); out_norms(0)
                accumulate(0)
                read_u2(2)
                gate(1); out_norms(1)
                accumulate(1)
                read_u2(3)
                gate(2); out_norms(2)
                accumulate(2)
                gate(3); out_norms(3)
                accumulate(3)

            first_then_loop(dve, NK, head)

            d_acc.wait(dve, NK, 0)
            dve.wait_ge(m_in, M_LOADS)
            n = 0
            for w in (qg_s, qu_s, qd_s):
                dve.tensor_scalar(q8a[:], w[:], 240.0, -240.0, ALU.min, ALU.max, saturate=False).then_inc(m_q, 1)
                dve.tensor_scalar(qdif[:], w[:], 0.5, 240.0, ALU.mult, ALU.min).then_inc(m_q, 1)
                dve.scalar_tensor_tensor(out=qm[:], in0=w[:], scalar=-1.0, in1=w[:], op0=ALU.mult, op1=ALU.max).then_inc(m_q, 1)
                dve.wait_ge(m_q, n + 3)
                dve.tensor_scalar(q8b[:], qdif[:], -240.0, None, ALU.max, saturate=False).then_inc(m_q, 1)
                dve.wait_ge(m_q, n + 4)
                dve.scalar_tensor_tensor(out=qdif[:], in0=q8b[:], scalar=2.0, in1=q8a[:], op0=ALU.mult, op1=ALU.subtract).then_inc(m_q, 1)
                dve.wait_ge(m_q, n + 5)
                dve.scalar_tensor_tensor(out=qdif[:], in0=qm[:], scalar=240.0, in1=qdif[:], op0=ALU.is_gt, op1=ALU.mult).then_inc(m_q, 1)
                dve.wait_ge(m_q, n + 6)
                dve.tensor_tensor(w[:], qdif[:], q8a[:], ALU.add).then_inc(m_q, 1)
                dve.wait_ge(m_q, n + 7)
                n += 7
            dve.wait_ge(picked, 2)
            dve.tensor_copy(idx_f[:], idx_i[:]).then_inc(m_pick, 1)
            dve.wait_ge(m_pick, 1)
            dve.tensor_scalar(pick[:], idx_f[:], own[:, 0:1], None, ALU.is_equal).then_inc(m_pick, 1)
            dve.wait_ge(m_pick, 2)

            def mlps(g):
                m_x1T_ready.wait(dve, g, 1)
                dve.tensor_copy(x1T[:, 0, :], rest.bank(("x", 0))[:]).then_inc(m_x1T.sem, 1)

                def keep_own(dst, src, b0, nb, done):
                    dve.tensor_tensor(dst.rearrange("p (b t) -> p b t", b=nb), src.rearrange("p (b t) -> p b t", b=nb),
                                      pick[:, bass.ds(g * G + b0, nb)].rearrange("p (b t) -> p b t", t=1).broadcast_to([P, nb, S]),
                                      ALU.mult).then_inc(done.sem, 1)

                for n in range(2):
                    m_lg_ready.wait(dve, g, n + 1)
                    m_gu_ready.wait(dve, g, 0)
                    keep_own(lg[:, n, :], rest.bank(("lg", n))[:], 0, G, m_lg)
                for ct in range(I2 // P):
                    m_gu_ready.wait(dve, g, 2 * ct + 2)
                    m_sg.wait(dve, g, ct + 1)
                    m_y_ready.wait(dve, g, 0)
                    dve.tensor_tensor(hT[:, ct, :], sg[:, ct % 2, :], pairs.bank(("u", ct))[:], ALU.mult).then_inc(m_h.sem, 1)
                for n in range(2):
                    m_ld_ready.wait(dve, g, n + 1)
                    m_y_ready.wait(dve, g, 0)
                    keep_own(lg[:, 2, n * 256:(n + 1) * 256], rest.bank(("ld", n))[:, 0:256], 2 * n, 2, m_ld)
                for ft in range(I3 // P):
                    m_fgu_ready.wait(dve, g, 2 * ft + 2)
                    m_fs.wait(dve, g, ft + 1)
                    m_d_ready.wait(dve, g, 0)
                    dve.scalar_tensor_tensor(out=fT[:, ft, :], in0=pairs.bank(("fu", ft))[:], scalar=usc[:, ft:ft + 1], in1=sg[:, ft % 2, :],
                                             op0=ALU.mult, op1=ALU.mult).then_inc(m_f.sem, 1)
                for b in range(G):
                    m_d_ready.wait(dve, g, b + 1)
                    dve.tensor_tensor(dn[:, b % 2, :], rest.bank(("d", b))[:, 0:D], dsc[:], ALU.mult).then_inc(m_dn.sem, 1)
                    m_dn.wait(dve, g, b + 1)
                    m_out.wait(dve, g, 0)
                    dve.tensor_tensor(og[:, b, :], dn[:, b % 2, :], x1g[:, b, :], ALU.add).then_inc(m_og.sem, 1)

            first_then_loop(dve, NG, mlps)


_INS = ['x', 'cond_1', 'itok_B_0_7', 'L0_cond_Wq', 'L0_cond_Wk', 'L0_cond_Wv', 'L0_cond_Wo', 'L0_attn_W_qkv', 'L0_attn_W_z',
        'L0_attn_W_b', 'L0_attn_W_a', 'L0_attn_conv_w', 'L0_attn_dt_bias', 'L0_attn_A_log', 'L0_attn_norm_w', 'L0_attn_W_out',
        'L0_cond2_Wg', 'L0_cond2_Wu', 'L0_cond2_Wd', 'L0_cond2_Ag', 'L0_cond2_Bg', 'L0_cond2_Au', 'L0_cond2_Bu', 'L0_cond2_Ad',
        'L0_cond2_Bd', 'L0_ffn_gate_w', 'L0_ffn_up_w', 'L0_ffn_down_w', 'L0_ffn_gate_scale', 'L0_ffn_up_scale', 'L0_ffn_down_scale']


def kernel(**inputs):
    import numpy as np
    import concourse.bacc as bacc
    from concourse.bass_utils import run_bass_kernel_spmd

    nc = bacc.Bacc("TRN2", target_bir_lowering=False, num_devices=1)
    arrays, args = {}, []
    for name in _INS:
        a = np.ascontiguousarray(inputs[name])
        arrays[f"in_{name}"] = a
        args.append(nc.dram_tensor(f"in_{name}", a.shape, mybir.dt.from_np(a.dtype), kind="ExternalInput").ap())
    out = nc.dram_tensor("out", (B, S, D), F32, kind="ExternalOutput").ap()
    build(nc, *args, out)
    r = run_bass_kernel_spmd(nc, [arrays], core_ids=[0])
    return r.results[0]["out"]
```

```python
from contextlib import ExitStack

import concourse.bass as bass
from concourse import mybir

F32 = mybir.dt.float32
BF16 = mybir.dt.bfloat16
FP8 = mybir.dt.float8e4
I32 = mybir.dt.int32
ALU = mybir.AluOpType
ACT = mybir.ActivationFunctionType
AX_X = mybir.AxisListType.X

P = 128
B, S, D = 16, 128, 256
DC = D // P
G = 4
NG = B // G
TG = G * S
NH_A, HD_A = 16, 16
NK, NV, DK, DV, KC = 16, 32, 128, 128, 4
HH = NV // NK
UN = B * HH
UG = G * HH
BK = 32
EPS = 1e-6
BIG = 1e30
RSQRT_SEED = 1597463007.0
N_AD, RK, I2, I3 = 8, 16, 1024, 768


class Signal:

    def __init__(self, sem, per):
        self.sem, self.per, self.passed = sem, per, {}

    def wait(self, eng, step, n):
        seen, most = self.passed.get(id(eng), (None, 0))
        if seen is step and most >= n:
            return
        self.passed[id(eng)] = (step, n)
        value = step * self.per + n
        if isinstance(value, int) and value <= 0:
            return
        eng.wait_ge(self.sem, value)


def first_then_loop(eng, steps, body):
    body(0)
    with eng.Fori(1, steps) as step:
        body(step)


def loop_then_last(eng, steps, body):
    body(0, False)
    with eng.Fori(1, steps - 1) as step:
        body(step, False)
    body(steps - 1, True)


class Banks:

    def __init__(self, banks, uses):
        assert len(uses) % len(banks) == 0
        self.banks, self.uses = banks, uses
        self.index = {key: n for n, (key, _, _) in enumerate(uses)}

    def bank(self, key):
        return self.banks[self.index[key] % len(self.banks)]

    def wait_free(self, eng, step, key, left_out=None):
        n = self.index[key] - len(self.banks)
        while left_out and n >= 0 and self.uses[n][0][0] == left_out:
            n -= len(self.banks)
        _, reader, count = self.uses[n]
        reader.wait(eng, step, count if n >= 0 else count - reader.per)


def build(nc, x, prec, adapter, Wq, Wk, Wv, Wo, W_qkv, W_z, W_b, W_a, conv_w, dt_bias, A_log, norm_w,
          W_out, Wg, Wu, Wd, Ag, Bg, Au, Bu, Ad, Bd, gate_w, up_w, down_w, gate_s, up_s, down_s, out):
    top = ExitStack()

    def sem(name):
        return top.enter_context(nc.semaphore(name))

    def sig(name, per):
        return Signal(sem(name), per)

    def tile(stack, name, shape, dt=F32):
        return stack.enter_context(nc.sbuf_tensor(name, shape, dt))

    with top:
        ps = [top.enter_context(nc.psum_tensor(f"bank{i}", [P, 512], F32)) for i in range(8)]

        acc = tile(top, "acc", [P, B, D])
        ident = tile(top, "ident", [P, P])
        identb = tile(top, "identb", [P, P], BF16)
        later_t = tile(top, "later_t", [P, P])
        upto_t = tile(top, "upto_t", [P, P])
        ones = tile(top, "ones", [P, 1])
        cm_qk = tile(top, "cm_qk", [P, P], BF16)
        cm_kq = tile(top, "cm_kq", [P, P], BF16)
        head_even = tile(top, "head_even", [P, 1])
        head_odd = tile(top, "head_odd", [P, 1])
        part = tile(top, "part", [P, 3], I32)
        own = tile(top, "own", [P, 1])

        consts = sem("consts")
        x_in = sem("x_in")

        fr = ExitStack()
        beta = tile(top, "beta", [P, NK, B, HH])
        gdec = tile(top, "gdec", [P, NK, B, HH])
        xT = tile(top, "xT", [P, DC, B * S])
        w_raw = tile(fr, "w_raw", [P, 4, 2, D])
        w_t = tile(fr, "w_t", [P, 4, 2, D])
        w_ba = tile(fr, "w_ba", [P, DC, 2, NV])
        xg = tile(fr, "xg", [P, G, D])
        xgT = tile(fr, "xgT", [P, DC, TG])
        precb = tile(fr, "precb", [P, B])
        precs = tile(fr, "precs", [P, B])
        qTa = tile(fr, "qTa", [P, 2, TG])
        kTe = tile(fr, "kTe", [P, 2, TG])
        kTo = tile(fr, "kTo", [P, 2, TG])
        vg = tile(fr, "vg", [P, G, D])
        rmax = tile(fr, "rmax", [P, 2, 4])
        nmax = tile(fr, "nmax", [P, 2, 4])
        rsum = tile(fr, "rsum", [P, 2, NH_A])
        rinv = tile(fr, "rinv", [P, 2, NH_A])
        prob = tile(fr, "prob", [P, 2, 4, P])
        probT = tile(fr, "probT", [P, 2, 4, P])
        oa = tile(fr, "oa", [P, G, D])
        oTg = tile(fr, "oTg", [P, 2, TG])
        cTg = tile(fr, "cTg", [P, DC, TG])
        ba = tile(fr, "ba", [P, 2 * NV, B])
        dtb = tile(fr, "dtb", [P, NV])
        alog = tile(fr, "alog", [P, NV])
        nega = tile(fr, "nega", [P, NV])
        sp = [tile(fr, f"sp{i}", [P, NV, B]) for i in range(4)]

        fr.close()
        gd = ExitStack()
        wqk = tile(gd, "wqk", [P, DC, 2, P])
        wv = tile(gd, "wv", [P, DC, HH * DV])
        wz = tile(gd, "wz", [P, DC, HH * DV])
        wo_in = tile(gd, "wo_in", [P, HH, D])
        wo = tile(gd, "wo", [P, HH, D])
        cwq = tile(gd, "cwq", [P, 2, KC])
        cwv = tile(gd, "cwv", [P, HH, KC])
        nw = tile(gd, "nw", [P, 1])
        cbuf = tile(gd, "cbuf", [P, 4, TG])
        kq = tile(gd, "kq", [P, NG, 2, TG])
        V = tile(gd, "V", [P, UG, P])
        E = tile(gd, "E", [P, 2, 4, P])
        Bm = tile(gd, "Bm", [P, UN, P])
        att = tile(gd, "att", [P, UN, P])
        w_tok = tile(gd, "w_tok", [P, UN, P])
        zg = tile(gd, "zg", [P, HH, B * S])
        Ue = tile(gd, "Ue", [P, UN, P])
        Le = tile(gd, "Le", [P, UN, 2 * BK])
        diag_l = tile(gd, "diag_l", [P, UN, BK])
        diag_u = tile(gd, "diag_u", [P, UN, BK])
        lane_T = tile(gd, "lane_T", [P, BK, BK])
        lane_p = tile(gd, "lane_p", [P, (BK // 2) ** 2])
        vT = tile(gd, "vT", [P, HH, TG])
        Y1 = lane_T
        Y2 = tile(gd, "Y2", [P, 2, UG, 2 * BK])
        up = tile(gd, "up", [P, 2, 4, P])
        sqo = tile(gd, "sqo", [P, 2, 4, P])
        go = tile(gd, "go", [P, 2, 4, P])
        sqb = [t[:].rearrange("p h n i -> p h (n i)") for t in (sqo, go)]
        ssum = tile(gd, "ssum", [P, 2 * B])
        ksum = tile(gd, "ksum", [P, B])
        krec = tile(gd, "krec", [P, B])
        qeps = tile(gd, "qeps", [P, B])
        cpos = tile(gd, "cpos", [P, B, HH])
        cneg = tile(gd, "cneg", [P, B, HH])
        knorm = tile(gd, "knorm", [P, B])
        nt = tile(gd, "nt", [P, 3, UN])
        osc = tile(gd, "osc", [P, B, HH])
        gd.close()

        bk = ExitStack()
        wg_s = tile(bk, "wg_s", [P, DC, I2])
        wu_s = tile(bk, "wu_s", [P, DC, I2])
        wd_s = tile(bk, "wd_s", [P, I2 // P, D])
        ag_s = tile(bk, "ag_s", [P, DC, N_AD, RK])
        au_s = tile(bk, "au_s", [P, DC, N_AD, RK])
        ad_s = tile(bk, "ad_s", [P, I2 // P, N_AD, RK])
        bg_s = tile(bk, "bg_s", [P, I2])
        bu_s = tile(bk, "bu_s", [P, I2])
        bd_s = tile(bk, "bd_s", [P, D])
        qg_s = tile(bk, "qg_s", [P, DC * I3])
        qu_s = tile(bk, "qu_s", [P, DC * I3])
        qd_s = tile(bk, "qd_s", [P, I3 // P * D])
        q8a = tile(bk, "q8a", [P, DC * I3], FP8)
        q8b = tile(bk, "q8b", [P, DC * I3], FP8)
        qm = tile(bk, "qm", [P, DC * I3])
        qdif = tile(bk, "qdif", [P, DC * I3])
        gsc = tile(bk, "gsc", [P, I3 // P])
        usc = tile(bk, "usc", [P, I3 // P])
        dsc = tile(bk, "dsc", [P, D])
        idx_i = tile(bk, "idx_i", [P, B], I32)
        idx_f = tile(bk, "idx_f", [P, B])
        pick = tile(bk, "pick", [P, B])
        x1g = tile(bk, "x1g", [P, G, D])
        x1T = tile(bk, "x1T", [P, DC, TG])
        lg = tile(bk, "lg", [P, 3, TG])
        sg = tile(bk, "sg", [P, 2, TG])
        hT = tile(bk, "hT", [P, I2 // P, TG])
        yT = tile(bk, "yT", [P, DC, TG])
        fT = tile(bk, "fT", [P, I3 // P, TG])
        og = tile(bk, "og", [P, G, D])
        dn = tile(bk, "dn", [P, 2, D])
        bk.close()

        dram_w = {0: Wq, 1: Wk, 2: Wv, 3: Wo}

        a_win = sem("a_win")
        a_small_in = sem("a_small_in")
        a_xg_in = Signal(sem("a_xg_in"), 16)
        a_wt_ready = sem("a_wt_ready")
        a_wt_read = sem("a_wt_read")
        a_prec = sem("a_prec")
        a_x_ready, a_x_read = sig("a_x_ready", 2), sig("a_x_read", 2)
        a_q_ready, a_q_read = sig("a_q_ready", 2), sig("a_q_read", 2)
        a_k_ready, a_k_read = sig("a_k_ready", 2), sig("a_k_read", 4)
        a_v_ready, a_v_read = sig("a_v_ready", 2), sig("a_v_read", 2)
        a_s_ready, a_max, a_nmax = sig("a_s_ready", 16), sig("a_max", 16), sig("a_nmax", 16)
        a_prob = sig("a_prob", 16)
        a_pt_ready, a_pt_read = sig("a_pt_ready", 16), sig("a_pt_read", 16)
        a_pv_ready = sig("a_pv_ready", 16)
        a_rinv, a_o_read = sig("a_rinv", G), sig("a_o_read", G)
        a_ot_ready, a_ot_read = sig("a_ot_ready", 2), sig("a_ot_read", 2)
        a_c_ready, a_c_read = sig("a_c_ready", 2), sig("a_c_read", 2)
        a_xT = sig("a_xT", 1)
        a_ba_ready, a_ba_read = sig("a_ba_ready", G), sig("a_ba_read", G)
        gates, gates_act, picked = sem("gates"), sem("gates_act"), sem("picked")

        d_nw_in = sem("d_nw_in")
        d_cwq_in, d_cwv_in = Signal(sem("d_cwq_in"), 32), Signal(sem("d_cwv_in"), 16)
        d_qk_in = Signal(sem("d_qk_in"), 32)
        d_v_in, d_z_in, d_o_in = (Signal(sem(n), 16) for n in ("d_v_in", "d_z_in", "d_o_in"))
        d_wo = sig("d_wo", 1)
        d_qk_ready, d_v_ready, d_z_ready = sig("d_qk_ready", 8), sig("d_v_ready", 8), sig("d_z_ready", 8)
        d_tap_q, d_conv_q, d_step_q, d_silu_q = sig("d_tap_q", 8), sig("d_conv_q", 8), sig("d_step_q", 16), sig("d_silu_q", 8)
        d_tap_v, d_conv_v, d_step_v, d_silu_v = sig("d_tap_v", 8), sig("d_conv_v", 8), sig("d_step_v", 16), sig("d_silu_v", 8)
        d_zg = sig("d_zg", 8)
        d_sq, d_ss_ready, d_ss_read = sig("d_sq", NG), sig("d_ss_ready", NG), sig("d_ss_read", 1)
        d_rec, d_c1, d_c, d_cneg = (sig(n, 1) for n in ("d_rec", "d_c1", "d_c", "d_cneg"))
        d_V = sig("d_V", 8)
        d_gk_ready, d_ea_ready, d_E, d_B = (sig(n, 8) for n in ("d_gk_ready", "d_ea_ready", "d_E", "d_B"))
        d_diag = sig("d_diag", NG)
        d_lanes, d_solve, d_unlane = sig("d_lanes", 3), sig("d_solve", 2 * (BK - 1)), sig("d_unlane", 2)
        d_newt, d_knorm = sig("d_newt", 11), sig("d_knorm", 1)
        d_spread_l, d_spread_u = sig("d_spread_l", 4), sig("d_spread_u", 4)
        d_y1_ready, d_y1_read, d_t1_ready, d_t1_read = (sig(n, 4) for n in
                                                        ("d_y1_ready", "d_y1_read", "d_t1_ready", "d_t1_read"))
        d_y2_ready, d_y2_read, d_u2_ready, d_u2_read = (sig(n, NG) for n in
                                                        ("d_y2_ready", "d_y2_read", "d_u2_ready", "d_u2_read"))
        d_vt_ready, d_w = sig("d_vt_ready", 8), sig("d_w", 8)
        d_u_ready, d_up, d_o_ready, d_sqo, d_go = (sig(n, 8) for n in ("d_u_ready", "d_up", "d_o_ready", "d_sqo", "d_go"))
        d_so_ready, d_so_read, d_nto, d_osc = sig("d_so_ready", 8), sig("d_so_read", NG), sig("d_nto", 11 * NG), sig("d_osc", NG)
        d_y_ready, d_acc_step, d_acc = sig("d_y_ready", B), sig("d_acc_step", B), sig("d_acc", B)
        zeroed = sem("zeroed")

        m_in = sem("m_in")
        m_q = sem("m_q")
        m_idx, m_pick = sem("m_idx"), sem("m_pick")
        m_x1, m_x1T_ready, m_x1T = sig("m_x1", 1), sig("m_x1T_ready", 2), sig("m_x1T", 2)
        m_lg_ready, m_lg = sig("m_lg_ready", 2), sig("m_lg", 2)
        m_gu_ready, m_sg, m_h = sig("m_gu_ready", 16), sig("m_sg", 8), sig("m_h", 8)
        m_ld_ready, m_ld = sig("m_ld_ready", 2), sig("m_ld", 2)
        m_y_ready, m_y = sig("m_y_ready", 2), sig("m_y", 2)
        m_fgu_ready, m_fs, m_f = sig("m_fgu_ready", 12), sig("m_fs", 6), sig("m_f", 6)
        m_d_ready, m_dn, m_og = sig("m_d_ready", 4), sig("m_dn", 4), sig("m_og", 4)
        m_out = Signal(sem("m_out"), 16)

        PE_ORDER = [("ea", 0), ("gk", 0), ("ea", 1), ("gk", 1), ("ea", 2), ("gk", 2), ("ea", 3), ("gk", 3),
                    ("v", 0), ("z", 0), ("next", 0), ("v", 1), ("z", 1), ("vt", 0), ("next", 1), ("ss", 0),
                    ("v", 2), ("z", 2), ("vt", 1), ("next", 2), ("ss", 1), ("v", 3), ("z", 3), ("y1", 0), ("y1", 1),
                    ("vt", 2), ("next", 3), ("ss", 2), ("t1", 0), ("t1", 1), ("vt", 3), ("ss", 3),
                    ("y2", 0), ("y2", 1), ("u2", 0), ("y2", 2), ("u2", 1),
                    ("u", 0), ("y2", 3), ("u2", 2), ("o", 0), ("u", 1), ("u2", 3), ("so", 0), ("o", 1), ("y", 0), ("u", 2),
                    ("so", 1), ("o", 2), ("y", 1), ("u", 3), ("so", 2), ("o", 3), ("y", 2), ("so", 3), ("y", 3)]
        CONV = [(kind, g, t) for kind, g in PE_ORDER if kind in ("v", "next") for t in range(2)]
        conv_slot = {c: n % 4 for n, c in enumerate(CONV)}

        proj_uses, work_uses, small_uses = [], [], []
        for kind, g in PE_ORDER:
            if kind == "next":
                proj_uses += [((kind, g, t), d_conv_q, 8 + 2 * g + t + 1) for t in range(2)]
            elif kind == "v":
                proj_uses += [((kind, g, t), d_conv_v, 2 * g + t + 1) for t in range(2)]
            elif kind == "z":
                proj_uses += [((kind, g, t), d_zg, 2 * g + t + 1) for t in range(2)]
            elif kind == "ss" and g == 0:
                small_uses += [(("ss", 0), d_ss_read, 2)]
            elif kind == "gk":
                work_uses += [(("gk", g, h), d_B, 2 * g + h + 1) for h in range(2)]
            elif kind == "ea":
                proj_uses += [(("ea", g, h), d_E, 2 * g + h + 1) for h in range(2)]
            elif kind == "vt":
                work_uses += [((kind, g, h), d_w, 2 * g + h + 1) for h in range(2)]
            elif kind in ("y1", "t1"):
                work_uses += [((kind, g, p), d_y1_read if kind == "y1" else d_t1_read, 2 * g + p + 1) for p in range(2)]
            elif kind in ("y2", "u2"):
                work_uses += [((kind, g), d_y2_read if kind == "y2" else d_u2_read, g + 1)]
            elif kind in ("u", "o"):
                work_uses += [((kind, g, h), d_up if kind == "u" else d_go, 2 * g + h + 1) for h in range(2)]
            elif kind == "so":
                small_uses += [(("so", g), d_so_read, g + 1)]
            elif kind == "y":
                proj_uses += [((kind, g, b), d_acc, G * g + b + 1) for b in range(G)]
        proj_uses += [(("pad", n), d_acc, B) for n in range(-len(proj_uses) % 3)]
        ahead = Banks(ps[0:3], [((g, t), d_conv_q, 2 * g + t + 1) for g in range(NG) for t in range(2)] + [(None, d_conv_q, 8)])
        proj = Banks(ps[0:3], proj_uses)
        work = Banks(ps[3:7], work_uses)
        sums, small = Banks(ps[7:8], small_uses), ps[7]
        front = Banks(ps[0:4], [(("x", n), a_x_read, 2) for n in range(2)] + [(("q", n), a_q_read, n + 1) for n in range(2)]
                      + [(("k", n), a_k_read, 2 * n + 2) for n in range(2)] + [(("v", n), a_v_read, n + 1) for n in range(2)]
                      + [(("pv", b), a_o_read, b + 1) for b in range(G)] + [(("ot", n), a_ot_read, n + 1) for n in range(2)]
                      + [(("c", n), a_c_read, n + 1) for n in range(2)] + [(("ba", b), a_ba_read, b + 1) for b in range(G)])
        score = Banks(ps[4:6], [(n, a_prob, n + 1) for n in range(4 * G)])
        turned = Banks(ps[6:8], [(n, a_pt_read, n + 1) for n in range(4 * G)])
        pairs = []
        for c in range(I2 // P):
            pairs += [(("g", c), m_sg, c + 1), (("u", c), m_h, c + 1)]
        for c in range(I3 // P):
            pairs += [(("fg", c), m_fs, c + 1), (("fu", c), m_f, c + 1)]
        pairs = Banks(ps[0:4], pairs)
        rest = Banks(ps[4:8], [(("x", n), m_x1T, n + 1) for n in range(2)] + [(("lg", n), m_lg, n + 1) for n in range(2)]
                     + [(("ld", n), m_ld, n + 1) for n in range(2)] + [(("y", n), m_y, n + 1) for n in range(2)]
                     + [(("d", b), m_dn, b + 1) for b in range(G)])
        SK, SQ, SO = 0, B, 2 * B

        block = top.enter_context(nc.Block())
        CONSTS = 17
        GATE_STEPS = 9
        M_LOADS = 16 * (11 + 2 * DC + I2 // P + 2)

        @block.sync
        def _(sp_):
            for n in range(4):
                sp_.dma_start(w_raw[:, n, :, :], dram_w[n].rearrange("(c p) d -> p c d", p=P)).then_inc(a_win, 16)

            def load_xg(g):
                a_x_ready.wait(sp_, g, 0)
                sp_.dma_start(xg[:], x[bass.ds(g * G, G), :, :].rearrange("b t d -> t b d")).then_inc(a_xg_in.sem, 16)

            for t, v in ((dtb, dt_bias), (alog, A_log)):
                sp_.dma_start(t[:], v.rearrange("(a n) -> a n", a=1).broadcast_to([P, NV])).then_inc(a_small_in, 16)
            sp_.dma_start(precb[:], prec.rearrange("b a -> a b").broadcast_to([P, B])).then_inc(a_small_in, 16)
            for n, v in enumerate((W_b, W_a)):
                sp_.dma_start(w_ba[:, :, n, :], v.rearrange("(c p) n -> p c n", p=P)).then_inc(a_small_in, 16)
            first_then_loop(sp_, NG, load_xg)
            for g in range(NG):
                sp_.dma_start(acc[:, G * g:G * g + G, :], x[G * g:G * g + G, :, :].rearrange("b t d -> t b d")).then_inc(x_in, 16)

            sp_.wait_ge(gates, GATE_STEPS)
            taps = conv_w.rearrange("(n p) j -> p n j", p=P)
            sp_.dma_start(nw[:], norm_w.rearrange("(p a) -> p a", a=1)).then_inc(d_nw_in, 16)
            qkv = W_qkv.rearrange("(c p) n -> p c n", p=P)
            zz = W_z.rearrange("(c p) n -> p c n", p=P)

            def load_qk(head, step):
                of_k, of_q = qkv[:, :, bass.ds(head * DK + NK * DK, DK)], qkv[:, :, bass.ds(head * DK, DK)]
                d_qk_ready.wait(sp_, step, 8)
                sp_.dma_start(wqk[:, :, 0, :], of_k).then_inc(d_qk_in.sem, 16)
                sp_.dma_start(wqk[:, :, 1, :], of_q).then_inc(d_qk_in.sem, 16)
                d_conv_q.wait(sp_, step, 8)
                for t, first in ((0, head + NK), (1, head + 0)):
                    sp_.dma_start(cwq[:, t:t + 1, :], taps[:, bass.ds(first, 1), :]).then_inc(d_cwq_in.sem, 16)

            load_qk(0, -1)

            def load_head(kh, last):
                d_v_ready.wait(sp_, kh, 0)
                d_z_ready.wait(sp_, kh, 0)
                sp_.dma_start(wv[:], qkv[:, :, bass.ds(kh * HH * DV + 2 * NK * DK, HH * DV)]).then_inc(d_v_in.sem, 16)
                sp_.dma_start(wz[:], zz[:, :, bass.ds(kh * HH * DV, HH * DV)]).then_inc(d_z_in.sem, 16)
                d_conv_v.wait(sp_, kh, 0)
                sp_.dma_start(cwv[:], taps[:, bass.ds(kh * HH + 2 * NK, HH), :]).then_inc(d_cwv_in.sem, 16)
                if not last:
                    load_qk(kh + 1, kh)
                d_wo.wait(sp_, kh, 0)
                sp_.dma_start(wo_in[:], W_out.rearrange("(h p) f -> p h f", p=P)[:, bass.ds(kh * HH, HH), :]).then_inc(d_o_in.sem, 16)

            loop_then_last(sp_, NK, load_head)

            d_acc.wait(sp_, NK, 0)
            for dst, src in (
                (wg_s[:], Wg.rearrange("(c p) n -> p c n", p=P)), (wu_s[:], Wu.rearrange("(c p) n -> p c n", p=P)),
                (bg_s[:], Bg.rearrange("n r i -> (n r) i")), (bu_s[:], Bu.rearrange("n r i -> (n r) i")),
                (wd_s[:], Wd.rearrange("(c p) n -> p c n", p=P)), (bd_s[:], Bd.rearrange("n r i -> (n r) i")),
                (qg_s[:].rearrange("p (c n) -> p c n", c=DC), gate_w.rearrange("(c p) n -> p c n", p=P)),
                (qu_s[:].rearrange("p (c n) -> p c n", c=DC), up_w.rearrange("(c p) n -> p c n", p=P)),
                (qd_s[:].rearrange("p (c n) -> p c n", c=I3 // P), down_w.rearrange("(c p) n -> p c n", p=P)),
                (dsc[:], down_s.rearrange("(a n) -> a n", a=1).broadcast_to([P, D])),
                (idx_i[:], adapter.rearrange("(a n) -> a n", a=1).broadcast_to([P, B])),
            ):
                sp_.dma_start(dst, src).then_inc(m_in, 16)
            for c in range(DC):
                sp_.dma_start(ag_s[:, c], Ag[:, c * P:(c + 1) * P, :].rearrange("n p r -> p n r")).then_inc(m_in, 16)
                sp_.dma_start(au_s[:, c], Au[:, c * P:(c + 1) * P, :].rearrange("n p r -> p n r")).then_inc(m_in, 16)
            for c in range(I2 // P):
                sp_.dma_start(ad_s[:, c], Ad[:, c * P:(c + 1) * P, :].rearrange("n p r -> p n r")).then_inc(m_in, 16)
            with nc.allow_non_contiguous_dma("scales by channel, once"):
                sp_.dma_start(gsc[:], gate_s.rearrange("(c p) -> p c", p=P)).then_inc(m_in, 16)
                sp_.dma_start(usc[:], up_s.rearrange("(c p) -> p c", p=P)).then_inc(m_in, 16)

            def store(g):
                m_og.wait(sp_, g, 4)
                sp_.dma_start(out[bass.ds(g * G, G), :, :].rearrange("b t d -> t b d"), og[:]).then_inc(m_out.sem, 16)

            first_then_loop(sp_, NG, store)
            m_out.wait(sp_, NG, 0)



        @block.gpsimd
        def _(pool):
            for t, v in ((ident, 0.0), (later_t, 1.0), (upto_t, 1.0), (cm_qk, 0.0), (cm_kq, 0.0), (identb, 0.0),
                         (ones, 1.0)):
                pool.memset(t[:], v).then_inc(consts, 1)
            pool.iota(part[:, 0:1], pattern=[[0, 1]], base=0, channel_multiplier=1).then_inc(consts, 1)
            pool.wait_ge(consts, 8)
            for t in (ident, identb):
                pool.affine_select(out=t[:], in_=t[:], compare_op=ALU.not_equal, fill=1.0, base=0,
                                   pattern=[[-1, P]], channel_multiplier=1).then_inc(consts, 1)
            for t, op, fill, sign in ((later_t, ALU.is_gt, 0.0, 1), (upto_t, ALU.is_ge, 0.0, -1),
                                      (cm_qk, ALU.is_ge, -BIG, 1), (cm_kq, ALU.is_ge, -BIG, -1)):
                pool.affine_select(out=t[:], in_=t[:], compare_op=op, fill=fill, base=0,
                                   pattern=[[-sign, P]], channel_multiplier=sign).then_inc(consts, 1)

            def keep_group(g):
                a_c_read.wait(pool, g, 2)
                pool.tensor_copy(xT[:, :, bass.ds(g * TG, TG)], cTg[:]).then_inc(a_xT.sem, 1)

            first_then_loop(pool, NG, keep_group)

            pool.wait_ge(gates, GATE_STEPS)
            a_xT.wait(pool, NG, 0)
            pool.memset(Ue[:], 0.0).then_inc(zeroed, 1)
            pool.memset(Le[:], 0.0).then_inc(zeroed, 1)

            def decay_terms(step, n, ahead):
                g, h = n // 2, n % 2
                d_ea_ready.wait(pool, step, n + ahead * 8 - 1)
                pool.tensor_tensor(V[:, 4 * h:4 * h + 4, :], upto_t[:].rearrange("p (a i) -> p a i", a=1).broadcast_to([P, 4, P]),
                                   gdec[:, bass.ds(step + ahead, 1), G * g + 2 * h:G * g + 2 * h + 2, :].rearrange("p a b (h i) -> p (a b h) i", i=1)
                                   .broadcast_to([P, 4, P]), ALU.mult).then_inc(d_V.sem, 1)

            decay_terms(0, 0, 0)
            decay_terms(0, 1, 0)

            def head(kh, last):
                for n in range(2, 8):
                    decay_terms(kh, n, 0)
                d_o_in.wait(pool, kh, 16)
                d_y_ready.wait(pool, kh, 0)
                pool.tensor_tensor(wo[:], wo_in[:], nw[:].rearrange("p (a b) -> p a b", a=1).broadcast_to([P, HH, D]), ALU.mult
                                   ).then_inc(d_wo.sem, 1)
                d_lanes.wait(pool, kh, 3)
                lane_A = diag_u
                for j in range(BK - 1):
                    h, w = BK - 1 - j, j + 1
                    rows = lane_T[:, j + 1:BK, 0:w]
                    prod = lane_p[:, 0:h * w].rearrange("p (i k) -> p i k", k=w)
                    d_solve.wait(pool, kh, 2 * j)
                    pool.tensor_tensor(prod, lane_A[:, j + 1:BK, j:j + 1].broadcast_to([P, h, w]),
                                       lane_T[:, j:j + 1, 0:w].broadcast_to([P, h, w]), ALU.mult).then_inc(d_solve.sem, 1)
                    d_solve.wait(pool, kh, 1 + 2 * j)
                    pool.tensor_tensor(rows, rows, prod, ALU.add).then_inc(d_solve.sem, 1)
                if not last:
                    decay_terms(kh, 0, 1)
                    decay_terms(kh, 1, 1)

            pool.wait_ge(d_nw_in, 16)
            loop_then_last(pool, NK, head)

            d_acc.wait(pool, NK, 0)

            def take_group(g):
                m_og.wait(pool, g, 0)
                pool.tensor_copy(x1g[:], acc[:, bass.ds(g * G, G), :]).then_inc(m_x1.sem, 1)

            first_then_loop(pool, NG, take_group)

        @block.tensor
        def _(pe):
            def mm(out_, lhsT, rhs, start, stop):
                return pe.matmul(out_, lhsT, rhs, start=start, stop=stop)

            pe.wait_ge(consts, CONSTS)
            pe.wait_ge(a_win, 64)
            for n in range(4):
                for e in range(2):
                    for d in range(2):
                        i = pe.transpose(ps[n][:, (2 * d + e) * P:(2 * d + e + 1) * P], w_raw[:, n, e, d * P:(d + 1) * P], ident[:])
                i.then_inc(a_wt_ready, 1)
            pe.wait_ge(a_wt_read, 4)
            pe.wait_ge(a_small_in, 80)

            def attend(g):
                a_xg_in.wait(pe, g, 16)
                for c in range(DC):
                    front.wait_free(pe, g, ("x", c))
                    for b in range(G):
                        i = pe.transpose(front.bank(("x", c))[:, b * P:(b + 1) * P], xg[:, b, c * P:(c + 1) * P], ident[:])
                    i.then_inc(a_x_ready.sem, 1)
                a_x_read.wait(pe, g, 2)
                for n, (name, ready) in enumerate((("q", a_q_ready), ("k", a_k_ready))):
                    for e in range(2):
                        front.wait_free(pe, g, (name, e))
                        for c in range(DC):
                            i = mm(front.bank((name, e))[:], w_t[:, n, c, e * P:(e + 1) * P], xgT[:, c, :], c == 0, c == DC - 1)
                        i.then_inc(ready.sem, 1)
                for m in range(2):
                    front.wait_free(pe, g, ("v", m))
                    for b in range(2):
                        for c in range(DC):
                            i = mm(front.bank(("v", m))[:, b * D:(b + 1) * D], xgT[:, c, (2 * m + b) * S:(2 * m + b + 1) * S],
                                   w_t[:, 2, c, :], c == 0, c == DC - 1)
                    i.then_inc(a_v_ready.sem, 1)
                a_q_read.wait(pe, g, 2)
                a_k_read.wait(pe, g, 4)
                a_v_read.wait(pe, g, 2)

                def scores(n):
                    b, j = n // 4, n % 4
                    score.wait_free(pe, g, n)
                    pe.matmul(score.bank(n)[:], identb[:], cm_qk[:].rearrange("p (a k) -> p a k", a=1).broadcast_to([P, 4, P]),
                              start=True, stop=False)
                    for s in range(4):
                        e, kt = s // 2, (kTe, kTo)[s % 2]
                        rows = slice(32 * j, 32 * j + 32)
                        i = mm(score.bank(n)[:, s * P:(s + 1) * P], qTa[rows, e, b * S:(b + 1) * S], kt[rows, e, b * S:(b + 1) * S],
                               False, s == 3)
                    i.then_inc(a_s_ready.sem, 1)

                def turn(n):
                    a_prob.wait(pe, g, n + 1)
                    turned.wait_free(pe, g, n)
                    for s in range(4):
                        i = pe.transpose(turned.bank(n)[:, s * P:(s + 1) * P], prob[:, n % 2, s, :], ident[:])
                    i.then_inc(a_pt_ready.sem, 1)

                def values(n):
                    b, j = n // 4, n % 4
                    a_pt_read.wait(pe, g, n + 1)
                    if j == 0:
                        front.wait_free(pe, g, ("pv", b))
                    for s in range(4):
                        h = 8 * (s // 2) + 2 * j + s % 2
                        i = mm(front.bank(("pv", b))[:, h * HD_A:(h + 1) * HD_A], probT[:, n % 2, s, :],
                               vg[:, b, h * HD_A:(h + 1) * HD_A], True, True)
                    i.then_inc(a_pv_ready.sem, 1)

                scores(0)
                scores(1)
                for n in range(4 * G + 1):
                    if n < 4 * G:
                        turn(n)
                    if n + 2 < 4 * G:
                        scores(n + 2)
                    if n >= 1:
                        values(n - 1)
                a_o_read.wait(pe, g, G)
                for e in range(2):
                    front.wait_free(pe, g, ("ot", e))
                    for b in range(G):
                        i = pe.transpose(front.bank(("ot", e))[:, b * P:(b + 1) * P], oa[:, b, e * P:(e + 1) * P], ident[:])
                    i.then_inc(a_ot_ready.sem, 1)
                a_ot_read.wait(pe, g, 2)
                for f in range(DC):
                    front.wait_free(pe, g, ("c", f))
                    for e in range(2):
                        i = mm(front.bank(("c", f))[:], w_t[:, 3, e, f * P:(f + 1) * P], oTg[:, e, :], e == 0, e == 1)
                    i.then_inc(a_c_ready.sem, 1)
                a_c_read.wait(pe, g, 2)
                for b in range(G):
                    front.wait_free(pe, g, ("ba", b))
                    for c in range(DC):
                        i = mm(front.bank(("ba", b))[:, 0:2 * NV], cTg[:, c, b * S:(b + 1) * S],
                               w_ba[:, c, :, :].rearrange("p a n -> p (a n)"), c == 0, c == DC - 1)
                    i.then_inc(a_ba_ready.sem, 1)

            first_then_loop(pe, NG, attend)

            pe.wait_ge(gates, GATE_STEPS)
            a_xT.wait(pe, NG, 0)
            pe.wait_ge(zeroed, 2)

            def project_qk(step, g, banks, key):
                d_qk_in.wait(pe, step, 64)
                for t in range(2):
                    banks.wait_free(pe, 0 if banks is ahead else step, key(t))
                    for c in range(DC):
                        i = mm(banks.bank(key(t))[:], wqk[:, c, t, :], xT[:, c, g * TG:(g + 1) * TG], c == 0, c == DC - 1)
                    i.then_inc(d_qk_ready.sem, 1)

            def sums_of_squares(step, g):
                d_sq.wait(pe, step, NG + g + 1)
                for t, col in enumerate((SK, SQ)):
                    for b in range(G):
                        i = mm(small[:, col + G * g + b:col + G * g + b + 1], sqb[g % 2][:, t, b * S:(b + 1) * S], ones[:], True, True)
                i.then_inc(d_ss_ready.sem, 1)

            for g in range(NG):
                project_qk(-1, g, ahead, lambda t: (g, t))
            for g in range(NG):
                sums_of_squares(-1, g)
            d_conv_q.wait(pe, 0, 8)

            def head(kh, last):
                def project(kind, g, loaded, weights, ready):
                    loaded.wait(pe, kh, 16)
                    for t in range(2):
                        proj.wait_free(pe, kh, (kind, g, t), "next" if last else None)
                        for c in range(DC):
                            i = mm(proj.bank((kind, g, t))[:], weights[:, c, t * DV:(t + 1) * DV], xT[:, c, g * TG:(g + 1) * TG], c == 0, c == DC - 1)
                        i.then_inc(ready.sem, 1)

                def products(g):
                    d_silu_q.wait(pe, kh, 2 * g + 2)
                    for h in range(2):
                        work.wait_free(pe, kh, ("gk", g, h))
                        for b in range(2):
                            t0 = (2 * h + b) * S
                            i = mm(work.bank(("gk", g, h))[:, b * 2 * P:(b + 1) * 2 * P], kq[:, g, 0, t0:t0 + S],
                                   kq[:, g, :, t0:t0 + S], True, True)
                        i.then_inc(d_gk_ready.sem, 1)

                def log_decays(g):
                    for h in range(2):
                        d_V.wait(pe, kh, 2 * g + h + 1)
                        proj.wait_free(pe, kh, ("ea", g, h))
                        mm(proj.bank(("ea", g, h))[:], later_t[:], V[:, 4 * h:4 * h + 4, :], True, False)
                        mm(proj.bank(("ea", g, h))[:], identb[:],
                           cm_kq[:].rearrange("p (a k) -> p a k", a=1).broadcast_to([P, 4, P]), False, True).then_inc(d_ea_ready.sem, 1)

                def sums_of_next(g):
                    if g == 0:
                        sums.wait_free(pe, kh, ("ss", 0))
                    sums_of_squares(kh, g)

                def turn_v(g):
                    d_silu_v.wait(pe, kh, 2 * g + 2)
                    for h in range(2):
                        work.wait_free(pe, kh, ("vt", g, h))
                        for b in range(2):
                            for hh in range(HH):
                                i = pe.transpose(work.bank(("vt", g, h))[:, (2 * b + hh) * P:(2 * b + hh + 1) * P],
                                                 vT[:, hh, (2 * h + b) * S:(2 * h + b + 1) * S], ident[:])
                        i.then_inc(d_vt_ready.sem, 1)

                def first_of_32(f):
                    for p in range(2):
                        lo, hi, both = slice(64 * p, 64 * p + BK), slice(64 * p + BK, 64 * p + 2 * BK), slice(64 * p, 64 * p + 2 * BK)
                        d_unlane.wait(pe, kh, 2)
                        work.wait_free(pe, kh, ("y1", f, p))
                        bank = work.bank(("y1", f, p))
                        for n in range(16):
                            u = 16 * f + n
                            rows = both if n == 0 else hi
                            i = mm(bank[rows, n * BK:(n + 1) * BK], Bm[lo, u, rows], diag_l[lo, u, :], True, True)
                        i.then_inc(d_y1_ready.sem, 1)

                def second_of_32(f):
                    for p in range(2):
                        lo, hi = slice(64 * p, 64 * p + BK), slice(64 * p + BK, 64 * p + 2 * BK)
                        d_y1_read.wait(pe, kh, 2 * f + p + 1)
                        work.wait_free(pe, kh, ("t1", f, p))
                        bank = work.bank(("t1", f, p))
                        for n in range(16):
                            u = 16 * f + n
                            rows, units = (slice(64 * p, 64 * p + 2 * BK), slice(u, u + 2)) if n == 0 else (lo, slice(u, u + 1))
                            mm(bank[rows, n * BK:(n + 1) * BK], Y1[hi, units, :].rearrange("p a b -> p (a b)"), diag_u[hi, u, :], True, True)
                            i = mm(bank[hi, n * BK:(n + 1) * BK], diag_u[hi, u, :], Y1[hi, u, :], True, True)
                        i.then_inc(d_t1_ready.sem, 1)

                def first_of_64(g):
                    d_spread_l.wait(pe, kh, 4)
                    d_t1_read.wait(pe, kh, 2 * (g // 2) + 2)
                    work.wait_free(pe, kh, ("y2", g))
                    for n in range(UG):
                        u = UG * g + n
                        rows = slice(0 if n == 0 else 64, 128)
                        i = mm(work.bank(("y2", g))[rows, n * 64:(n + 1) * 64], Bm[0:64, u, rows], Le[0:64, u, :], True, True)
                    i.then_inc(d_y2_ready.sem, 1)

                def second_of_64(g):
                    d_spread_u.wait(pe, kh, 4)
                    d_y2_read.wait(pe, kh, g + 1)
                    work.wait_free(pe, kh, ("u2", g))
                    for n in range(UG):
                        u = UG * g + n
                        cols = slice(0, 2) if n == 0 else slice(n, n + 1)
                        i = mm(work.bank(("u2", g))[0:128 if n == 0 else 64, n * 64:(n + 1) * 64],
                               Y2[64:128, g % 2, cols, :].rearrange("p a b -> p (a b)"), Ue[64:128, u, 64:128], True, True)
                    i.then_inc(d_u2_ready.sem, 1)

                def inverse_times_v(g):
                    d_u2_read.wait(pe, kh, g + 1)
                    for h in range(2):
                        d_w.wait(pe, kh, 2 * g + h + 1)
                        work.wait_free(pe, kh, ("u", g, h))
                        for n in range(4):
                            u = UG * g + 4 * h + n
                            i = mm(work.bank(("u", g, h))[:, n * P:(n + 1) * P], Ue[:, u, :], w_tok[:, u, :], True, True)
                        i.then_inc(d_u_ready.sem, 1)

                def attention(g):
                    for h in range(2):
                        d_up.wait(pe, kh, 2 * g + h + 1)
                        work.wait_free(pe, kh, ("o", g, h))
                        for n in range(4):
                            u = UG * g + 4 * h + n
                            i = mm(work.bank(("o", g, h))[:, n * P:(n + 1) * P], up[:, h, n, :], att[:, u, :], True, True)
                        i.then_inc(d_o_ready.sem, 1)

                def squares_of_outputs(g):
                    sums.wait_free(pe, kh, ("so", g), "ss" if last else None)
                    for h in range(2):
                        d_sqo.wait(pe, kh, 2 * g + h + 1)
                        for n in range(4):
                            u = UG * g + 4 * h + n
                            i = mm(small[:, SO + u:SO + u + 1], sqo[:, h, n, :], ones[:], True, True)
                        i.then_inc(d_so_ready.sem, 1)

                def project_out(g):
                    d_wo.wait(pe, kh, 1)
                    for b in range(G):
                        d_go.wait(pe, kh, 2 * g + b // 2 + 1)
                        proj.wait_free(pe, kh, ("y", g, b), "next" if last else None)
                        for hh in range(HH):
                            i = mm(proj.bank(("y", g, b))[:, hh * D:(hh + 1) * D], go[:, b // 2, 2 * (b % 2) + hh, :], wo[:, hh, :], True, True)
                        i.then_inc(d_y_ready.sem, 1)

                stage = {"ea": log_decays, "gk": products, "ss": sums_of_next, "vt": turn_v, "y1": first_of_32, "t1": second_of_32, "y2": first_of_64, "u2": second_of_64,
                         "u": inverse_times_v, "o": attention, "so": squares_of_outputs, "y": project_out,
                         "v": lambda g: project("v", g, d_v_in, wv, d_v_ready), "z": lambda g: project("z", g, d_z_in, wz, d_z_ready),
                         "next": lambda g: project_qk(kh, g, proj, lambda t: ("next", g, t))}
                for kind, g in PE_ORDER:
                    if not (last and kind in ("next", "ss")):
                        stage[kind](g)

            loop_then_last(pe, NK, head)

            d_acc.wait(pe, NK, 0)
            pe.wait_ge(m_in, M_LOADS)
            pe.wait_ge(m_q, 21)
            def mlps(g):
                m_x1.wait(pe, g, 1)
                for c in range(DC):
                    rest.wait_free(pe, g, ("x", c))
                    for b in range(G):
                        i = pe.transpose(rest.bank(("x", c))[:, b * P:(b + 1) * P], x1g[:, b, c * P:(c + 1) * P], ident[:])
                    i.then_inc(m_x1T_ready.sem, 1)
                m_x1T.wait(pe, g, 2)
                for n, a in enumerate((ag_s, au_s)):
                    rest.wait_free(pe, g, ("lg", n))
                    for c in range(DC):
                        i = mm(rest.bank(("lg", n))[:], a[:, c].rearrange("p n r -> p (n r)"), x1T[:, c, :], c == 0, c == DC - 1)
                    i.then_inc(m_lg_ready.sem, 1)
                for ct in range(I2 // P):
                    cols = slice(ct * P, (ct + 1) * P)
                    for n, (name, w, bb) in enumerate((("g", wg_s, bg_s), ("u", wu_s, bu_s))):
                        pairs.wait_free(pe, g, (name, ct))
                        for c in range(DC):
                            mm(pairs.bank((name, ct))[:], w[:, c, cols], x1T[:, c, :], c == 0, False)
                        if ct == 0:
                            m_lg.wait(pe, g, n + 1)
                        mm(pairs.bank((name, ct))[:], bb[:, cols], lg[:, n, :], False, True).then_inc(m_gu_ready.sem, 1)
                m_h.wait(pe, g, I2 // P)
                for n in range(2):
                    rest.wait_free(pe, g, ("ld", n))
                    for ct in range(I2 // P):
                        i = mm(rest.bank(("ld", n))[:, 0:256], ad_s[:, ct].rearrange("p n r -> p (n r)"),
                               hT[:, ct, n * 256:(n + 1) * 256], ct == 0, ct == I2 // P - 1)
                    i.then_inc(m_ld_ready.sem, 1)
                for e in range(DC):
                    rest.wait_free(pe, g, ("y", e))
                    for ct in range(I2 // P):
                        mm(rest.bank(("y", e))[:], wd_s[:, ct, e * P:(e + 1) * P], hT[:, ct, :], ct == 0, False)
                    m_ld.wait(pe, g, 2)
                    mm(rest.bank(("y", e))[:], bd_s[:, e * P:(e + 1) * P], lg[:, 2, :], False, True).then_inc(m_y_ready.sem, 1)
                m_y.wait(pe, g, 2)
                for ft in range(I3 // P):
                    for name, w in (("fg", qg_s), ("fu", qu_s)):
                        pairs.wait_free(pe, g, (name, ft))
                        for c in range(DC):
                            i = mm(pairs.bank((name, ft))[:], w[:, c * I3 + ft * P:c * I3 + (ft + 1) * P], yT[:, c, :], c == 0, c == DC - 1)
                        i.then_inc(m_fgu_ready.sem, 1)
                m_f.wait(pe, g, I3 // P)
                for b in range(G):
                    rest.wait_free(pe, g, ("d", b))
                    for ft in range(I3 // P):
                        i = mm(rest.bank(("d", b))[:, 0:D], fT[:, ft, b * S:(b + 1) * S], qd_s[:, ft * D:(ft + 1) * D], ft == 0, ft == I3 // P - 1)
                    i.then_inc(m_d_ready.sem, 1)

            first_then_loop(pe, NG, mlps)

        @block.scalar
        def _(act):
            def f(out_, in_, fn, **kw):
                return act.activation(out_, in_, fn, **kw)

            for n in range(4):
                act.wait_ge(a_wt_ready, n + 1)
                f(w_t[:, n].rearrange("p a b -> p (a b)"), ps[n][:], ACT.Copy).then_inc(a_wt_read, 1)

            def attend(g):
                a_x_ready.wait(act, g, 2)
                f(xgT[:, 1, :], front.bank(("x", 1))[:], ACT.Copy).then_inc(a_x_read.sem, 1)
                for m in range(2):
                    a_v_ready.wait(act, g, m + 1)
                    a_pv_ready.wait(act, g, 0)
                    f(vg[:, 2 * m:2 * m + 2, :].rearrange("p b d -> p (b d)"), front.bank(("v", m))[:], ACT.Copy).then_inc(a_v_read.sem, 1)
                for n in range(4 * G):
                    b, j = n // 4, n % 4
                    a_nmax.wait(act, g, n + 1)
                    a_pt_ready.wait(act, g, n - 1)
                    if j == 0:
                        a_rinv.wait(act, g, b - 1)
                    for s in range(4):
                        h = 8 * (s // 2) + 2 * j + s % 2
                        i = f(prob[:, n % 2, s, :], score.bank(n)[:, s * P:(s + 1) * P], ACT.Exp, bias=nmax[:, n % 2, s:s + 1],
                              accum_out=rsum[:, b % 2, h:h + 1])
                    i.then_inc(a_prob.sem, 1)
                for e in range(2):
                    a_ot_ready.wait(act, g, e + 1)
                    a_c_ready.wait(act, g, 0)
                    f(oTg[:, e, :], front.bank(("ot", e))[:], ACT.Copy).then_inc(a_ot_read.sem, 1)
                for e in range(2):
                    a_c_ready.wait(act, g, e + 1)
                    a_xT.wait(act, g, 0)
                    a_ba_ready.wait(act, g, 0)
                    f(cTg[:, e, :], front.bank(("c", e))[:], ACT.Copy).then_inc(a_c_read.sem, 1)

            first_then_loop(act, NG, attend)

            a_ba_read.wait(act, NG, 0)
            f(sp[0][:], ba[:, 0:NV, :], ACT.Tanh, scale=0.5).then_inc(gates_act, 1)
            f(nega[:], alog[:], ACT.Exp).then_inc(gates_act, 1)
            act.wait_ge(gates, 2)
            f(sp[3][:], sp[2][:], ACT.Exp, scale=-1.0).then_inc(gates_act, 1)
            act.wait_ge(gates_act, 3)
            f(sp[2][:], sp[3][:], ACT.Ln, bias=1.0).then_inc(gates_act, 1)

            act.wait_ge(gates, GATE_STEPS)

            def free_slot(step, conv, last):
                n = CONV.index(conv) - 4
                while last and n >= 0 and CONV[n][0] == "next":
                    n -= 4
                kind, g, t = CONV[n]
                done = 2 * g + t + 1 - (0 if n >= 0 else 8)
                if kind == "v":
                    d_silu_v.wait(act, step, done)
                else:
                    d_silu_q.wait(act, step, 8 + done)

            def tap_qk(step, g, banks, key):
                d_cwq_in.wait(act, step, 64)
                for t in range(2):
                    d_qk_ready.wait(act, step, 8 + 2 * g + t + 1)
                    if banks is proj:
                        free_slot(step, ("next", g, t), False)
                    else:
                        d_silu_q.wait(act, step, 8 + 2 * g + t + 1 - 4)
                    f(cbuf[:, conv_slot["next", g, t] if banks is proj else (2 * g + t) % 4, :], banks.bank(key(t))[:], ACT.Copy,
                      scale=cwq[:, t, KC - 1:KC]).then_inc(d_tap_q.sem, 1)

            def silu_qk(step, g, in_steps):
                if in_steps:
                    d_gk_ready.wait(act, step, 2 * g + 2)
                for t in range(2):
                    d_conv_q.wait(act, step, 8 + 2 * g + t + 1)
                    f(kq[:, g, t, :], cbuf[:, conv_slot["next", g, t] if in_steps else (2 * g + t) % 4, :], ACT.Silu).then_inc(d_silu_q.sem, 1)

            def squares(step, g, in_steps):
                d_silu_q.wait(act, step, 8 + 2 * g + 2)
                if g >= 2:
                    d_ss_ready.wait(act, step, NG + g - 1)
                elif in_steps:
                    (d_so_ready, d_y_ready)[g].wait(act, step, 0)
                f(sqb[g % 2], kq[:, g], ACT.Square).then_inc(d_sq.sem, 1)

            tap_qk(-1, 0, ahead, lambda t: (0, t))
            for g in range(NG):
                if g + 1 < NG:
                    tap_qk(-1, g + 1, ahead, lambda t: (g + 1, t))
                silu_qk(-1, g, False)
            for g in range(NG):
                squares(-1, g, False)

            def head(kh, last):
                def tap_v(g):
                    d_cwv_in.wait(act, kh, 16)
                    for t in range(2):
                        d_v_ready.wait(act, kh, 2 * g + t + 1)
                        free_slot(kh, ("v", g, t), last)
                        f(cbuf[:, conv_slot["v", g, t], :], proj.bank(("v", g, t))[:], ACT.Copy, scale=cwv[:, t, KC - 1:KC]).then_inc(d_tap_v.sem, 1)

                def silu_v(g):
                    d_vt_ready.wait(act, kh, 2 * g)
                    for t in range(2):
                        d_conv_v.wait(act, kh, 2 * g + t + 1)
                        f(vT[:, t, :], cbuf[:, conv_slot["v", g, t], :], ACT.Silu).then_inc(d_silu_v.sem, 1)

                def tap_next(g):
                    if not last:
                        tap_qk(kh, g, proj, lambda t: ("next", g, t))

                def silu_next(g):
                    if not last:
                        silu_qk(kh, g, True)

                def z_silu(g):
                    for t in range(2):
                        d_z_ready.wait(act, kh, 2 * g + t + 1)
                        d_go.wait(act, kh, 2 * g + 2 - 8)
                        f(zg[:, t, g * TG:(g + 1) * TG], proj.bank(("z", g, t))[:], ACT.Silu).then_inc(d_zg.sem, 1)

                def squares_next(g):
                    if not last:
                        squares(kh, g, True)

                def decays(g):
                    for h in range(2):
                        d_ea_ready.wait(act, kh, 2 * g + h + 1)
                        d_B.wait(act, kh, 2 * g + h - 1)
                        f(E[:, h].rearrange("p u i -> p (u i)"), proj.bank(("ea", g, h))[:], ACT.Exp).then_inc(d_E.sem, 1)

                def keep_v(g):
                    d_knorm.wait(act, kh, 1)
                    d_u_ready.wait(act, kh, 2 * g + 2 - 8)
                    for h in range(2):
                        d_vt_ready.wait(act, kh, 2 * g + h + 1)
                        for b in range(2):
                            u = UG * g + 4 * h + 2 * b
                            s = G * g + 2 * h + b
                            i = f(w_tok[:, u:u + 2, :].rearrange("p u c -> p (u c)"), work.bank(("vt", g, h))[:, b * 2 * P:(b + 1) * 2 * P],
                                  ACT.Copy, scale=knorm[:, s:s + 1])
                        i.then_inc(d_w.sem, 1)

                def spread():
                    d_unlane.wait(act, kh, 2)
                    d_y2_ready.wait(act, kh, 0)
                    for r in range(4):
                        rows = slice(BK * r, BK * r + BK)
                        f(Le[rows, :, BK * (r % 2):BK * (r % 2) + BK], diag_l[rows], ACT.Copy).then_inc(d_spread_l.sem, 1)

                def read_y1(fh):
                    for p in range(2):
                        hi = slice(64 * p + BK, 64 * p + 2 * BK)
                        d_y1_ready.wait(act, kh, 2 * fh + p + 1)
                        d_t1_ready.wait(act, kh, 2 * fh + p + 1 - 4)
                        f(Y1[hi, 16 * fh:16 * fh + 16].rearrange("p u c -> p (u c)"), work.bank(("y1", fh, p))[hi, :], ACT.Copy).then_inc(d_y1_read.sem, 1)

                def read_y2(g):
                    d_y2_ready.wait(act, kh, g + 1)
                    d_u2_ready.wait(act, kh, g - 1)
                    f(Y2[64:128, g % 2].rearrange("p u c -> p (u c)"), work.bank(("y2", g))[64:128, :], ACT.Copy).then_inc(d_y2_read.sem, 1)

                def read_u(g):
                    for h in range(2):
                        d_u_ready.wait(act, kh, 2 * g + h + 1)
                        d_o_ready.wait(act, kh, 2 * g + h - 1)
                        for n in range(4):
                            b = G * g + 2 * h + n // 2
                            i = f(up[:, h, n, :], work.bank(("u", g, h))[:, n * P:(n + 1) * P], ACT.Copy, scale=cpos[:, b, n % 2:n % 2 + 1])
                        i.then_inc(d_up.sem, 1)

                def square_o(g):
                    for h in range(2):
                        d_o_ready.wait(act, kh, 2 * g + h + 1)
                        d_so_ready.wait(act, kh, 2 * g + h - 1)
                        f(sqo[:, h].rearrange("p u c -> p (u c)"), work.bank(("o", g, h))[:], ACT.Square).then_inc(d_sqo.sem, 1)

                for g in range(NG):
                    decays(g)
                tap_v(0); z_silu(0)
                tap_next(0); silu_v(0)
                tap_v(1); silu_next(0); z_silu(1); keep_v(0); squares_next(0)
                tap_next(1); silu_v(1)
                tap_v(2); silu_next(1); z_silu(2); keep_v(1); squares_next(1)
                tap_next(2); silu_v(2)
                tap_v(3); silu_next(2); z_silu(3); read_y1(0); read_y1(1); keep_v(2); squares_next(2)
                tap_next(3); silu_v(3)
                spread()
                silu_next(3); squares_next(3); keep_v(3)
                read_y2(0)
                read_y2(1)
                read_y2(2)
                read_u(0)
                read_y2(3)
                if not last:
                    d_ss_ready.wait(act, kh, 2 * NG)
                square_o(0); read_u(1)
                square_o(1); read_u(2)
                square_o(2); read_u(3)
                square_o(3)

            loop_then_last(act, NK, head)

            d_acc.wait(act, NK, 0)
            act.wait_ge(m_in, M_LOADS)

            def mlps(g):
                m_x1T_ready.wait(act, g, 2)
                f(x1T[:, 1, :], rest.bank(("x", 1))[:], ACT.Copy).then_inc(m_x1T.sem, 1)
                for ct in range(I2 // P):
                    m_gu_ready.wait(act, g, 2 * ct + 1)
                    m_h.wait(act, g, ct - 1)
                    f(sg[:, ct % 2, :], pairs.bank(("g", ct))[:], ACT.Silu).then_inc(m_sg.sem, 1)
                for e in range(DC):
                    m_y_ready.wait(act, g, e + 1)
                    m_fgu_ready.wait(act, g, 0)
                    f(yT[:, e, :], rest.bank(("y", e))[:], ACT.Copy).then_inc(m_y.sem, 1)
                for ft in range(I3 // P):
                    m_fgu_ready.wait(act, g, 2 * ft + 1)
                    m_h.wait(act, g, I2 // P)
                    m_f.wait(act, g, ft - 1)
                    f(sg[:, ft % 2, :], pairs.bank(("fg", ft))[:], ACT.Silu, scale=gsc[:, ft:ft + 1]).then_inc(m_fs.sem, 1)

            first_then_loop(act, NG, mlps)

        @block.vector
        def _(dve):
            dve.wait_ge(consts, 14)
            dve.tensor_scalar(part[:, 1:2], part[:, 0:1], 16, None, ALU.bitwise_and).then_inc(consts, 1)
            dve.tensor_scalar(part[:, 2:3], part[:, 0:1], 4, None, ALU.logical_shift_right).then_inc(picked, 1)
            dve.wait_ge(consts, 15)
            dve.tensor_scalar(head_even[:], part[:, 1:2], 0, None, ALU.is_equal).then_inc(consts, 1)
            dve.tensor_scalar(head_odd[:], part[:, 1:2], 0, None, ALU.is_gt).then_inc(consts, 1)
            dve.wait_ge(picked, 1)
            dve.tensor_copy(own[:], part[:, 2:3]).then_inc(picked, 1)
            dve.wait_ge(a_small_in, 80)
            dve.tensor_scalar(precs[:], precb[:], 4.0, HD_A ** -0.5, ALU.min, ALU.mult).then_inc(a_prec, 1)
            dve.wait_ge(consts, CONSTS)
            dve.wait_ge(a_prec, 1)

            def attend(g):
                a_x_ready.wait(dve, g, 1)
                dve.tensor_copy(xgT[:, 0, :], front.bank(("x", 0))[:]).then_inc(a_x_read.sem, 1)
                for e in range(2):
                    a_q_ready.wait(dve, g, e + 1)
                    a_s_ready.wait(dve, g, 0)
                    dve.tensor_tensor(qTa[:, e, :].rearrange("p (b t) -> p b t", b=G), front.bank(("q", e))[:].rearrange("p (b t) -> p b t", b=G),
                                      precs[:, bass.ds(g * G, G)].rearrange("p (b t) -> p b t", t=1).broadcast_to([P, G, S]),
                                      ALU.mult).then_inc(a_q_read.sem, 1)
                for e in range(2):
                    a_k_ready.wait(dve, g, e + 1)
                    for kt, mask in ((kTe, head_even), (kTo, head_odd)):
                        dve.tensor_scalar(kt[:, e, :], front.bank(("k", e))[:], mask[:, 0:1], None, ALU.mult).then_inc(a_k_read.sem, 1)

                def maxima(n):
                    a_s_ready.wait(dve, g, n + 1)
                    dve.tensor_reduce(rmax[:, n % 2, :], score.bank(n)[:].rearrange("p (s k) -> p s k", s=4), AX_X, ALU.max).then_inc(a_max.sem, 1)
                    a_max.wait(dve, g, n + 1)
                    a_prob.wait(dve, g, n - 1)
                    dve.tensor_scalar(nmax[:, n % 2, :], rmax[:, n % 2, :], -1.0, None, ALU.mult).then_inc(a_nmax.sem, 1)

                maxima(0)
                maxima(1)
                for n in range(4 * G):
                    b = n // 4
                    a_pt_ready.wait(dve, g, n + 1)
                    a_pv_ready.wait(dve, g, n - 1)
                    dve.tensor_copy(probT[:, n % 2].rearrange("p s q -> p (s q)"), turned.bank(n)[:]).then_inc(a_pt_read.sem, 1)
                    if n + 2 < 4 * G:
                        maxima(n + 2)
                    if n % 4 == 3:
                        dve.reciprocal(rinv[:, b % 2, :], rsum[:, b % 2, :]).then_inc(a_rinv.sem, 1)
                        a_rinv.wait(dve, g, b + 1)
                        a_pv_ready.wait(dve, g, n + 1)
                        a_ot_ready.wait(dve, g, 0)
                        dve.tensor_tensor(oa[:, b, :].rearrange("p (h d) -> p h d", h=NH_A),
                                          front.bank(("pv", b))[:, 0:D].rearrange("p (h d) -> p h d", h=NH_A),
                                          rinv[:, b % 2, :].rearrange("p (h d) -> p h d", d=1).broadcast_to([P, NH_A, HD_A]),
                                          ALU.mult).then_inc(a_o_read.sem, 1)
                for b in range(G):
                    a_ba_ready.wait(dve, g, b + 1)
                    dve.tensor_copy(ba[:, :, bass.ds(g * G + b, 1)], front.bank(("ba", b))[:, 0:2 * NV].rearrange("p (c a) -> p c a", a=1)
                                    ).then_inc(a_ba_read.sem, 1)

            first_then_loop(dve, NG, attend)

            by_batch = lambda t: t.rearrange("p (n a) -> p n a", a=1).broadcast_to([P, NV, B])
            a_ba_read.wait(dve, NG, 0)
            dve.tensor_tensor(sp[1][:], ba[:, NV:2 * NV, :], by_batch(dtb[:]), ALU.add).then_inc(gates, 1)
            dve.wait_ge(gates, 1)
            flat = [t[:].rearrange("p n b -> p (n b)") for t in sp]
            dve.scalar_tensor_tensor(out=flat[2], in0=flat[1], scalar=-1.0, in1=flat[1], op0=ALU.mult, op1=ALU.max).then_inc(gates, 1)
            dve.wait_ge(gates_act, 2)
            for hh in range(HH):
                dve.tensor_scalar(beta[:, :, :, hh], sp[0][:].rearrange("p (k h) b -> p h k b", h=HH)[:, hh], 0.5, 0.5,
                                  ALU.mult, ALU.add).then_inc(gates, 1)
            dve.tensor_scalar(alog[:], nega[:], -1.0, None, ALU.mult).then_inc(gates, 1)
            dve.wait_ge(gates_act, 4)
            dve.scalar_tensor_tensor(out=flat[3], in0=flat[1], scalar=0.0, in1=flat[2], op0=ALU.max, op1=ALU.add).then_inc(gates, 1)
            dve.wait_ge(gates, 6)
            dve.tensor_tensor(sp[0][:], sp[3][:], by_batch(alog[:]), ALU.mult).then_inc(gates, 1)
            dve.wait_ge(gates, 7)
            for hh in range(HH):
                dve.tensor_copy(gdec[:, :, :, hh], sp[0][:].rearrange("p (k h) b -> p h k b", h=HH)[:, hh]).then_inc(gates, 1)
            dve.wait_ge(gates, GATE_STEPS)
            dve.wait_ge(x_in, 64)

            def rsqrt(kh, y, v, t, steps, first):
                n = first
                dve.tensor_scalar(t.bitcast(I32), v.bitcast(I32), 1, None, ALU.logical_shift_right).then_inc(steps.sem, 1)
                steps.wait(dve, kh, n + 1)
                dve.tensor_scalar(y.bitcast(I32), t.bitcast(I32), -1.0, RSQRT_SEED, ALU.mult, ALU.add).then_inc(steps.sem, 1)
                n += 2
                for k in range(3):
                    steps.wait(dve, kh, n)
                    dve.tensor_tensor(t, y, y, ALU.mult).then_inc(steps.sem, 1)
                    steps.wait(dve, kh, n + 1)
                    dve.scalar_tensor_tensor(out=t, in0=t, scalar=-0.5, in1=v, op0=ALU.mult, op1=ALU.mult).then_inc(steps.sem, 1)
                    steps.wait(dve, kh, n + 2)
                    i = dve.scalar_tensor_tensor(out=y, in0=t, scalar=1.5, in1=y, op0=ALU.add, op1=ALU.mult)
                    n += 3
                    i.then_inc(steps.sem, 1)
                return n

            def convolve(step, bank, buf, weights, n, tap, taps_done, steps):
                tap.wait(dve, step, n + 1)
                taps = bank[:].rearrange("p (b t) -> p b t", b=G)
                whole = buf.rearrange("p (b t) -> p b t", b=G)
                for d in range(1, KC):
                    if d > 1:
                        steps.wait(dve, step, 2 * n + d - 1)
                    i = dve.scalar_tensor_tensor(out=whole[:, :, d:S], in0=taps[:, :, 0:S - d], scalar=weights[:, KC - 1 - d:KC - d],
                                                 in1=whole[:, :, d:S], op0=ALU.mult, op1=ALU.add)
                    i.then_inc(taps_done.sem if d == KC - 1 else steps.sem, 1)

            d_cwq_in.wait(dve, -1, 64)
            for g in range(NG):
                for t in range(2):
                    convolve(-1, ahead.bank((g, t)), cbuf[:, (2 * g + t) % 4, :], cwq[:, t, :], 8 + 2 * g + t, d_tap_q, d_conv_q, d_step_q)

            def keep_sums(step):
                d_ss_ready.wait(dve, step, 2 * NG)
                dve.tensor_copy(ssum[:], small[:, SK:SK + 2 * B]).then_inc(d_ss_read.sem, 1)

            keep_sums(-1)

            def head(kh, last):
                def conv_v(g):
                    d_cwv_in.wait(dve, kh, 16)
                    for t in range(2):
                        convolve(kh, proj.bank(("v", g, t)), cbuf[:, conv_slot["v", g, t], :], cwv[:, t, :], 2 * g + t, d_tap_v, d_conv_v, d_step_v)

                def conv_next(g):
                    if last:
                        return
                    d_cwq_in.wait(dve, kh, 64)
                    for t in range(2):
                        convolve(kh, proj.bank(("next", g, t)), cbuf[:, conv_slot["next", g, t], :], cwq[:, t, :], 8 + 2 * g + t, d_tap_q, d_conv_q, d_step_q)

                def factors():
                    d_ss_read.wait(dve, kh, 1)
                    d_osc.wait(dve, kh, 0)
                    dve.tensor_scalar(ksum[:], ssum[:, SK:SK + B], EPS, None, ALU.add).then_inc(d_rec.sem, 1)
                    dve.tensor_scalar(qeps[:], ssum[:, SQ:SQ + B], EPS * DK, EPS * EPS * DK, ALU.mult, ALU.add)
                    d_rec.wait(dve, kh, 1)
                    dve.reciprocal(krec[:], ksum[:]).then_inc(d_c1.sem, 1)
                    d_c1.wait(dve, kh, 1)
                    d_up.wait(dve, kh, 0)
                    dve.tensor_tensor(cpos[:], beta[:, bass.ds(kh, 1), :, :].rearrange("p a b h -> p (a b) h"),
                                      krec[:].rearrange("p (b h) -> p b h", h=1).broadcast_to([P, B, HH]), ALU.mult).then_inc(d_c.sem, 1)
                    d_c.wait(dve, kh, 1)
                    dve.tensor_scalar(cneg[:], cpos[:], -1.0, None, ALU.mult).then_inc(d_cneg.sem, 1)

                def masks(g):
                    d_y2_ready.wait(dve, kh, 0)
                    d_o_ready.wait(dve, kh, 2 * g + 2 - 8)
                    for h in range(2):
                        d_E.wait(dve, kh, 2 * g + h + 1)
                        d_gk_ready.wait(dve, kh, 2 * g + h + 1)
                        gk = work.bank(("gk", g, h))[:].rearrange("p (b t i) -> p b t i", b=2, t=2)
                        u = UG * g + 4 * h
                        dve.tensor_tensor(att[:, u:u + 4, :].rearrange("p (b h) i -> p b h i", b=2),
                                          gk[:, :, 1:2, :].broadcast_to([P, 2, HH, P]),
                                          E[:, h].rearrange("p (b h) i -> p b h i", b=2), ALU.mult)
                        d_cneg.wait(dve, kh, 1)
                        for n in range(4):
                            u = UG * g + 4 * h + n
                            b = G * g + 2 * h + n // 2
                            i = dve.scalar_tensor_tensor(out=Bm[:, u, :], in0=gk[:, n // 2, 0, :], scalar=cneg[:, b, n % 2:n % 2 + 1],
                                                         in1=E[:, h, n, :], op0=ALU.mult, op1=ALU.mult)
                        i.then_inc(d_B.sem, 1)

                def diagonal(g):
                    d_B.wait(dve, kh, 2 * g + 2)
                    us = slice(UG * g, UG * g + UG)
                    for r in range(4):
                        rows = slice(BK * r, BK * r + BK)
                        i = dve.tensor_copy(diag_l[rows, us, :], Bm[rows, us, rows])
                    i.then_inc(d_diag.sem, 1)

                def to_lanes():
                    dve.memset(lane_T[:], 0.0).then_inc(d_lanes.sem, 1)
                    d_lanes.wait(dve, kh, 1)
                    dve.memset(lane_T[:].rearrange("p a b -> p (a b)")[:, 0:BK * BK:BK + 1], 1.0).then_inc(d_lanes.sem, 1)
                    d_diag.wait(dve, kh, NG)
                    dve.transpose(diag_u[:], diag_l[:].rearrange("p u a -> p a u")).then_inc(d_lanes.sem, 1)

                def from_lanes():
                    d_solve.wait(dve, kh, d_solve.per)
                    dve.transpose(diag_l[:].rearrange("p u k -> p k u"), lane_T[:].rearrange("p i k -> p k i")).then_inc(d_unlane.sem, 1)
                    dve.transpose(diag_u[:].rearrange("p u i -> p i u"), lane_T[:]).then_inc(d_unlane.sem, 1)

                def key_norms():
                    d_rec.wait(dve, kh, 1)
                    d_w.wait(dve, kh, 0)
                    rsqrt(kh, nt[:, 0, 0:B], ksum[:], nt[:, 1, 0:B], d_newt, 0)
                    d_newt.wait(dve, kh, 11)
                    dve.tensor_tensor(knorm[:], nt[:, 0, 0:B], ksum[:], ALU.mult).then_inc(d_knorm.sem, 1)

                def spread():
                    d_unlane.wait(dve, kh, 2)
                    d_u_ready.wait(dve, kh, 0)
                    for r in range(4):
                        rows = slice(BK * r, BK * r + BK)
                        dve.tensor_copy(Ue[rows, :, rows], diag_u[rows]).then_inc(d_spread_u.sem, 1)

                def read_t1(fh):
                    us = slice(16 * fh, 16 * fh + 16)
                    for p in range(2):
                        lo, hi = slice(64 * p, 64 * p + BK), slice(64 * p + BK, 64 * p + 2 * BK)
                        d_t1_ready.wait(dve, kh, 2 * fh + p + 1)
                        d_u_ready.wait(dve, kh, 0)
                        bank = work.bank(("t1", fh, p))[:].rearrange("p (u c) -> p u c", c=BK)
                        dve.tensor_copy(Le[hi, us, 0:BK], bank[hi])
                        dve.tensor_copy(Ue[lo, us, hi], bank[lo]).then_inc(d_t1_read.sem, 1)

                def read_u2(g):
                    d_u2_ready.wait(dve, kh, g + 1)
                    dve.tensor_copy(Ue[0:64, UG * g:UG * g + UG, 64:128],
                                    work.bank(("u2", g))[0:64, :].rearrange("p (u c) -> p u c", c=64)).then_inc(d_u2_read.sem, 1)

                def gate(g, h):
                    d_sqo.wait(dve, kh, 2 * g + h + 1)
                    d_zg.wait(dve, kh, 2 * g + 2)
                    d_y_ready.wait(dve, kh, G * g + 2 * h + 2 - G)
                    t0 = g * TG + h * 2 * S
                    dve.tensor_tensor(go[:, h].rearrange("p (b h) t -> p b h t", b=2), work.bank(("o", g, h))[:].rearrange("p (b h t) -> p b h t", b=2, h=HH),
                                      zg[:, :, t0:t0 + 2 * S].rearrange("p h (b t) -> p b h t", b=2), ALU.mult).then_inc(d_go.sem, 1)

                def out_norms(g):
                    bs = slice(G * g, G * g + G)
                    v = nt[:, 2, 0:UG]
                    d_so_ready.wait(dve, kh, 2 * g + 2)
                    dve.scalar_tensor_tensor(out=v.rearrange("p (b h) -> p b h", h=HH),
                                             in0=small[:, SO + UG * g:SO + UG * g + UG].rearrange("p (b h) -> p b h", h=HH), scalar=1.0 / DV,
                                             in1=qeps[:, bs].rearrange("p (b h) -> p b h", h=1).broadcast_to([P, G, HH]),
                                             op0=ALU.mult, op1=ALU.add).then_inc(d_so_read.sem, 1)
                    d_so_read.wait(dve, kh, g + 1)
                    n = rsqrt(kh, nt[:, 0, 0:UG], v, nt[:, 1, 0:UG], d_nto, 11 * g)
                    d_nto.wait(dve, kh, n)
                    dve.tensor_copy(osc[:, bs, :].rearrange("p b h -> p (b h)"), nt[:, 0, 0:UG]).then_inc(d_osc.sem, 1)
                    d_osc.wait(dve, kh, g + 1)

                def accumulate(g, h):
                    for b in (2 * h, 2 * h + 1):
                        s = G * g + b
                        d_y_ready.wait(dve, kh, s + 1)
                        for hh in range(HH):
                            if hh:
                                d_acc_step.wait(dve, kh, s + 1)
                            i = dve.scalar_tensor_tensor(out=acc[:, s, :], in0=proj.bank(("y", g, b))[:, hh * D:(hh + 1) * D], scalar=osc[:, s, hh:hh + 1],
                                                         in1=acc[:, s, :], op0=ALU.mult, op1=ALU.add)
                            i.then_inc(d_acc.sem if hh else d_acc_step.sem, 1)

                factors()
                for g in range(NG):
                    masks(g)
                    diagonal(g)
                to_lanes()
                key_norms()
                for g in range(NG - 1):
                    conv_v(g)
                    conv_next(g)
                from_lanes()
                conv_v(NG - 1)
                spread()
                conv_next(NG - 1)
                read_t1(0)
                read_t1(1)
                if not last:
                    keep_sums(kh)
                read_u2(0)
                read_u2(1)
                read_u2(2)
                gate(0, 0)
                gate(0, 1)
                read_u2(3)
                for g in range(NG):
                    out_norms(g)
                    for h in range(2):
                        if g + 1 < NG:
                            gate(g + 1, h)
                        accumulate(g, h)

            loop_then_last(dve, NK, head)

            d_acc.wait(dve, NK, 0)
            dve.wait_ge(m_in, M_LOADS)
            n = 0
            for w in (qg_s, qu_s, qd_s):
                dve.tensor_scalar(q8a[:], w[:], 240.0, -240.0, ALU.min, ALU.max, saturate=False).then_inc(m_q, 1)
                dve.tensor_scalar(qdif[:], w[:], 0.5, 240.0, ALU.mult, ALU.min).then_inc(m_q, 1)
                dve.scalar_tensor_tensor(out=qm[:], in0=w[:], scalar=-1.0, in1=w[:], op0=ALU.mult, op1=ALU.max).then_inc(m_q, 1)
                dve.wait_ge(m_q, n + 3)
                dve.tensor_scalar(q8b[:], qdif[:], -240.0, None, ALU.max, saturate=False).then_inc(m_q, 1)
                dve.wait_ge(m_q, n + 4)
                dve.scalar_tensor_tensor(out=qdif[:], in0=q8b[:], scalar=2.0, in1=q8a[:], op0=ALU.mult, op1=ALU.subtract).then_inc(m_q, 1)
                dve.wait_ge(m_q, n + 5)
                dve.scalar_tensor_tensor(out=qdif[:], in0=qm[:], scalar=240.0, in1=qdif[:], op0=ALU.is_gt, op1=ALU.mult).then_inc(m_q, 1)
                dve.wait_ge(m_q, n + 6)
                dve.tensor_tensor(w[:], qdif[:], q8a[:], ALU.add).then_inc(m_q, 1)
                dve.wait_ge(m_q, n + 7)
                n += 7
            dve.wait_ge(picked, 2)
            dve.tensor_copy(idx_f[:], idx_i[:]).then_inc(m_pick, 1)
            dve.wait_ge(m_pick, 1)
            dve.tensor_scalar(pick[:], idx_f[:], own[:, 0:1], None, ALU.is_equal).then_inc(m_pick, 1)
            dve.wait_ge(m_pick, 2)

            def mlps(g):
                m_x1T_ready.wait(dve, g, 1)
                dve.tensor_copy(x1T[:, 0, :], rest.bank(("x", 0))[:]).then_inc(m_x1T.sem, 1)

                def keep_own(dst, src, b0, nb, done):
                    dve.tensor_tensor(dst.rearrange("p (b t) -> p b t", b=nb), src.rearrange("p (b t) -> p b t", b=nb),
                                      pick[:, bass.ds(g * G + b0, nb)].rearrange("p (b t) -> p b t", t=1).broadcast_to([P, nb, S]),
                                      ALU.mult).then_inc(done.sem, 1)

                for n in range(2):
                    m_lg_ready.wait(dve, g, n + 1)
                    m_gu_ready.wait(dve, g, 0)
                    keep_own(lg[:, n, :], rest.bank(("lg", n))[:], 0, G, m_lg)
                for ct in range(I2 // P):
                    m_gu_ready.wait(dve, g, 2 * ct + 2)
                    m_sg.wait(dve, g, ct + 1)
                    m_y_ready.wait(dve, g, 0)
                    dve.tensor_tensor(hT[:, ct, :], sg[:, ct % 2, :], pairs.bank(("u", ct))[:], ALU.mult).then_inc(m_h.sem, 1)
                for n in range(2):
                    m_ld_ready.wait(dve, g, n + 1)
                    m_y_ready.wait(dve, g, 0)
                    keep_own(lg[:, 2, n * 256:(n + 1) * 256], rest.bank(("ld", n))[:, 0:256], 2 * n, 2, m_ld)
                for ft in range(I3 // P):
                    m_fgu_ready.wait(dve, g, 2 * ft + 2)
                    m_fs.wait(dve, g, ft + 1)
                    m_d_ready.wait(dve, g, 0)
                    dve.scalar_tensor_tensor(out=fT[:, ft, :], in0=pairs.bank(("fu", ft))[:], scalar=usc[:, ft:ft + 1], in1=sg[:, ft % 2, :],
                                             op0=ALU.mult, op1=ALU.mult).then_inc(m_f.sem, 1)
                for b in range(G):
                    m_d_ready.wait(dve, g, b + 1)
                    dve.tensor_tensor(dn[:, b % 2, :], rest.bank(("d", b))[:, 0:D], dsc[:], ALU.mult).then_inc(m_dn.sem, 1)
                    m_dn.wait(dve, g, b + 1)
                    m_out.wait(dve, g, 0)
                    dve.tensor_tensor(og[:, b, :], dn[:, b % 2, :], x1g[:, b, :], ALU.add).then_inc(m_og.sem, 1)

            first_then_loop(dve, NG, mlps)


_INS = ['x', 'cond_1', 'itok_B_0_7', 'L0_cond_Wq', 'L0_cond_Wk', 'L0_cond_Wv', 'L0_cond_Wo', 'L0_attn_W_qkv', 'L0_attn_W_z',
        'L0_attn_W_b', 'L0_attn_W_a', 'L0_attn_conv_w', 'L0_attn_dt_bias', 'L0_attn_A_log', 'L0_attn_norm_w', 'L0_attn_W_out',
        'L0_cond2_Wg', 'L0_cond2_Wu', 'L0_cond2_Wd', 'L0_cond2_Ag', 'L0_cond2_Bg', 'L0_cond2_Au', 'L0_cond2_Bu', 'L0_cond2_Ad',
        'L0_cond2_Bd', 'L0_ffn_gate_w', 'L0_ffn_up_w', 'L0_ffn_down_w', 'L0_ffn_gate_scale', 'L0_ffn_up_scale', 'L0_ffn_down_scale']


def kernel(**inputs):
    import numpy as np
    import concourse.bacc as bacc
    from concourse.bass_utils import run_bass_kernel_spmd

    nc = bacc.Bacc("TRN2", target_bir_lowering=False, num_devices=1)
    arrays, args = {}, []
    for name in _INS:
        a = np.ascontiguousarray(inputs[name])
        arrays[f"in_{name}"] = a
        args.append(nc.dram_tensor(f"in_{name}", a.shape, mybir.dt.from_np(a.dtype), kind="ExternalInput").ap())
    out = nc.dram_tensor("out", (B, S, D), F32, kind="ExternalOutput").ap()
    build(nc, *args, out)
    r = run_bass_kernel_spmd(nc, [arrays], core_ids=[0])
    return r.results[0]["out"]
```

```python
from contextlib import ExitStack

import concourse.bass as bass
from concourse import mybir

F32 = mybir.dt.float32
BF16 = mybir.dt.bfloat16
FP8 = mybir.dt.float8e4
I32 = mybir.dt.int32
F32R = mybir.dt.float32r
ALU = mybir.AluOpType
ACT = mybir.ActivationFunctionType
AX_X = mybir.AxisListType.X

P = 128
B, S, D = 16, 128, 256
DC = D // P
G = 4
NG = B // G
TG = G * S
NH_A, HD_A = 16, 16
NK, NV, DK, DV, KC = 16, 32, 128, 128, 4
HH = NV // NK
UN = B * HH
UG = G * HH
BK = 32
EPS = 1e-6
BIG = 1e30
RSQRT_SEED = 1597463007.0
N_AD, RK, I2, I3 = 8, 16, 1024, 768


class Signal:

    def __init__(self, sem, per):
        self.sem, self.per, self.passed = sem, per, {}

    def wait(self, eng, step, n):
        seen, most = self.passed.get(id(eng), (None, 0))
        if seen is step and most >= n:
            return
        self.passed[id(eng)] = (step, n)
        value = step * self.per + n
        if isinstance(value, int) and value <= 0:
            return
        eng.wait_ge(self.sem, value)


def first_then_loop(eng, steps, body):
    body(0)
    with eng.Fori(1, steps) as step:
        body(step)


def loop_then_last(eng, steps, body):
    body(0, False)
    with eng.Fori(1, steps - 1) as step:
        body(step, False)
    body(steps - 1, True)


class Banks:

    def __init__(self, banks, uses):
        assert len(uses) % len(banks) == 0
        self.banks, self.uses = banks, uses
        self.index = {key: n for n, (key, _, _) in enumerate(uses)}

    def bank(self, key):
        return self.banks[self.index[key] % len(self.banks)]

    def wait_free(self, eng, step, key, left_out=()):
        n = self.index[key] - len(self.banks)
        while left_out and n >= 0 and self.uses[n][0][0] in left_out:
            n -= len(self.banks)
        _, reader, count = self.uses[n]
        reader.wait(eng, step, count if n >= 0 else count - reader.per)


def build(nc, x, prec, adapter, Wq, Wk, Wv, Wo, W_qkv, W_z, W_b, W_a, conv_w, dt_bias, A_log, norm_w,
          W_out, Wg, Wu, Wd, Ag, Bg, Au, Bu, Ad, Bd, gate_w, up_w, down_w, gate_s, up_s, down_s, out):
    top = ExitStack()

    def sem(name):
        return top.enter_context(nc.semaphore(name))

    def sig(name, per):
        return Signal(sem(name), per)

    def tile(stack, name, shape, dt=F32):
        return stack.enter_context(nc.sbuf_tensor(name, shape, dt))

    with top:
        ps = [top.enter_context(nc.psum_tensor(f"bank{i}", [P, 512], F32)) for i in range(8)]

        acc = tile(top, "acc", [P, B, D])
        ident = tile(top, "ident", [P, P])
        identb = tile(top, "identb", [P, P], BF16)
        later_t = tile(top, "later_t", [P, P])
        upto_t = tile(top, "upto_t", [P, P])
        ones = tile(top, "ones", [P, 1])
        cm_qk = tile(top, "cm_qk", [P, P], BF16)
        cm_kq = tile(top, "cm_kq", [P, P], BF16)
        head_even = tile(top, "head_even", [P, 1])
        head_odd = tile(top, "head_odd", [P, 1])
        part = tile(top, "part", [P, 3], I32)
        own = tile(top, "own", [P, 1])

        consts = sem("consts")
        x_in = sem("x_in")

        fr = ExitStack()
        beta = tile(top, "beta", [P, NK, B, HH])
        gdec = tile(top, "gdec", [P, NK, B, HH])
        xT = tile(top, "xT", [P, DC, B * S])
        w_raw = tile(fr, "w_raw", [P, 4, 2, D])
        w_t = tile(fr, "w_t", [P, 4, 2, D])
        w_ba = tile(fr, "w_ba", [P, DC, 2, NV])
        xg = tile(fr, "xg", [P, G, D])
        xgT = tile(fr, "xgT", [P, DC, TG])
        precb = tile(fr, "precb", [P, B])
        precs = tile(fr, "precs", [P, B])
        qTa = tile(fr, "qTa", [P, 2, TG])
        kTe = tile(fr, "kTe", [P, 2, TG])
        kTo = tile(fr, "kTo", [P, 2, TG])
        vg = tile(fr, "vg", [P, G, D])
        rmax = tile(fr, "rmax", [P, 2, 4])
        nmax = tile(fr, "nmax", [P, 2, 4])
        rsum = tile(fr, "rsum", [P, 2, NH_A])
        rinv = tile(fr, "rinv", [P, 2, NH_A])
        prob = tile(fr, "prob", [P, 2, 4, P])
        probT = tile(fr, "probT", [P, 2, 4, P])
        oa = tile(fr, "oa", [P, G, D])
        oTg = tile(fr, "oTg", [P, 2, TG])
        cTg = tile(fr, "cTg", [P, DC, TG])
        ba = tile(fr, "ba", [P, 2 * NV, B])
        dtb = tile(fr, "dtb", [P, NV])
        alog = tile(fr, "alog", [P, NV])
        nega = tile(fr, "nega", [P, NV])
        sp = [tile(fr, f"sp{i}", [P, NV, B]) for i in range(4)]

        fr.close()
        gd = ExitStack()
        wv = tile(gd, "wv", [P, DC, HH * DV])
        wz = tile(gd, "wz", [P, DC, HH * DV])
        wo_in = tile(gd, "wo_in", [P, HH, D])
        wo = tile(gd, "wo", [P, HH, D])
        cbuf = tile(gd, "cbuf", [P, 4, TG])
        kq = tile(gd, "kq", [P, NG, 2, TG])
        V = tile(gd, "V", [P, UG, P])
        E = tile(gd, "E", [P, 2, 4, P])
        wqk = tile(gd, "wqk", [P, DC, 2, P])
        Bm = tile(gd, "Bm", [P, UN, P])
        Le = tile(gd, "Le", [P, UN, 2 * BK])
        diag_l = tile(gd, "diag_l", [P, UN, BK])
        diag_u = tile(gd, "diag_u", [P, UN, BK])
        lane_T = tile(gd, "lane_T", [P, BK, BK])
        Y1 = lane_T
        lane_p = tile(gd, "lane_p", [P, (BK // 2) ** 2])
        vT = tile(gd, "vT", [P, HH, TG])
        Y2 = tile(gd, "Y2", [P, 2, UG, 2 * BK])
        att = tile(gd, "att", [P, UN, P])
        w_tok = tile(gd, "w_tok", [P, UN, P])
        zg = tile(gd, "zg", [P, HH, B * S])
        Ue = tile(gd, "Ue", [P, UN, P])
        cwq = tile(gd, "cwq", [P, 2, KC])
        cwv = tile(gd, "cwv", [P, HH, KC])
        nw = tile(gd, "nw", [P, 1])
        up = tile(gd, "up", [P, 2, 4, P])
        sqo = tile(gd, "sqo", [P, 2, 4, P])
        go = tile(gd, "go", [P, 2, 4, P])
        sqb = [t[:].rearrange("p h n i -> p h (n i)") for t in (sqo, go)]
        ssum = tile(gd, "ssum", [P, 2 * B])
        ksum = tile(gd, "ksum", [P, B])
        krec = tile(gd, "krec", [P, B])
        qeps = tile(gd, "qeps", [P, B])
        cpos = tile(gd, "cpos", [P, B, HH])
        cneg = tile(gd, "cneg", [P, B, HH])
        knorm = tile(gd, "knorm", [P, B])
        nt = tile(gd, "nt", [P, 3, UN])
        osc = tile(gd, "osc", [P, B, HH])
        gd.close()

        bk = ExitStack()
        FREE_WORDS = 2 * TG + NG * 2 * TG + UG * P + 2 * 4 * P + DC * 2 * P
        tile(bk, "unused_from_wv", [P, 4 * HH * D - B - B - DC * TG - 2 * D])
        idx_f = tile(bk, "idx_f", [P, B])
        pick = tile(bk, "pick", [P, B])
        x1g = tile(bk, "x1g", [P, G, D])
        yT = tile(bk, "yT", [P, DC, TG])
        dn = tile(bk, "dn", [P, 2, D])
        qg_s = tile(bk, "qg_s", [P, DC * I3])
        qu_s = tile(bk, "qu_s", [P, DC * I3])
        qm = tile(bk, "qm", [P, DC * I3])
        qdif = tile(bk, "qdif", [P, DC * I3])
        q8a = tile(bk, "q8a", [P, DC * I3], FP8)
        q8b = tile(bk, "q8b", [P, DC * I3], FP8)
        dsc = tile(bk, "dsc", [P, D])
        idx_i = tile(bk, "idx_i", [P, B], I32)
        gsc = tile(bk, "gsc", [P, I3 // P])
        usc = tile(bk, "usc", [P, I3 // P])
        tile(bk, "unused_up_to_Bm", [P, FREE_WORDS - 4 * DC * I3 - DC * I3 // 2 - D - B - 2 * 8])
        wg_s = tile(bk, "wg_s", [P, DC, I2])
        wu_s = tile(bk, "wu_s", [P, DC, I2])
        wd_s = tile(bk, "wd_s", [P, I2 // P, D])
        ag_s = tile(bk, "ag_s", [P, DC, N_AD, RK])
        au_s = tile(bk, "au_s", [P, DC, N_AD, RK])
        ad_s = tile(bk, "ad_s", [P, I2 // P, N_AD, RK])
        bg_s = tile(bk, "bg_s", [P, I2])
        bu_s = tile(bk, "bu_s", [P, I2])
        bd_s = tile(bk, "bd_s", [P, D])
        qd_s = tile(bk, "qd_s", [P, I3 // P * D])
        x1T = tile(bk, "x1T", [P, DC, TG])
        lg = tile(bk, "lg", [P, 3, TG])
        sg = tile(bk, "sg", [P, 2, TG])
        hT = tile(bk, "hT", [P, I2 // P, TG])
        yh = tile(bk, "yh", [P, DC, TG], F32R)
        yl = tile(bk, "yl", [P, DC, TG], F32R)
        fT = qdif[:, 0:2 * TG].rearrange("p (a t) -> p a t", a=2)
        fh = tile(bk, "fh", [P, I3 // P, TG], F32R)
        fl = tile(bk, "fl", [P, I3 // P, TG], F32R)
        qg_r = tile(bk, "qg_r", [P, DC * I3], F32R)
        qu_r = tile(bk, "qu_r", [P, DC * I3], F32R)
        qd_r = tile(bk, "qd_r", [P, I3 // P * D], F32R)
        og = qm[:, 0:G * D].rearrange("p (b d) -> p b d", b=G)
        bk.close()

        dram_w = {0: Wq, 1: Wk, 2: Wv, 3: Wo}

        a_win = sem("a_win")
        a_small_in = sem("a_small_in")
        a_xg_in = Signal(sem("a_xg_in"), 16)
        a_wt_ready = sem("a_wt_ready")
        a_wt_read = sem("a_wt_read")
        a_prec = sem("a_prec")
        a_x_ready, a_x_read = sig("a_x_ready", 2), sig("a_x_read", 2)
        a_q_ready, a_q_read = sig("a_q_ready", 2), sig("a_q_read", 2)
        a_k_ready, a_k_read = sig("a_k_ready", 2), sig("a_k_read", 4)
        a_v_ready, a_v_read = sig("a_v_ready", 2), sig("a_v_read", 2)
        a_s_ready, a_max, a_nmax = sig("a_s_ready", 16), sig("a_max", 16), sig("a_nmax", 16)
        a_prob = sig("a_prob", 16)
        a_pt_ready, a_pt_read = sig("a_pt_ready", 16), sig("a_pt_read", 16)
        a_pv_ready = sig("a_pv_ready", 16)
        a_rinv, a_o_read = sig("a_rinv", G), sig("a_o_read", G)
        a_ot_ready, a_ot_read = sig("a_ot_ready", 2), sig("a_ot_read", 2)
        a_c_ready, a_c_read = sig("a_c_ready", 2), sig("a_c_read", 2)
        a_xT = sig("a_xT", 1)
        a_ba_ready, a_ba_read = sig("a_ba_ready", G), sig("a_ba_read", G)
        gates, gates_act, picked = sem("gates"), sem("gates_act"), sem("picked")

        d_nw_in = sem("d_nw_in")
        d_cwq_in, d_cwv_in = Signal(sem("d_cwq_in"), 32), Signal(sem("d_cwv_in"), 16)
        d_qk_in = Signal(sem("d_qk_in"), 32)
        d_v_in, d_z_in, d_o_in = (Signal(sem(n), 16) for n in ("d_v_in", "d_z_in", "d_o_in"))
        d_wo = sig("d_wo", 1)
        d_qk_ready, d_v_ready, d_z_ready = sig("d_qk_ready", 8), sig("d_v_ready", 8), sig("d_z_ready", 8)
        d_tap_q, d_conv_q, d_step_q, d_silu_q = sig("d_tap_q", 8), sig("d_conv_q", 8), sig("d_step_q", 16), sig("d_silu_q", 8)
        d_tap_v, d_conv_v, d_step_v, d_silu_v = sig("d_tap_v", 8), sig("d_conv_v", 8), sig("d_step_v", 16), sig("d_silu_v", 8)
        d_zg = sig("d_zg", 8)
        d_sq, d_ss_ready, d_ss_read = sig("d_sq", NG), sig("d_ss_ready", NG), sig("d_ss_read", 1)
        d_rec, d_c1, d_c, d_cneg = (sig(n, 1) for n in ("d_rec", "d_c1", "d_c", "d_cneg"))
        d_V = sig("d_V", 8)
        d_gk_ready, d_ea_ready, d_E, d_B = (sig(n, 8) for n in ("d_gk_ready", "d_ea_ready", "d_E", "d_B"))
        d_diag = sig("d_diag", NG)
        d_lanes, d_solve, d_unlane = sig("d_lanes", 3), sig("d_solve", 2 * (BK - 1)), sig("d_unlane", 2)
        d_newt, d_knorm = sig("d_newt", 11), sig("d_knorm", 1)
        d_spread_l, d_spread_u = sig("d_spread_l", 4), sig("d_spread_u", 4)
        d_y1_ready, d_y1_read, d_t1_ready, d_t1_read = (sig(n, 4) for n in
                                                        ("d_y1_ready", "d_y1_read", "d_t1_ready", "d_t1_read"))
        d_y2_ready, d_y2_read, d_u2_ready, d_u2_read = (sig(n, NG) for n in
                                                        ("d_y2_ready", "d_y2_read", "d_u2_ready", "d_u2_read"))
        d_vt_ready, d_w = sig("d_vt_ready", 8), sig("d_w", 8)
        d_u_ready, d_up, d_o_ready, d_sqo, d_go = (sig(n, 8) for n in ("d_u_ready", "d_up", "d_o_ready", "d_sqo", "d_go"))
        d_so_ready, d_so_read, d_nto, d_osc = sig("d_so_ready", 8), sig("d_so_read", NG), sig("d_nto", 11 * NG), sig("d_osc", NG)
        d_y_ready, d_acc_step, d_acc = sig("d_y_ready", B), sig("d_acc_step", B), sig("d_acc", B)
        zeroed = sem("zeroed")

        m_q_in, m_w_in, m_qr = sem("m_q_in"), sem("m_w_in"), sem("m_qr")
        m_yh, m_yl, m_fh, m_fl = sig("m_yh", DC), sig("m_yl", DC), sig("m_fh", 6), sig("m_fl", 6)
        m_q = sem("m_q")
        m_pick = sem("m_pick")
        m_x1, m_x1T_ready, m_x1T = sig("m_x1", 1), sig("m_x1T_ready", 2), sig("m_x1T", 2)
        m_lg_ready, m_lg = sig("m_lg_ready", 2), sig("m_lg", 2)
        m_gu_ready, m_sg, m_h = sig("m_gu_ready", 16), sig("m_sg", 8), sig("m_h", 8)
        m_ld_ready, m_ld = sig("m_ld_ready", 2), sig("m_ld", 2)
        m_y_ready, m_y = sig("m_y_ready", 2), sig("m_y", 2)
        m_fgu_ready, m_fs, m_f = sig("m_fgu_ready", 12), sig("m_fs", 6), sig("m_f", 6)
        m_d_ready, m_dn, m_og = sig("m_d_ready", 4), sig("m_dn", 4), sig("m_og", 4)
        m_out = Signal(sem("m_out"), 16)

        PE_ORDER = [("ea", 0), ("gk", 0), ("ea", 1), ("gk", 1), ("ea", 2), ("gk", 2), ("ea", 3), ("gk", 3),
                    ("z", 0), ("v", 0), ("z", 1), ("next", 0), ("v", 1), ("vt", 0), ("next", 1), ("ss", 0),
                    ("z", 2), ("v", 2), ("vt", 1), ("next", 2), ("ss", 1), ("z", 3), ("v", 3), ("vt", 2), ("y1", 0), ("y1", 1), ("next", 3),
                    ("t1", 0), ("t1", 1), ("vt", 3), ("ss", 2), ("y2", 0), ("y2", 1), ("u2", 0), ("y2", 2), ("u2", 1),
                    ("u", 0), ("y2", 3), ("ss", 3), ("u2", 2), ("o", 0), ("u", 1), ("u2", 3), ("so", 0), ("o", 1), ("u", 2), ("y", 0),
                    ("so", 1), ("o", 2), ("u", 3), ("y", 1), ("so", 2), ("o", 3), ("y", 2), ("so", 3), ("y", 3)]
        CONV = [(kind, g, t) for kind, g in PE_ORDER if kind in ("v", "next") for t in range(2)]
        conv_slot = {c: n % 4 for n, c in enumerate(CONV)}

        proj_uses, work_uses, small_uses = [], [], []
        for kind, g in PE_ORDER:
            if kind == "next":
                proj_uses += [((kind, g, t), d_conv_q, 8 + 2 * g + t + 1) for t in range(2)]
            elif kind == "v":
                proj_uses += [((kind, g, t), d_conv_v, 2 * g + t + 1) for t in range(2)]
            elif kind == "z":
                proj_uses += [((kind, g, t), d_zg, 2 * g + t + 1) for t in range(2)]
            elif kind == "ss" and g == 0:
                small_uses += [(("ss", 0), d_ss_read, 2)]
            elif kind == "gk":
                work_uses += [(("gk", g, h), d_B, 2 * g + h + 1) for h in range(2)]
            elif kind == "ea":
                proj_uses += [(("ea", g, h), d_E, 2 * g + h + 1) for h in range(2)]
            elif kind == "vt":
                work_uses += [((kind, g, h), d_w, 2 * g + h + 1) for h in range(2)]
            elif kind in ("y1", "t1"):
                work_uses += [((kind, g, p), d_y1_read if kind == "y1" else d_t1_read, 2 * g + p + 1) for p in range(2)]
            elif kind in ("y2", "u2"):
                work_uses += [((kind, g), d_y2_read if kind == "y2" else d_u2_read, g + 1)]
            elif kind in ("u", "o"):
                work_uses += [((kind, g, h), d_up if kind == "u" else d_go, 2 * g + h + 1) for h in range(2)]
            elif kind == "so":
                small_uses += [(("so", g), d_so_read, g + 1)]
            elif kind == "y":
                (work_uses if g == NG - 1 else proj_uses).extend( [((kind, g, b), d_acc, G * g + b + 1) for b in range(G)])
        proj_uses += [(("pad", n), d_acc, B) for n in range(-len(proj_uses) % 3)]
        ahead = Banks(ps[0:3], [((g, t), d_conv_q, 2 * g + t + 1) for g in range(NG) for t in range(2)] + [(None, d_conv_q, 8)])
        proj = Banks(ps[0:3], proj_uses)
        work = Banks(ps[3:7], work_uses)
        ring_y = lambda g: work if g == NG - 1 else proj
        sums, small = Banks(ps[7:8], small_uses), ps[7]
        front = Banks(ps[0:4], [(("x", n), a_x_read, 2) for n in range(2)] + [(("q", n), a_q_read, n + 1) for n in range(2)]
                      + [(("k", n), a_k_read, 2 * n + 2) for n in range(2)] + [(("v", n), a_v_read, n + 1) for n in range(2)]
                      + [(("pv", b), a_o_read, b + 1) for b in range(G)] + [(("ot", n), a_ot_read, n + 1) for n in range(2)]
                      + [(("c", n), a_c_read, n + 1) for n in range(2)] + [(("ba", b), a_ba_read, b + 1) for b in range(G)])
        score = Banks(ps[4:6], [(n, a_prob, n + 1) for n in range(4 * G)])
        turned = Banks(ps[6:8], [(n, a_pt_read, n + 1) for n in range(4 * G)])
        pairs = []
        for c in range(I2 // P):
            pairs += [(("g", c), m_sg, c + 1), (("u", c), m_h, c + 1)]
        for c in range(I3 // P):
            pairs += [(("fg", c), m_fs, c + 1), (("fu", c), m_f, c + 1)]
        pairs = Banks(ps[0:4], pairs)
        rest = Banks(ps[4:8], [(("ld", n), m_ld, n + 1) for n in range(2)] + [(("y", n), m_y, n + 1) for n in range(2)]
                     + [(("x", n), m_x1T, 2 + n + 1) for n in range(2)] + [(("lg", n), m_lg, 2 + n + 1) for n in range(2)]
                     + [(("d", b), m_dn, b + 1) for b in range(G)])
        SK, SQ, SO = 0, B, 2 * B

        block = top.enter_context(nc.Block())
        CONSTS = 17
        GATE_STEPS = 9
        Q_LOADS, W_LOADS = 16 * 6, 16 * (7 + 2 * DC + I2 // P)

        @block.sync
        def _(sp_):
            for n in range(4):
                sp_.dma_start(w_raw[:, n, :, :], dram_w[n].rearrange("(c p) d -> p c d", p=P)).then_inc(a_win, 16)

            def load_xg(g):
                a_x_ready.wait(sp_, g, 0)
                sp_.dma_start(xg[:], x[bass.ds(g * G, G), :, :].rearrange("b t d -> t b d")).then_inc(a_xg_in.sem, 16)

            for t, v in ((dtb, dt_bias), (alog, A_log)):
                sp_.dma_start(t[:], v.rearrange("(a n) -> a n", a=1).broadcast_to([P, NV])).then_inc(a_small_in, 16)
            sp_.dma_start(precb[:], prec.rearrange("b a -> a b").broadcast_to([P, B])).then_inc(a_small_in, 16)
            for n, v in enumerate((W_b, W_a)):
                sp_.dma_start(w_ba[:, :, n, :], v.rearrange("(c p) n -> p c n", p=P)).then_inc(a_small_in, 16)
            first_then_loop(sp_, NG, load_xg)
            for g in range(NG):
                sp_.dma_start(acc[:, G * g:G * g + G, :], x[G * g:G * g + G, :, :].rearrange("b t d -> t b d")).then_inc(x_in, 16)

            sp_.wait_ge(gates, GATE_STEPS)
            taps = conv_w.rearrange("(n p) j -> p n j", p=P)
            sp_.dma_start(nw[:], norm_w.rearrange("(p a) -> p a", a=1)).then_inc(d_nw_in, 16)
            qkv = W_qkv.rearrange("(c p) n -> p c n", p=P)
            zz = W_z.rearrange("(c p) n -> p c n", p=P)

            def load_qk(head, step):
                of_k, of_q = qkv[:, :, bass.ds(head * DK + NK * DK, DK)], qkv[:, :, bass.ds(head * DK, DK)]
                d_qk_ready.wait(sp_, step, 8)
                sp_.dma_start(wqk[:, :, 0, :], of_k).then_inc(d_qk_in.sem, 16)
                sp_.dma_start(wqk[:, :, 1, :], of_q).then_inc(d_qk_in.sem, 16)
                d_conv_q.wait(sp_, step, 8)
                for t, first in ((0, head + NK), (1, head + 0)):
                    sp_.dma_start(cwq[:, t:t + 1, :], taps[:, bass.ds(first, 1), :]).then_inc(d_cwq_in.sem, 16)

            load_qk(0, -1)

            def load_head(kh, last):
                d_v_ready.wait(sp_, kh, 0)
                d_z_ready.wait(sp_, kh, 0)
                sp_.dma_start(wv[:], qkv[:, :, bass.ds(kh * HH * DV + 2 * NK * DK, HH * DV)]).then_inc(d_v_in.sem, 16)
                sp_.dma_start(wz[:], zz[:, :, bass.ds(kh * HH * DV, HH * DV)]).then_inc(d_z_in.sem, 16)
                d_conv_v.wait(sp_, kh, 0)
                sp_.dma_start(cwv[:], taps[:, bass.ds(kh * HH + 2 * NK, HH), :]).then_inc(d_cwv_in.sem, 16)
                if not last:
                    load_qk(kh + 1, kh)
                d_wo.wait(sp_, kh, 0)
                sp_.dma_start(wo_in[:], W_out.rearrange("(h p) f -> p h f", p=P)[:, bass.ds(kh * HH, HH), :]).then_inc(d_o_in.sem, 16)

            loop_then_last(sp_, NK, load_head)

            assert all(conv_slot["v", g, t] < 2 for g in range(NG) for t in range(2))
            for reader, n in ((d_B, 8), (d_ea_ready, 8), (d_qk_ready, 8), (d_silu_q, 8)):
                reader.wait(sp_, NK - 1, n)
            sp_.dma_start(qg_s[:].rearrange("p (c n) -> p c n", c=DC), gate_w.rearrange("(c p) n -> p c n", p=P)).then_inc(m_q_in, 16)
            sp_.dma_start(qu_s[:].rearrange("p (c n) -> p c n", c=DC), up_w.rearrange("(c p) n -> p c n", p=P)).then_inc(m_q_in, 16)
            sp_.dma_start(dsc[:], down_s.rearrange("(a n) -> a n", a=1).broadcast_to([P, D])).then_inc(m_q_in, 16)
            sp_.dma_start(idx_i[:], adapter.rearrange("(a n) -> a n", a=1).broadcast_to([P, B])).then_inc(m_q_in, 16)
            with nc.allow_non_contiguous_dma("scales by channel, once"):
                sp_.dma_start(gsc[:], gate_s.rearrange("(c p) -> p c", p=P)).then_inc(m_q_in, 16)
                sp_.dma_start(usc[:], up_s.rearrange("(c p) -> p c", p=P)).then_inc(m_q_in, 16)
            d_u2_ready.wait(sp_, NK - 1, NG)
            for c in range(DC):
                sp_.dma_start(ag_s[:, c], Ag[:, c * P:(c + 1) * P, :].rearrange("n p r -> p n r")).then_inc(m_w_in, 16)
                sp_.dma_start(au_s[:, c], Au[:, c * P:(c + 1) * P, :].rearrange("n p r -> p n r")).then_inc(m_w_in, 16)
            for dst, src in (
                (wg_s[:], Wg.rearrange("(c p) n -> p c n", p=P)), (wu_s[:], Wu.rearrange("(c p) n -> p c n", p=P)),
                (bg_s[:], Bg.rearrange("n r i -> (n r) i")), (bu_s[:], Bu.rearrange("n r i -> (n r) i")),
                (wd_s[:], Wd.rearrange("(c p) n -> p c n", p=P)), (bd_s[:], Bd.rearrange("n r i -> (n r) i")),
                (qd_s[:].rearrange("p (c n) -> p c n", c=I3 // P), down_w.rearrange("(c p) n -> p c n", p=P)),
            ):
                sp_.dma_start(dst, src).then_inc(m_w_in, 16)
            for c in range(I2 // P):
                sp_.dma_start(ad_s[:, c], Ad[:, c * P:(c + 1) * P, :].rearrange("n p r -> p n r")).then_inc(m_w_in, 16)

            def store(g):
                m_og.wait(sp_, g, 4)
                sp_.dma_start(out[bass.ds(g * G, G), :, :].rearrange("b t d -> t b d"), og).then_inc(m_out.sem, 16)

            first_then_loop(sp_, NG, store)
            m_out.wait(sp_, NG, 0)



        @block.gpsimd
        def _(pool):
            for t, v in ((ident, 0.0), (later_t, 1.0), (upto_t, 1.0), (cm_qk, 0.0), (cm_kq, 0.0), (identb, 0.0),
                         (ones, 1.0)):
                pool.memset(t[:], v).then_inc(consts, 1)
            pool.iota(part[:, 0:1], pattern=[[0, 1]], base=0, channel_multiplier=1).then_inc(consts, 1)
            pool.wait_ge(consts, 8)
            for t in (ident, identb):
                pool.affine_select(out=t[:], in_=t[:], compare_op=ALU.not_equal, fill=1.0, base=0,
                                   pattern=[[-1, P]], channel_multiplier=1).then_inc(consts, 1)
            for t, op, fill, sign in ((later_t, ALU.is_gt, 0.0, 1), (upto_t, ALU.is_ge, 0.0, -1),
                                      (cm_qk, ALU.is_ge, -BIG, 1), (cm_kq, ALU.is_ge, -BIG, -1)):
                pool.affine_select(out=t[:], in_=t[:], compare_op=op, fill=fill, base=0,
                                   pattern=[[-sign, P]], channel_multiplier=sign).then_inc(consts, 1)

            def keep_group(g):
                a_c_read.wait(pool, g, 2)
                pool.tensor_copy(xT[:, :, bass.ds(g * TG, TG)], cTg[:]).then_inc(a_xT.sem, 1)

            first_then_loop(pool, NG, keep_group)

            pool.wait_ge(gates, GATE_STEPS)
            a_xT.wait(pool, NG, 0)
            pool.memset(Ue[:], 0.0).then_inc(zeroed, 1)
            pool.memset(Le[:], 0.0).then_inc(zeroed, 1)

            def decay_terms(step, n, ahead):
                g, h = n // 2, n % 2
                d_ea_ready.wait(pool, step, n + ahead * 8 - 1)
                pool.tensor_tensor(V[:, 4 * h:4 * h + 4, :], upto_t[:].rearrange("p (a i) -> p a i", a=1).broadcast_to([P, 4, P]),
                                   gdec[:, bass.ds(step + ahead, 1), G * g + 2 * h:G * g + 2 * h + 2, :].rearrange("p a b (h i) -> p (a b h) i", i=1)
                                   .broadcast_to([P, 4, P]), ALU.mult).then_inc(d_V.sem, 1)

            decay_terms(0, 0, 0)
            decay_terms(0, 1, 0)

            def head(kh, last):
                for n in range(2, 8):
                    decay_terms(kh, n, 0)
                d_o_in.wait(pool, kh, 16)
                d_y_ready.wait(pool, kh, 0)
                pool.tensor_tensor(wo[:], wo_in[:], nw[:].rearrange("p (a b) -> p a b", a=1).broadcast_to([P, HH, D]), ALU.mult
                                   ).then_inc(d_wo.sem, 1)
                d_lanes.wait(pool, kh, 3)
                lane_A = diag_u
                for j in range(BK - 1):
                    h, w = BK - 1 - j, j + 1
                    rows = lane_T[:, j + 1:BK, 0:w]
                    prod = lane_p[:, 0:h * w].rearrange("p (i k) -> p i k", k=w)
                    d_solve.wait(pool, kh, 2 * j)
                    pool.tensor_tensor(prod, lane_A[:, j + 1:BK, j:j + 1].broadcast_to([P, h, w]),
                                       lane_T[:, j:j + 1, 0:w].broadcast_to([P, h, w]), ALU.mult).then_inc(d_solve.sem, 1)
                    d_solve.wait(pool, kh, 1 + 2 * j)
                    pool.tensor_tensor(rows, rows, prod, ALU.add).then_inc(d_solve.sem, 1)
                if not last:
                    decay_terms(kh, 0, 1)
                    decay_terms(kh, 1, 1)

            pool.wait_ge(d_nw_in, 16)
            loop_then_last(pool, NK, head)

            d_acc.wait(pool, NK, 0)

            def take_group(g):
                m_x1T_ready.wait(pool, g, 0)
                pool.tensor_copy(x1g[:], acc[:, bass.ds(g * G, G), :]).then_inc(m_x1.sem, 1)

            first_then_loop(pool, NG, take_group)

        @block.tensor
        def _(pe):
            def mm(out_, lhsT, rhs, start, stop):
                return pe.matmul(out_, lhsT, rhs, start=start, stop=stop)

            pe.wait_ge(consts, CONSTS)
            pe.wait_ge(a_win, 64)
            for n in range(4):
                for e in range(2):
                    for d in range(2):
                        i = pe.transpose(ps[n][:, (2 * d + e) * P:(2 * d + e + 1) * P], w_raw[:, n, e, d * P:(d + 1) * P], ident[:])
                i.then_inc(a_wt_ready, 1)
            pe.wait_ge(a_wt_read, 4)
            pe.wait_ge(a_small_in, 80)

            def attend(g):
                a_xg_in.wait(pe, g, 16)
                for c in range(DC):
                    front.wait_free(pe, g, ("x", c))
                    for b in range(G):
                        i = pe.transpose(front.bank(("x", c))[:, b * P:(b + 1) * P], xg[:, b, c * P:(c + 1) * P], ident[:])
                    i.then_inc(a_x_ready.sem, 1)
                a_x_read.wait(pe, g, 2)
                for n, (name, ready) in enumerate((("q", a_q_ready), ("k", a_k_ready))):
                    for e in range(2):
                        front.wait_free(pe, g, (name, e))
                        for c in range(DC):
                            i = mm(front.bank((name, e))[:], w_t[:, n, c, e * P:(e + 1) * P], xgT[:, c, :], c == 0, c == DC - 1)
                        i.then_inc(ready.sem, 1)
                for m in range(2):
                    front.wait_free(pe, g, ("v", m))
                    for b in range(2):
                        for c in range(DC):
                            i = mm(front.bank(("v", m))[:, b * D:(b + 1) * D], xgT[:, c, (2 * m + b) * S:(2 * m + b + 1) * S],
                                   w_t[:, 2, c, :], c == 0, c == DC - 1)
                    i.then_inc(a_v_ready.sem, 1)
                a_q_read.wait(pe, g, 2)
                a_k_read.wait(pe, g, 4)
                a_v_read.wait(pe, g, 2)

                def scores(n):
                    b, j = n // 4, n % 4
                    score.wait_free(pe, g, n)
                    pe.matmul(score.bank(n)[:], identb[:], cm_qk[:].rearrange("p (a k) -> p a k", a=1).broadcast_to([P, 4, P]),
                              start=True, stop=False)
                    for s in range(4):
                        e, kt = s // 2, (kTe, kTo)[s % 2]
                        rows = slice(32 * j, 32 * j + 32)
                        i = mm(score.bank(n)[:, s * P:(s + 1) * P], qTa[rows, e, b * S:(b + 1) * S], kt[rows, e, b * S:(b + 1) * S],
                               False, s == 3)
                    i.then_inc(a_s_ready.sem, 1)

                def turn(n):
                    a_prob.wait(pe, g, n + 1)
                    turned.wait_free(pe, g, n)
                    for s in range(4):
                        i = pe.transpose(turned.bank(n)[:, s * P:(s + 1) * P], prob[:, n % 2, s, :], ident[:])
                    i.then_inc(a_pt_ready.sem, 1)

                def values(n):
                    b, j = n // 4, n % 4
                    a_pt_read.wait(pe, g, n + 1)
                    if j == 0:
                        front.wait_free(pe, g, ("pv", b))
                    for s in range(4):
                        h = 8 * (s // 2) + 2 * j + s % 2
                        i = mm(front.bank(("pv", b))[:, h * HD_A:(h + 1) * HD_A], probT[:, n % 2, s, :],
                               vg[:, b, h * HD_A:(h + 1) * HD_A], True, True)
                    i.then_inc(a_pv_ready.sem, 1)

                scores(0)
                scores(1)
                for n in range(4 * G + 1):
                    if n < 4 * G:
                        turn(n)
                    if n + 2 < 4 * G:
                        scores(n + 2)
                    if n >= 1:
                        values(n - 1)
                a_o_read.wait(pe, g, G)
                for e in range(2):
                    front.wait_free(pe, g, ("ot", e))
                    for b in range(G):
                        i = pe.transpose(front.bank(("ot", e))[:, b * P:(b + 1) * P], oa[:, b, e * P:(e + 1) * P], ident[:])
                    i.then_inc(a_ot_ready.sem, 1)
                a_ot_read.wait(pe, g, 2)
                for f in range(DC):
                    front.wait_free(pe, g, ("c", f))
                    for e in range(2):
                        i = mm(front.bank(("c", f))[:], w_t[:, 3, e, f * P:(f + 1) * P], oTg[:, e, :], e == 0, e == 1)
                    i.then_inc(a_c_ready.sem, 1)
                a_c_read.wait(pe, g, 2)
                for b in range(G):
                    front.wait_free(pe, g, ("ba", b))
                    for c in range(DC):
                        i = mm(front.bank(("ba", b))[:, 0:2 * NV], cTg[:, c, b * S:(b + 1) * S],
                               w_ba[:, c, :, :].rearrange("p a n -> p (a n)"), c == 0, c == DC - 1)
                    i.then_inc(a_ba_ready.sem, 1)

            first_then_loop(pe, NG, attend)

            pe.wait_ge(gates, GATE_STEPS)
            a_xT.wait(pe, NG, 0)
            pe.wait_ge(zeroed, 2)

            def project_qk(step, g, banks, key):
                d_qk_in.wait(pe, step, 64)
                for t in range(2):
                    banks.wait_free(pe, 0 if banks is ahead else step, key(t))
                    for c in range(DC):
                        i = mm(banks.bank(key(t))[:], wqk[:, c, t, :], xT[:, c, g * TG:(g + 1) * TG], c == 0, c == DC - 1)
                    i.then_inc(d_qk_ready.sem, 1)

            def sums_of_squares(step, g):
                d_sq.wait(pe, step, NG + g + 1)
                for t, col in enumerate((SK, SQ)):
                    for b in range(G):
                        i = mm(small[:, col + G * g + b:col + G * g + b + 1], sqb[g % 2][:, t, b * S:(b + 1) * S], ones[:], True, True)
                i.then_inc(d_ss_ready.sem, 1)

            for g in range(NG):
                project_qk(-1, g, ahead, lambda t: (g, t))
            for g in range(NG):
                sums_of_squares(-1, g)
            d_conv_q.wait(pe, 0, 8)

            def head(kh, last):
                def project(kind, g, loaded, weights, ready):
                    loaded.wait(pe, kh, 16)
                    for t in range(2):
                        proj.wait_free(pe, kh, (kind, g, t), ("next",) if last else ())
                        for c in range(DC):
                            i = mm(proj.bank((kind, g, t))[:], weights[:, c, t * DV:(t + 1) * DV], xT[:, c, g * TG:(g + 1) * TG], c == 0, c == DC - 1)
                        i.then_inc(ready.sem, 1)

                def products(g):
                    d_silu_q.wait(pe, kh, 2 * g + 2)
                    for h in range(2):
                        work.wait_free(pe, kh, ("gk", g, h))
                        for b in range(2):
                            t0 = (2 * h + b) * S
                            i = mm(work.bank(("gk", g, h))[:, b * 2 * P:(b + 1) * 2 * P], kq[:, g, 0, t0:t0 + S],
                                   kq[:, g, :, t0:t0 + S], True, True)
                        i.then_inc(d_gk_ready.sem, 1)

                def log_decays(g):
                    for h in range(2):
                        d_V.wait(pe, kh, 2 * g + h + 1)
                        proj.wait_free(pe, kh, ("ea", g, h))
                        mm(proj.bank(("ea", g, h))[:], later_t[:], V[:, 4 * h:4 * h + 4, :], True, False)
                        mm(proj.bank(("ea", g, h))[:], identb[:],
                           cm_kq[:].rearrange("p (a k) -> p a k", a=1).broadcast_to([P, 4, P]), False, True).then_inc(d_ea_ready.sem, 1)

                def sums_of_next(g):
                    if g == 0:
                        sums.wait_free(pe, kh, ("ss", 0))
                    sums_of_squares(kh, g)

                def turn_v(g):
                    d_silu_v.wait(pe, kh, 2 * g + 2)
                    for h in range(2):
                        work.wait_free(pe, kh, ("vt", g, h))
                        for b in range(2):
                            for hh in range(HH):
                                i = pe.transpose(work.bank(("vt", g, h))[:, (2 * b + hh) * P:(2 * b + hh + 1) * P],
                                                 vT[:, hh, (2 * h + b) * S:(2 * h + b + 1) * S], ident[:])
                        i.then_inc(d_vt_ready.sem, 1)

                def first_of_32(f):
                    for p in range(2):
                        lo, hi, both = slice(64 * p, 64 * p + BK), slice(64 * p + BK, 64 * p + 2 * BK), slice(64 * p, 64 * p + 2 * BK)
                        d_unlane.wait(pe, kh, 2)
                        work.wait_free(pe, kh, ("y1", f, p))
                        bank = work.bank(("y1", f, p))
                        for n in range(16):
                            u = 16 * f + n
                            rows = both if n == 0 else hi
                            i = mm(bank[rows, n * BK:(n + 1) * BK], Bm[lo, u, rows], diag_l[lo, u, :], True, True)
                        i.then_inc(d_y1_ready.sem, 1)

                def second_of_32(f):
                    for p in range(2):
                        lo, hi = slice(64 * p, 64 * p + BK), slice(64 * p + BK, 64 * p + 2 * BK)
                        d_y1_read.wait(pe, kh, 2 * f + p + 1)
                        work.wait_free(pe, kh, ("t1", f, p))
                        bank = work.bank(("t1", f, p))
                        for n in range(16):
                            u = 16 * f + n
                            rows, units = (slice(64 * p, 64 * p + 2 * BK), slice(u, u + 2)) if n == 0 else (lo, slice(u, u + 1))
                            mm(bank[rows, n * BK:(n + 1) * BK], Y1[hi, units, :].rearrange("p a b -> p (a b)"), diag_u[hi, u, :], True, True)
                            i = mm(bank[hi, n * BK:(n + 1) * BK], diag_u[hi, u, :], Y1[hi, u, :], True, True)
                        i.then_inc(d_t1_ready.sem, 1)

                def first_of_64(g):
                    d_spread_l.wait(pe, kh, 4)
                    d_t1_read.wait(pe, kh, 2 * (g // 2) + 2)
                    work.wait_free(pe, kh, ("y2", g))
                    for n in range(UG):
                        u = UG * g + n
                        rows = slice(0 if n == 0 else 64, 128)
                        i = mm(work.bank(("y2", g))[rows, n * 64:(n + 1) * 64], Bm[0:64, u, rows], Le[0:64, u, :], True, True)
                    i.then_inc(d_y2_ready.sem, 1)

                def second_of_64(g):
                    d_spread_u.wait(pe, kh, 4)
                    d_y2_read.wait(pe, kh, g + 1)
                    work.wait_free(pe, kh, ("u2", g))
                    for n in range(UG):
                        u = UG * g + n
                        cols = slice(0, 2) if n == 0 else slice(n, n + 1)
                        i = mm(work.bank(("u2", g))[0:128 if n == 0 else 64, n * 64:(n + 1) * 64],
                               Y2[64:128, g % 2, cols, :].rearrange("p a b -> p (a b)"), Ue[64:128, u, 64:128], True, True)
                    i.then_inc(d_u2_ready.sem, 1)

                def inverse_times_v(g):
                    d_u2_read.wait(pe, kh, g + 1)
                    for h in range(2):
                        d_w.wait(pe, kh, 2 * g + h + 1)
                        work.wait_free(pe, kh, ("u", g, h))
                        for n in range(4):
                            u = UG * g + 4 * h + n
                            i = mm(work.bank(("u", g, h))[:, n * P:(n + 1) * P], Ue[:, u, :], w_tok[:, u, :], True, True)
                        i.then_inc(d_u_ready.sem, 1)

                def attention(g):
                    for h in range(2):
                        d_up.wait(pe, kh, 2 * g + h + 1)
                        work.wait_free(pe, kh, ("o", g, h))
                        for n in range(4):
                            u = UG * g + 4 * h + n
                            i = mm(work.bank(("o", g, h))[:, n * P:(n + 1) * P], up[:, h, n, :], att[:, u, :], True, True)
                        i.then_inc(d_o_ready.sem, 1)

                def squares_of_outputs(g):
                    sums.wait_free(pe, kh, ("so", g), ("ss",) if last else ())
                    for h in range(2):
                        d_sqo.wait(pe, kh, 2 * g + h + 1)
                        for n in range(4):
                            u = UG * g + 4 * h + n
                            i = mm(small[:, SO + u:SO + u + 1], sqo[:, h, n, :], ones[:], True, True)
                        i.then_inc(d_so_ready.sem, 1)

                def project_out(g):
                    d_wo.wait(pe, kh, 1)
                    for b in range(G):
                        d_go.wait(pe, kh, 2 * g + b // 2 + 1)
                        ring_y(g).wait_free(pe, kh, ("y", g, b), ("next",) if last else ())
                        for hh in range(HH):
                            i = mm(ring_y(g).bank(("y", g, b))[:, hh * D:(hh + 1) * D], go[:, b // 2, 2 * (b % 2) + hh, :], wo[:, hh, :], True, True)
                        i.then_inc(d_y_ready.sem, 1)

                stage = {"ea": log_decays, "gk": products, "ss": sums_of_next, "vt": turn_v, "y1": first_of_32, "t1": second_of_32, "y2": first_of_64, "u2": second_of_64,
                         "u": inverse_times_v, "o": attention, "so": squares_of_outputs, "y": project_out,
                         "v": lambda g: project("v", g, d_v_in, wv, d_v_ready), "z": lambda g: project("z", g, d_z_in, wz, d_z_ready),
                         "next": lambda g: project_qk(kh, g, proj, lambda t: ("next", g, t))}
                for kind, g in PE_ORDER:
                    if not (last and kind in ("next", "ss")):
                        stage[kind](g)

            loop_then_last(pe, NK, head)

            d_acc.wait(pe, NK, 0)
            pe.wait_ge(m_w_in, W_LOADS)

            def enter(group, ring_step):
                m_x1.wait(pe, group, 1)
                for c in range(DC):
                    if ring_step is not None:
                        rest.wait_free(pe, ring_step, ("x", c))
                    for b in range(G):
                        i = pe.transpose(rest.bank(("x", c))[:, b * P:(b + 1) * P], x1g[:, b, c * P:(c + 1) * P], ident[:])
                    i.then_inc(m_x1T_ready.sem, 1)
                m_x1T.wait(pe, group, 2)
                for n, a in enumerate((ag_s, au_s)):
                    if ring_step is not None:
                        rest.wait_free(pe, ring_step, ("lg", n))
                    for c in range(DC):
                        i = mm(rest.bank(("lg", n))[:], a[:, c].rearrange("p n r -> p (n r)"), x1T[:, c, :], c == 0, c == DC - 1)
                    i.then_inc(m_lg_ready.sem, 1)

            enter(0, None)

            def mlps(g, last):
                for ct in range(I2 // P):
                    cols = slice(ct * P, (ct + 1) * P)
                    for n, (name, w, bb) in enumerate((("g", wg_s, bg_s), ("u", wu_s, bu_s))):
                        pairs.wait_free(pe, g, (name, ct))
                        for c in range(DC):
                            mm(pairs.bank((name, ct))[:], w[:, c, cols], x1T[:, c, :], c == 0, False)
                        if ct == 0:
                            m_lg.wait(pe, g, n + 1)
                        mm(pairs.bank((name, ct))[:], bb[:, cols], lg[:, n, :], False, True).then_inc(m_gu_ready.sem, 1)
                m_h.wait(pe, g, I2 // P)
                for n in range(2):
                    rest.wait_free(pe, g, ("ld", n))
                    for ct in range(I2 // P):
                        i = mm(rest.bank(("ld", n))[:, 0:256], ad_s[:, ct].rearrange("p n r -> p (n r)"),
                               hT[:, ct, n * 256:(n + 1) * 256], ct == 0, ct == I2 // P - 1)
                    i.then_inc(m_ld_ready.sem, 1)
                for e in range(DC):
                    rest.wait_free(pe, g, ("y", e))
                    for ct in range(I2 // P):
                        mm(rest.bank(("y", e))[:], wd_s[:, ct, e * P:(e + 1) * P], hT[:, ct, :], ct == 0, False)
                    m_ld.wait(pe, g, 2)
                    mm(rest.bank(("y", e))[:], bd_s[:, e * P:(e + 1) * P], lg[:, 2, :], False, True).then_inc(m_y_ready.sem, 1)
                if not last:
                    enter(g + 1, g)
                pe.wait_ge(m_qr, 2)
                m_yl.wait(pe, g, DC)
                for ft in range(I3 // P):
                    for name, w in (("fg", qg_r), ("fu", qu_r)):
                        pairs.wait_free(pe, g, (name, ft))
                        for c in range(DC):
                            for part in (yh, yl):
                                i = mm(pairs.bank((name, ft))[:], w[:, c * I3 + ft * P:c * I3 + (ft + 1) * P], part[:, c, :],
                                       c == 0 and part is yh, c == DC - 1 and part is yl)
                        i.then_inc(m_fgu_ready.sem, 1)
                pe.wait_ge(m_qr, 3)
                m_fl.wait(pe, g, I3 // P)
                for b in range(G):
                    rest.wait_free(pe, g, ("d", b), ("x", "lg") if last else ())
                    for ft in range(I3 // P):
                        for part in (fh, fl):
                            i = mm(rest.bank(("d", b))[:, 0:D], part[:, ft, b * S:(b + 1) * S], qd_r[:, ft * D:(ft + 1) * D],
                                   ft == 0 and part is fh, ft == I3 // P - 1 and part is fl)
                    i.then_inc(m_d_ready.sem, 1)

            loop_then_last(pe, NG, mlps)

        @block.scalar
        def _(act):
            def f(out_, in_, fn, **kw):
                return act.activation(out_, in_, fn, **kw)

            for n in range(4):
                act.wait_ge(a_wt_ready, n + 1)
                f(w_t[:, n].rearrange("p a b -> p (a b)"), ps[n][:], ACT.Copy).then_inc(a_wt_read, 1)

            def attend(g):
                a_x_ready.wait(act, g, 2)
                f(xgT[:, 1, :], front.bank(("x", 1))[:], ACT.Copy).then_inc(a_x_read.sem, 1)
                for m in range(2):
                    a_v_ready.wait(act, g, m + 1)
                    a_pv_ready.wait(act, g, 0)
                    f(vg[:, 2 * m:2 * m + 2, :].rearrange("p b d -> p (b d)"), front.bank(("v", m))[:], ACT.Copy).then_inc(a_v_read.sem, 1)
                for n in range(4 * G):
                    b, j = n // 4, n % 4
                    a_nmax.wait(act, g, n + 1)
                    a_pt_ready.wait(act, g, n - 1)
                    if j == 0:
                        a_rinv.wait(act, g, b - 1)
                    for s in range(4):
                        h = 8 * (s // 2) + 2 * j + s % 2
                        i = f(prob[:, n % 2, s, :], score.bank(n)[:, s * P:(s + 1) * P], ACT.Exp, bias=nmax[:, n % 2, s:s + 1],
                              accum_out=rsum[:, b % 2, h:h + 1])
                    i.then_inc(a_prob.sem, 1)
                for e in range(2):
                    a_ot_ready.wait(act, g, e + 1)
                    a_c_ready.wait(act, g, 0)
                    f(oTg[:, e, :], front.bank(("ot", e))[:], ACT.Copy).then_inc(a_ot_read.sem, 1)
                for e in range(2):
                    a_c_ready.wait(act, g, e + 1)
                    a_xT.wait(act, g, 0)
                    a_ba_ready.wait(act, g, 0)
                    f(cTg[:, e, :], front.bank(("c", e))[:], ACT.Copy).then_inc(a_c_read.sem, 1)

            first_then_loop(act, NG, attend)

            a_ba_read.wait(act, NG, 0)
            f(sp[0][:], ba[:, 0:NV, :], ACT.Tanh, scale=0.5).then_inc(gates_act, 1)
            f(nega[:], alog[:], ACT.Exp).then_inc(gates_act, 1)
            act.wait_ge(gates, 2)
            f(sp[3][:], sp[2][:], ACT.Exp, scale=-1.0).then_inc(gates_act, 1)
            act.wait_ge(gates_act, 3)
            f(sp[2][:], sp[3][:], ACT.Ln, bias=1.0).then_inc(gates_act, 1)

            act.wait_ge(gates, GATE_STEPS)

            def free_slot(step, conv, last):
                n = CONV.index(conv) - 4
                while last and n >= 0 and CONV[n][0] == "next":
                    n -= 4
                kind, g, t = CONV[n]
                done = 2 * g + t + 1 - (0 if n >= 0 else 8)
                if kind == "v":
                    d_silu_v.wait(act, step, done)
                else:
                    d_silu_q.wait(act, step, 8 + done)

            def tap_qk(step, g, banks, key):
                d_cwq_in.wait(act, step, 64)
                for t in range(2):
                    d_qk_ready.wait(act, step, 8 + 2 * g + t + 1)
                    if banks is proj:
                        free_slot(step, ("next", g, t), False)
                    else:
                        d_silu_q.wait(act, step, 8 + 2 * g + t + 1 - 4)
                    f(cbuf[:, conv_slot["next", g, t] if banks is proj else (2 * g + t) % 4, :], banks.bank(key(t))[:], ACT.Copy,
                      scale=cwq[:, t, KC - 1:KC]).then_inc(d_tap_q.sem, 1)

            def silu_qk(step, g, in_steps):
                if in_steps:
                    d_gk_ready.wait(act, step, 2 * g + 2)
                for t in range(2):
                    d_conv_q.wait(act, step, 8 + 2 * g + t + 1)
                    f(kq[:, g, t, :], cbuf[:, conv_slot["next", g, t] if in_steps else (2 * g + t) % 4, :], ACT.Silu).then_inc(d_silu_q.sem, 1)

            def squares(step, g, in_steps):
                d_silu_q.wait(act, step, 8 + 2 * g + 2)
                if g >= 2:
                    d_ss_ready.wait(act, step, NG + g - 1)
                elif in_steps:
                    (d_so_ready, d_y_ready)[g].wait(act, step, 0)
                f(sqb[g % 2], kq[:, g], ACT.Square).then_inc(d_sq.sem, 1)

            tap_qk(-1, 0, ahead, lambda t: (0, t))
            for g in range(NG):
                if g + 1 < NG:
                    tap_qk(-1, g + 1, ahead, lambda t: (g + 1, t))
                silu_qk(-1, g, False)
            for g in range(NG):
                squares(-1, g, False)

            def head(kh, last):
                def tap_v(g):
                    d_cwv_in.wait(act, kh, 16)
                    for t in range(2):
                        d_v_ready.wait(act, kh, 2 * g + t + 1)
                        free_slot(kh, ("v", g, t), last)
                        f(cbuf[:, conv_slot["v", g, t], :], proj.bank(("v", g, t))[:], ACT.Copy, scale=cwv[:, t, KC - 1:KC]).then_inc(d_tap_v.sem, 1)

                def silu_v(g):
                    d_vt_ready.wait(act, kh, 2 * g)
                    for t in range(2):
                        d_conv_v.wait(act, kh, 2 * g + t + 1)
                        f(vT[:, t, :], cbuf[:, conv_slot["v", g, t], :], ACT.Silu).then_inc(d_silu_v.sem, 1)

                def tap_next(g):
                    if not last:
                        tap_qk(kh, g, proj, lambda t: ("next", g, t))

                def silu_next(g):
                    if not last:
                        silu_qk(kh, g, True)

                def z_silu(g, ts=range(2)):
                    for t in ts:
                        d_z_ready.wait(act, kh, 2 * g + t + 1)
                        d_go.wait(act, kh, 2 * g + 2 - 8)
                        f(zg[:, t, g * TG:(g + 1) * TG], proj.bank(("z", g, t))[:], ACT.Silu).then_inc(d_zg.sem, 1)

                def squares_next(g):
                    if not last:
                        squares(kh, g, True)

                def decays(g):
                    for h in range(2):
                        d_ea_ready.wait(act, kh, 2 * g + h + 1)
                        d_B.wait(act, kh, 2 * g + h - 1)
                        f(E[:, h].rearrange("p u i -> p (u i)"), proj.bank(("ea", g, h))[:], ACT.Exp).then_inc(d_E.sem, 1)

                def diagonal(g):
                    d_B.wait(act, kh, 2 * g + 2)
                    d_spread_l.wait(act, kh, 0)
                    us = slice(UG * g, UG * g + UG)
                    for r in range(4):
                        rows = slice(BK * r, BK * r + BK)
                        i = f(diag_l[rows, us, :], Bm[rows, us, rows], ACT.Copy)
                    i.then_inc(d_diag.sem, 1)

                def keep_v(g):
                    d_knorm.wait(act, kh, 1)
                    d_u_ready.wait(act, kh, 2 * g + 2 - 8)
                    for h in range(2):
                        d_vt_ready.wait(act, kh, 2 * g + h + 1)
                        for b in range(2):
                            u = UG * g + 4 * h + 2 * b
                            s = G * g + 2 * h + b
                            i = f(w_tok[:, u:u + 2, :].rearrange("p u c -> p (u c)"), work.bank(("vt", g, h))[:, b * 2 * P:(b + 1) * 2 * P],
                                  ACT.Copy, scale=knorm[:, s:s + 1])
                        i.then_inc(d_w.sem, 1)

                def spread():
                    d_unlane.wait(act, kh, 2)
                    d_y2_ready.wait(act, kh, 0)
                    for r in range(4):
                        rows = slice(BK * r, BK * r + BK)
                        f(Le[rows, :, BK * (r % 2):BK * (r % 2) + BK], diag_l[rows], ACT.Copy).then_inc(d_spread_l.sem, 1)

                def read_y1(fh):
                    for p in range(2):
                        hi = slice(64 * p + BK, 64 * p + 2 * BK)
                        d_y1_ready.wait(act, kh, 2 * fh + p + 1)
                        d_t1_ready.wait(act, kh, 2 * fh + p + 1 - 4)
                        f(Y1[hi, 16 * fh:16 * fh + 16].rearrange("p u c -> p (u c)"), work.bank(("y1", fh, p))[hi, :], ACT.Copy).then_inc(d_y1_read.sem, 1)

                def read_y2(g):
                    d_y2_ready.wait(act, kh, g + 1)
                    d_u2_ready.wait(act, kh, g - 1)
                    f(Y2[64:128, g % 2].rearrange("p u c -> p (u c)"), work.bank(("y2", g))[64:128, :], ACT.Copy).then_inc(d_y2_read.sem, 1)

                def read_u2(g):
                    d_u2_ready.wait(act, kh, g + 1)
                    f(Ue[0:64, UG * g:UG * g + UG, 64:128],
                      work.bank(("u2", g))[0:64, :].rearrange("p (u c) -> p u c", c=64), ACT.Copy).then_inc(d_u2_read.sem, 1)

                def read_u(g):
                    for h in range(2):
                        d_u_ready.wait(act, kh, 2 * g + h + 1)
                        d_o_ready.wait(act, kh, 2 * g + h - 1)
                        for n in range(4):
                            b = G * g + 2 * h + n // 2
                            i = f(up[:, h, n, :], work.bank(("u", g, h))[:, n * P:(n + 1) * P], ACT.Copy, scale=cpos[:, b, n % 2:n % 2 + 1])
                        i.then_inc(d_up.sem, 1)

                def square_o(g):
                    for h in range(2):
                        d_o_ready.wait(act, kh, 2 * g + h + 1)
                        d_so_ready.wait(act, kh, 2 * g + h - 1)
                        f(sqo[:, h].rearrange("p u c -> p (u c)"), work.bank(("o", g, h))[:], ACT.Square).then_inc(d_sqo.sem, 1)

                decays(0)
                for g in range(NG):
                    if g + 1 < NG:
                        decays(g + 1)
                    else:
                        z_silu(0, (0,))
                    diagonal(g)
                z_silu(0, (1,)); tap_v(0); z_silu(1)
                tap_next(0); silu_v(0)
                tap_v(1); silu_next(0); keep_v(0); squares_next(0)
                tap_next(1); silu_v(1)
                z_silu(2); tap_v(2); silu_next(1); keep_v(1); squares_next(1)
                tap_next(2); silu_v(2)
                z_silu(3); tap_v(3); silu_next(2)
                keep_v(2); read_y1(0); read_y1(1)
                spread()
                silu_v(3); squares_next(2); keep_v(3)
                tap_next(3)
                read_y2(0)
                silu_next(3)
                read_y2(1)
                squares_next(3)
                read_y2(2)
                read_u2(0)
                read_u2(1)
                read_u(0)
                read_y2(3)
                read_u2(2)
                if not last:
                    d_ss_ready.wait(act, kh, 2 * NG)
                square_o(0); read_u(1); read_u2(3)
                square_o(1); read_u(2)
                square_o(2); read_u(3)
                square_o(3)

            loop_then_last(act, NK, head)

            d_acc.wait(act, NK, 0)
            act.wait_ge(m_q_in, Q_LOADS)
            act.wait_ge(m_q, 14)
            for dst, src in ((qg_r, qg_s), (qu_r, qu_s)):
                f(dst[:], src[:], ACT.Copy).then_inc(m_qr, 1)

            def enter(group):
                m_x1T_ready.wait(act, group, 2)
                m_gu_ready.wait(act, group, 0)
                f(x1T[:, 1, :], rest.bank(("x", 1))[:], ACT.Copy).then_inc(m_x1T.sem, 1)

            enter(0)

            def mlps(g, last):
                for ct in range(I2 // P):
                    m_gu_ready.wait(act, g, 2 * ct + 1)
                    m_h.wait(act, g, ct - 1)
                    f(sg[:, ct % 2, :], pairs.bank(("g", ct))[:], ACT.Silu).then_inc(m_sg.sem, 1)
                for e in range(DC):
                    m_y_ready.wait(act, g, e + 1)
                    m_fgu_ready.wait(act, g, 0)
                    f(yT[:, e, :], rest.bank(("y", e))[:], ACT.Copy).then_inc(m_y.sem, 1)
                if not last:
                    enter(g + 1)
                if isinstance(g, int) and g == 0:
                    act.wait_ge(m_q, 21)
                    f(qd_r[:], qd_s[:], ACT.Copy).then_inc(m_qr, 1)
                for ft in range(I3 // P):
                    m_fgu_ready.wait(act, g, 2 * ft + 1)
                    m_h.wait(act, g, I2 // P)
                    m_f.wait(act, g, ft - 1)
                    f(sg[:, ft % 2, :], pairs.bank(("fg", ft))[:], ACT.Silu, scale=gsc[:, ft:ft + 1]).then_inc(m_fs.sem, 1)

            loop_then_last(act, NG, mlps)

        @block.vector
        def _(dve):
            dve.wait_ge(consts, 14)
            dve.tensor_scalar(part[:, 1:2], part[:, 0:1], 16, None, ALU.bitwise_and).then_inc(consts, 1)
            dve.tensor_scalar(part[:, 2:3], part[:, 0:1], 4, None, ALU.logical_shift_right).then_inc(picked, 1)
            dve.wait_ge(consts, 15)
            dve.tensor_scalar(head_even[:], part[:, 1:2], 0, None, ALU.is_equal).then_inc(consts, 1)
            dve.tensor_scalar(head_odd[:], part[:, 1:2], 0, None, ALU.is_gt).then_inc(consts, 1)
            dve.wait_ge(picked, 1)
            dve.tensor_copy(own[:], part[:, 2:3]).then_inc(picked, 1)
            dve.wait_ge(a_small_in, 80)
            dve.tensor_scalar(precs[:], precb[:], 4.0, HD_A ** -0.5, ALU.min, ALU.mult).then_inc(a_prec, 1)
            dve.wait_ge(consts, CONSTS)
            dve.wait_ge(a_prec, 1)

            def attend(g):
                a_x_ready.wait(dve, g, 1)
                dve.tensor_copy(xgT[:, 0, :], front.bank(("x", 0))[:]).then_inc(a_x_read.sem, 1)
                for e in range(2):
                    a_q_ready.wait(dve, g, e + 1)
                    a_s_ready.wait(dve, g, 0)
                    dve.tensor_tensor(qTa[:, e, :].rearrange("p (b t) -> p b t", b=G), front.bank(("q", e))[:].rearrange("p (b t) -> p b t", b=G),
                                      precs[:, bass.ds(g * G, G)].rearrange("p (b t) -> p b t", t=1).broadcast_to([P, G, S]),
                                      ALU.mult).then_inc(a_q_read.sem, 1)
                for e in range(2):
                    a_k_ready.wait(dve, g, e + 1)
                    for kt, mask in ((kTe, head_even), (kTo, head_odd)):
                        dve.tensor_scalar(kt[:, e, :], front.bank(("k", e))[:], mask[:, 0:1], None, ALU.mult).then_inc(a_k_read.sem, 1)

                def maxima(n):
                    a_s_ready.wait(dve, g, n + 1)
                    dve.tensor_reduce(rmax[:, n % 2, :], score.bank(n)[:].rearrange("p (s k) -> p s k", s=4), AX_X, ALU.max).then_inc(a_max.sem, 1)
                    a_max.wait(dve, g, n + 1)
                    a_prob.wait(dve, g, n - 1)
                    dve.tensor_scalar(nmax[:, n % 2, :], rmax[:, n % 2, :], -1.0, None, ALU.mult).then_inc(a_nmax.sem, 1)

                maxima(0)
                maxima(1)
                for n in range(4 * G):
                    b = n // 4
                    a_pt_ready.wait(dve, g, n + 1)
                    a_pv_ready.wait(dve, g, n - 1)
                    dve.tensor_copy(probT[:, n % 2].rearrange("p s q -> p (s q)"), turned.bank(n)[:]).then_inc(a_pt_read.sem, 1)
                    if n + 2 < 4 * G:
                        maxima(n + 2)
                    if n % 4 == 3:
                        dve.reciprocal(rinv[:, b % 2, :], rsum[:, b % 2, :]).then_inc(a_rinv.sem, 1)
                        a_rinv.wait(dve, g, b + 1)
                        a_pv_ready.wait(dve, g, n + 1)
                        a_ot_ready.wait(dve, g, 0)
                        dve.tensor_tensor(oa[:, b, :].rearrange("p (h d) -> p h d", h=NH_A),
                                          front.bank(("pv", b))[:, 0:D].rearrange("p (h d) -> p h d", h=NH_A),
                                          rinv[:, b % 2, :].rearrange("p (h d) -> p h d", d=1).broadcast_to([P, NH_A, HD_A]),
                                          ALU.mult).then_inc(a_o_read.sem, 1)
                for b in range(G):
                    a_ba_ready.wait(dve, g, b + 1)
                    dve.tensor_copy(ba[:, :, bass.ds(g * G + b, 1)], front.bank(("ba", b))[:, 0:2 * NV].rearrange("p (c a) -> p c a", a=1)
                                    ).then_inc(a_ba_read.sem, 1)

            first_then_loop(dve, NG, attend)

            by_batch = lambda t: t.rearrange("p (n a) -> p n a", a=1).broadcast_to([P, NV, B])
            a_ba_read.wait(dve, NG, 0)
            dve.tensor_tensor(sp[1][:], ba[:, NV:2 * NV, :], by_batch(dtb[:]), ALU.add).then_inc(gates, 1)
            dve.wait_ge(gates, 1)
            flat = [t[:].rearrange("p n b -> p (n b)") for t in sp]
            dve.scalar_tensor_tensor(out=flat[2], in0=flat[1], scalar=-1.0, in1=flat[1], op0=ALU.mult, op1=ALU.max).then_inc(gates, 1)
            dve.wait_ge(gates_act, 2)
            for hh in range(HH):
                dve.tensor_scalar(beta[:, :, :, hh], sp[0][:].rearrange("p (k h) b -> p h k b", h=HH)[:, hh], 0.5, 0.5,
                                  ALU.mult, ALU.add).then_inc(gates, 1)
            dve.tensor_scalar(alog[:], nega[:], -1.0, None, ALU.mult).then_inc(gates, 1)
            dve.wait_ge(gates_act, 4)
            dve.scalar_tensor_tensor(out=flat[3], in0=flat[1], scalar=0.0, in1=flat[2], op0=ALU.max, op1=ALU.add).then_inc(gates, 1)
            dve.wait_ge(gates, 6)
            dve.tensor_tensor(sp[0][:], sp[3][:], by_batch(alog[:]), ALU.mult).then_inc(gates, 1)
            dve.wait_ge(gates, 7)
            for hh in range(HH):
                dve.tensor_copy(gdec[:, :, :, hh], sp[0][:].rearrange("p (k h) b -> p h k b", h=HH)[:, hh]).then_inc(gates, 1)
            dve.wait_ge(gates, GATE_STEPS)
            dve.wait_ge(x_in, 64)

            def rsqrt(kh, y, v, t, steps, first):
                n = first
                dve.tensor_scalar(t.bitcast(I32), v.bitcast(I32), 1, None, ALU.logical_shift_right).then_inc(steps.sem, 1)
                steps.wait(dve, kh, n + 1)
                dve.tensor_scalar(y.bitcast(I32), t.bitcast(I32), -1.0, RSQRT_SEED, ALU.mult, ALU.add).then_inc(steps.sem, 1)
                n += 2
                for k in range(3):
                    steps.wait(dve, kh, n)
                    dve.tensor_tensor(t, y, y, ALU.mult).then_inc(steps.sem, 1)
                    steps.wait(dve, kh, n + 1)
                    dve.scalar_tensor_tensor(out=t, in0=t, scalar=-0.5, in1=v, op0=ALU.mult, op1=ALU.mult).then_inc(steps.sem, 1)
                    steps.wait(dve, kh, n + 2)
                    i = dve.scalar_tensor_tensor(out=y, in0=t, scalar=1.5, in1=y, op0=ALU.add, op1=ALU.mult)
                    n += 3
                    i.then_inc(steps.sem, 1)
                return n

            def convolve(step, bank, buf, weights, n, tap, taps_done, steps):
                tap.wait(dve, step, n + 1)
                taps = bank[:].rearrange("p (b t) -> p b t", b=G)
                whole = buf.rearrange("p (b t) -> p b t", b=G)
                for d in range(1, KC):
                    if d > 1:
                        steps.wait(dve, step, 2 * n + d - 1)
                    i = dve.scalar_tensor_tensor(out=whole[:, :, d:S], in0=taps[:, :, 0:S - d], scalar=weights[:, KC - 1 - d:KC - d],
                                                 in1=whole[:, :, d:S], op0=ALU.mult, op1=ALU.add)
                    i.then_inc(taps_done.sem if d == KC - 1 else steps.sem, 1)

            d_cwq_in.wait(dve, -1, 64)
            for g in range(NG):
                for t in range(2):
                    convolve(-1, ahead.bank((g, t)), cbuf[:, (2 * g + t) % 4, :], cwq[:, t, :], 8 + 2 * g + t, d_tap_q, d_conv_q, d_step_q)

            def keep_sums(step):
                d_ss_ready.wait(dve, step, 2 * NG)
                dve.tensor_copy(ssum[:], small[:, SK:SK + 2 * B]).then_inc(d_ss_read.sem, 1)

            keep_sums(-1)

            def quantise(w, first, n):
                if first + n:
                    dve.wait_ge(m_q, first + n)
                if n == 0:
                    i = dve.tensor_scalar(q8a[:], w[:], 240.0, -240.0, ALU.min, ALU.max, saturate=False)
                elif n == 1:
                    i = dve.tensor_scalar(qdif[:], w[:], 0.5, 240.0, ALU.mult, ALU.min)
                elif n == 2:
                    i = dve.tensor_scalar(q8b[:], qdif[:], -240.0, None, ALU.max, saturate=False)
                elif n == 3:
                    i = dve.scalar_tensor_tensor(out=qm[:], in0=w[:], scalar=-1.0, in1=w[:], op0=ALU.mult, op1=ALU.max)
                elif n == 4:
                    i = dve.scalar_tensor_tensor(out=qdif[:], in0=q8b[:], scalar=2.0, in1=q8a[:], op0=ALU.mult, op1=ALU.subtract)
                elif n == 5:
                    i = dve.scalar_tensor_tensor(out=qdif[:], in0=qm[:], scalar=240.0, in1=qdif[:], op0=ALU.is_gt, op1=ALU.mult)
                else:
                    i = dve.tensor_tensor(w[:], qdif[:], q8a[:], ALU.add)
                i.then_inc(m_q, 1)

            def head(kh, last):
                def conv_v(g):
                    d_cwv_in.wait(dve, kh, 16)
                    for t in range(2):
                        convolve(kh, proj.bank(("v", g, t)), cbuf[:, conv_slot["v", g, t], :], cwv[:, t, :], 2 * g + t, d_tap_v, d_conv_v, d_step_v)

                def conv_next(g):
                    if last:
                        return
                    d_cwq_in.wait(dve, kh, 64)
                    for t in range(2):
                        convolve(kh, proj.bank(("next", g, t)), cbuf[:, conv_slot["next", g, t], :], cwq[:, t, :], 8 + 2 * g + t, d_tap_q, d_conv_q, d_step_q)

                def factors():
                    d_ss_read.wait(dve, kh, 1)
                    d_osc.wait(dve, kh, 0)
                    dve.tensor_scalar(ksum[:], ssum[:, SK:SK + B], EPS, None, ALU.add).then_inc(d_rec.sem, 1)
                    dve.tensor_scalar(qeps[:], ssum[:, SQ:SQ + B], EPS * DK, EPS * EPS * DK, ALU.mult, ALU.add)
                    d_rec.wait(dve, kh, 1)
                    dve.reciprocal(krec[:], ksum[:]).then_inc(d_c1.sem, 1)
                    d_c1.wait(dve, kh, 1)
                    d_up.wait(dve, kh, 0)
                    dve.tensor_tensor(cpos[:], beta[:, bass.ds(kh, 1), :, :].rearrange("p a b h -> p (a b) h"),
                                      krec[:].rearrange("p (b h) -> p b h", h=1).broadcast_to([P, B, HH]), ALU.mult).then_inc(d_c.sem, 1)
                    d_c.wait(dve, kh, 1)
                    dve.tensor_scalar(cneg[:], cpos[:], -1.0, None, ALU.mult).then_inc(d_cneg.sem, 1)

                def masks(g):
                    d_y2_ready.wait(dve, kh, 0)
                    d_o_ready.wait(dve, kh, 2 * g + 2 - 8)
                    for h in range(2):
                        d_E.wait(dve, kh, 2 * g + h + 1)
                        d_gk_ready.wait(dve, kh, 2 * g + h + 1)
                        gk = work.bank(("gk", g, h))[:].rearrange("p (b t i) -> p b t i", b=2, t=2)
                        u = UG * g + 4 * h
                        dve.tensor_tensor(att[:, u:u + 4, :].rearrange("p (b h) i -> p b h i", b=2),
                                          gk[:, :, 1:2, :].broadcast_to([P, 2, HH, P]),
                                          E[:, h].rearrange("p (b h) i -> p b h i", b=2), ALU.mult)
                        d_cneg.wait(dve, kh, 1)
                        for n in range(4):
                            u = UG * g + 4 * h + n
                            b = G * g + 2 * h + n // 2
                            i = dve.scalar_tensor_tensor(out=Bm[:, u, :], in0=gk[:, n // 2, 0, :], scalar=cneg[:, b, n % 2:n % 2 + 1],
                                                         in1=E[:, h, n, :], op0=ALU.mult, op1=ALU.mult)
                        i.then_inc(d_B.sem, 1)

                def clear_lanes():
                    dve.memset(lane_T[:], 0.0).then_inc(d_lanes.sem, 1)
                    d_lanes.wait(dve, kh, 1)
                    dve.memset(lane_T[:].rearrange("p a b -> p (a b)")[:, 0:BK * BK:BK + 1], 1.0).then_inc(d_lanes.sem, 1)

                def to_lanes():
                    d_diag.wait(dve, kh, NG)
                    dve.transpose(diag_u[:], diag_l[:].rearrange("p u a -> p a u")).then_inc(d_lanes.sem, 1)

                def from_lanes():
                    d_solve.wait(dve, kh, d_solve.per)
                    dve.transpose(diag_l[:].rearrange("p u k -> p k u"), lane_T[:].rearrange("p i k -> p k i")).then_inc(d_unlane.sem, 1)
                    dve.transpose(diag_u[:].rearrange("p u i -> p i u"), lane_T[:]).then_inc(d_unlane.sem, 1)

                def key_norms():
                    d_rec.wait(dve, kh, 1)
                    d_w.wait(dve, kh, 0)
                    rsqrt(kh, nt[:, 0, 0:B], ksum[:], nt[:, 1, 0:B], d_newt, 0)
                    d_newt.wait(dve, kh, 11)
                    dve.tensor_tensor(knorm[:], nt[:, 0, 0:B], ksum[:], ALU.mult).then_inc(d_knorm.sem, 1)

                def spread():
                    d_unlane.wait(dve, kh, 2)
                    d_u_ready.wait(dve, kh, 0)
                    for r in range(4):
                        rows = slice(BK * r, BK * r + BK)
                        dve.tensor_copy(Ue[rows, :, rows], diag_u[rows]).then_inc(d_spread_u.sem, 1)

                def read_t1(fh):
                    us = slice(16 * fh, 16 * fh + 16)
                    for p in range(2):
                        lo, hi = slice(64 * p, 64 * p + BK), slice(64 * p + BK, 64 * p + 2 * BK)
                        d_t1_ready.wait(dve, kh, 2 * fh + p + 1)
                        d_u_ready.wait(dve, kh, 0)
                        bank = work.bank(("t1", fh, p))[:].rearrange("p (u c) -> p u c", c=BK)
                        dve.tensor_copy(Le[hi, us, 0:BK], bank[hi])
                        dve.tensor_copy(Ue[lo, us, hi], bank[lo]).then_inc(d_t1_read.sem, 1)

                def gate(g, h):
                    d_sqo.wait(dve, kh, 2 * g + h + 1)
                    d_zg.wait(dve, kh, 2 * g + 2)
                    d_y_ready.wait(dve, kh, G * g + 2 * h + 2 - G)
                    t0 = g * TG + h * 2 * S
                    dve.tensor_tensor(go[:, h].rearrange("p (b h) t -> p b h t", b=2), work.bank(("o", g, h))[:].rearrange("p (b h t) -> p b h t", b=2, h=HH),
                                      zg[:, :, t0:t0 + 2 * S].rearrange("p h (b t) -> p b h t", b=2), ALU.mult).then_inc(d_go.sem, 1)

                def out_norms(g):
                    bs = slice(G * g, G * g + G)
                    v = nt[:, 2, 0:UG]
                    d_so_ready.wait(dve, kh, 2 * g + 2)
                    dve.scalar_tensor_tensor(out=v.rearrange("p (b h) -> p b h", h=HH),
                                             in0=small[:, SO + UG * g:SO + UG * g + UG].rearrange("p (b h) -> p b h", h=HH), scalar=1.0 / DV,
                                             in1=qeps[:, bs].rearrange("p (b h) -> p b h", h=1).broadcast_to([P, G, HH]),
                                             op0=ALU.mult, op1=ALU.add).then_inc(d_so_read.sem, 1)
                    d_so_read.wait(dve, kh, g + 1)
                    n = rsqrt(kh, nt[:, 0, 0:UG], v, nt[:, 1, 0:UG], d_nto, 11 * g)
                    d_nto.wait(dve, kh, n)
                    dve.tensor_copy(osc[:, bs, :].rearrange("p b h -> p (b h)"), nt[:, 0, 0:UG]).then_inc(d_osc.sem, 1)
                    d_osc.wait(dve, kh, g + 1)

                def accumulate(g, h):
                    for b in (2 * h, 2 * h + 1):
                        s = G * g + b
                        d_y_ready.wait(dve, kh, s + 1)
                        for hh in range(HH):
                            if hh:
                                d_acc_step.wait(dve, kh, s + 1)
                            i = dve.scalar_tensor_tensor(out=acc[:, s, :], in0=ring_y(g).bank(("y", g, b))[:, hh * D:(hh + 1) * D], scalar=osc[:, s, hh:hh + 1],
                                                         in1=acc[:, s, :], op0=ALU.mult, op1=ALU.add)
                            i.then_inc(d_acc.sem if hh else d_acc_step.sem, 1)

                factors()
                clear_lanes()
                for g in range(NG):
                    masks(g)
                to_lanes()
                for g in range(NG - 1):
                    conv_v(g)
                    if g == 0:
                        key_norms()
                    conv_next(g)
                if last:
                    dve.wait_ge(m_q_in, Q_LOADS)
                    for k, w in enumerate((qg_s, qu_s)):
                        for n in range(7):
                            quantise(w, 7 * k, n)
                from_lanes()
                conv_v(NG - 1)
                read_t1(0)
                read_t1(1)
                spread()
                conv_next(NG - 1)
                if not last:
                    keep_sums(kh)
                gate(0, 0)
                gate(0, 1)
                for g in range(NG):
                    out_norms(g)
                    for h in range(2):
                        accumulate(g, h)
                        if g + 1 < NG:
                            gate(g + 1, h)

            loop_then_last(dve, NK, head)

            d_acc.wait(dve, NK, 0)
            dve.wait_ge(m_q_in, Q_LOADS)
            dve.wait_ge(picked, 2)
            dve.tensor_copy(idx_f[:], idx_i[:]).then_inc(m_pick, 1)
            dve.wait_ge(m_pick, 1)
            dve.tensor_scalar(pick[:], idx_f[:], own[:, 0:1], None, ALU.is_equal).then_inc(m_pick, 1)
            dve.wait_ge(m_pick, 2)

            def keep_own(group, dst, src, b0, nb, done):
                dve.tensor_tensor(dst.rearrange("p (b t) -> p b t", b=nb), src.rearrange("p (b t) -> p b t", b=nb),
                                  pick[:, bass.ds(group * G + b0, nb)].rearrange("p (b t) -> p b t", t=1).broadcast_to([P, nb, S]),
                                  ALU.mult).then_inc(done.sem, 1)

            def enter(group):
                m_x1T_ready.wait(dve, group, 1)
                m_gu_ready.wait(dve, group, 0)
                dve.tensor_copy(x1T[:, 0, :], rest.bank(("x", 0))[:]).then_inc(m_x1T.sem, 1)

            def keep_lora(group):
                for n in range(2):
                    m_lg_ready.wait(dve, group, n + 1)
                    m_gu_ready.wait(dve, group, 0)
                    keep_own(group, lg[:, n, :], rest.bank(("lg", n))[:], 0, G, m_lg)

            enter(0)
            keep_lora(0)

            def mlps(g, last):
                begins = isinstance(g, int) and g == 0
                if begins:
                    dve.wait_ge(m_w_in, W_LOADS)
                for ct in range(I2 // P):
                    m_gu_ready.wait(dve, g, 2 * ct + 2)
                    m_sg.wait(dve, g, ct + 1)
                    m_y_ready.wait(dve, g, 0)
                    dve.tensor_tensor(hT[:, ct, :], sg[:, ct % 2, :], pairs.bank(("u", ct))[:], ALU.mult).then_inc(m_h.sem, 1)
                    if begins and ct < 7:
                        quantise(qd_s, 14, ct)
                for n in range(2):
                    m_ld_ready.wait(dve, g, n + 1)
                    m_y_ready.wait(dve, g, 0)
                    keep_own(g, lg[:, 2, n * 256:(n + 1) * 256], rest.bank(("ld", n))[:, 0:256], 2 * n, 2, m_ld)
                if not last:
                    enter(g + 1)
                for e in range(DC):
                    m_y.wait(dve, g, e + 1)
                    m_fgu_ready.wait(dve, g, 0)
                    dve.tensor_copy(yh[:, e, :], yT[:, e, :]).then_inc(m_yh.sem, 1)
                for e in range(DC):
                    m_yh.wait(dve, g, e + 1)
                    dve.tensor_tensor(yl[:, e, :], yT[:, e, :], yh[:, e, :].bitcast(F32), ALU.subtract).then_inc(m_yl.sem, 1)
                if not last:
                    keep_lora(g + 1)
                for ft in range(I3 // P):
                    m_fgu_ready.wait(dve, g, 2 * ft + 2)
                    m_fs.wait(dve, g, ft + 1)
                    m_d_ready.wait(dve, g, 0)
                    m_fl.wait(dve, g, ft - 1)
                    dve.scalar_tensor_tensor(out=fT[:, ft % 2, :], in0=pairs.bank(("fu", ft))[:], scalar=usc[:, ft:ft + 1], in1=sg[:, ft % 2, :],
                                             op0=ALU.mult, op1=ALU.mult).then_inc(m_f.sem, 1)
                    m_f.wait(dve, g, ft + 1)
                    dve.tensor_copy(fh[:, ft, :], fT[:, ft % 2, :]).then_inc(m_fh.sem, 1)
                    m_fh.wait(dve, g, ft + 1)
                    dve.tensor_tensor(fl[:, ft, :], fT[:, ft % 2, :], fh[:, ft, :].bitcast(F32), ALU.subtract).then_inc(m_fl.sem, 1)
                for b in range(G):
                    m_d_ready.wait(dve, g, b + 1)
                    dve.tensor_tensor(dn[:, b % 2, :], rest.bank(("d", b))[:, 0:D], dsc[:], ALU.mult).then_inc(m_dn.sem, 1)
                    m_dn.wait(dve, g, b + 1)
                    m_out.wait(dve, g, 0)
                    dve.tensor_tensor(og[:, b:b + 1, :], dn[:, b % 2:b % 2 + 1, :], acc[:, bass.ds(g * G + b, 1), :], ALU.add).then_inc(m_og.sem, 1)

            loop_then_last(dve, NG, mlps)


_INS = ['x', 'cond_1', 'itok_B_0_7', 'L0_cond_Wq', 'L0_cond_Wk', 'L0_cond_Wv', 'L0_cond_Wo', 'L0_attn_W_qkv', 'L0_attn_W_z',
        'L0_attn_W_b', 'L0_attn_W_a', 'L0_attn_conv_w', 'L0_attn_dt_bias', 'L0_attn_A_log', 'L0_attn_norm_w', 'L0_attn_W_out',
        'L0_cond2_Wg', 'L0_cond2_Wu', 'L0_cond2_Wd', 'L0_cond2_Ag', 'L0_cond2_Bg', 'L0_cond2_Au', 'L0_cond2_Bu', 'L0_cond2_Ad',
        'L0_cond2_Bd', 'L0_ffn_gate_w', 'L0_ffn_up_w', 'L0_ffn_down_w', 'L0_ffn_gate_scale', 'L0_ffn_up_scale', 'L0_ffn_down_scale']


def kernel(**inputs):
    import numpy as np
    import concourse.bacc as bacc
    from concourse.bass_utils import run_bass_kernel_spmd

    nc = bacc.Bacc("TRN2", target_bir_lowering=False, num_devices=1)
    arrays, args = {}, []
    for name in _INS:
        a = np.ascontiguousarray(inputs[name])
        arrays[f"in_{name}"] = a
        args.append(nc.dram_tensor(f"in_{name}", a.shape, mybir.dt.from_np(a.dtype), kind="ExternalInput").ap())
    out = nc.dram_tensor("out", (B, S, D), F32, kind="ExternalOutput").ap()
    build(nc, *args, out)
    r = run_bass_kernel_spmd(nc, [arrays], core_ids=[0])
    return r.results[0]["out"]
```
